# Optimizing a Trainium2 kernel written in Bass

```python
import numpy as np
import jax
import jax.numpy as jnp

def _softmax(x, axis=-1):
    return jax.nn.softmax(x, axis=axis)

def _gelu(x):
    return jax.nn.gelu(x, approximate=True)

def _silu(x):
    return jax.nn.silu(x)

def _sigmoid(x):
    return jax.nn.sigmoid(x)

def _layernorm(x, axis=-1, eps=1e-05):
    m = jnp.mean(x, axis=axis, keepdims=True)
    v = jnp.var(x, axis=axis, keepdims=True)
    return (x - m) / jnp.sqrt(v + eps)

def _scatter_add(tgt, idx, src, axis=0):
    return tgt.at[idx].add(src)

def _segment_sum(src, seg, n):
    return jax.ops.segment_sum(src, seg, n)
kernel_name = 'mk_decoder_preln_d2_seqx_r4_246d3b'

def setup_inputs(seed: int=0):
    np.random.seed(seed)
    _w = jnp.asarray

    def _rec_inputs():
        import jax
        import jax.numpy as jnp
        _rk = jax.random.key(seed)
        x = -0.0002928 + 1 * jax.random.normal(jax.random.fold_in(_rk, 1), (4, 1024, 256), jnp.float32)
        _lenS = 1024 - jax.random.randint(jax.random.fold_in(_rk, 7), (4,), 0, max(1, 1024 // 4) + 1, jnp.int32)
        _lenS2 = 77 - jax.random.randint(jax.random.fold_in(_rk, 8), (4,), 0, max(1, 77 // 4) + 1, jnp.int32)
        _ctx_1024P = jax.random.normal(jax.random.fold_in(_rk, 11), (4, 16, 256), jnp.float32)
        _ctx_1024c = jax.random.dirichlet(jax.random.fold_in(_rk, 511), 0.3 * jnp.ones((16,), jnp.float32), (4, 77))
        _ctx_1024t = jnp.einsum('bsk,bkd->bsd', _ctx_1024c, _ctx_1024P)
        _ctx_1024t = _ctx_1024t * jax.lax.rsqrt(jnp.mean(jnp.square(_ctx_1024t)) + 1e-12) * 0.953939
        ctx_1024 = -1.39393e-06 + 0.999914 * (_ctx_1024t + 0.3 * jax.random.normal(jax.random.fold_in(_rk, 611), (4, 77, 256), jnp.float32))
        fside_BxS2_0 = 0.0132156 + 1.00766 * jax.random.normal(jax.random.fold_in(_rk, 12), (4, 77), jnp.float32)
        _validS = jnp.arange(1024)[None, :] < _lenS[:, None]
        _validS2 = jnp.arange(77)[None, :] < _lenS2[:, None]
        _causal = jnp.tril(jnp.ones((1024, 1024), dtype=bool))
        mask_BxS2_bk0 = jnp.logical_not(jnp.broadcast_to(_validS2[:, :], (4, 77)))
        mask_BxS2_ff1 = jnp.where(jnp.ones((4, 77), dtype=bool), 1.0, 0.0).astype(jnp.float32)
        return (x, ctx_1024, fside_BxS2_0, mask_BxS2_bk0, mask_BxS2_ff1)
    x, ctx_1024, fside_BxS2_0, mask_BxS2_bk0, mask_BxS2_ff1 = _rec_inputs()

    def _L0_attn_setup():
        import jax, jax.numpy as jnp
        import numpy as np
        B, S, D, H = (2, 512, 256, 16)
        HD = D // H
        key = jax.random.key(seed)
        ks = jax.random.split(key, 16)
        sc = 0.02
        return {'hidden_states': jax.random.normal(ks[0], (B, S, D), jnp.float32), 'Wq': jax.random.normal(ks[1], (D, D), jnp.float32) * sc, 'bq': jnp.zeros((D,), jnp.float32), 'Wk': jax.random.normal(ks[2], (D, D), jnp.float32) * sc, 'bk': jnp.zeros((D,), jnp.float32), 'Wv': jax.random.normal(ks[3], (D, D), jnp.float32) * sc, 'bv': jnp.zeros((D,), jnp.float32), 'Wo': jax.random.normal(ks[4], (D, D), jnp.float32) * sc, 'bo': jnp.zeros((D,), jnp.float32), 'rel_W': jax.random.normal(ks[5], (3, 2 * D), jnp.float32) * sc, 'rel_b': jnp.zeros((3,), jnp.float32), 'logical_bias': jax.random.normal(ks[6], (H, 3), jnp.float32) * sc, 'gate_W': jax.random.normal(ks[7], (H, D), jnp.float32) * sc, 'gate_b': jnp.zeros((H,), jnp.float32)}
    _L0_attn_all = _L0_attn_setup()
    _L0_attn_in = {k: v for k, v in _L0_attn_all.items() if k in ('Wq', 'bq', 'Wk', 'bk', 'Wv', 'bv', 'Wo', 'bo', 'rel_W', 'rel_b', 'logical_bias', 'gate_W', 'gate_b')}
    del _L0_attn_all

    def _L0_xattn_setup():
        import jax, jax.numpy as jnp
        import numpy as np
        EMBED_DIM = 256
        NUM_HEADS = 16
        HEAD_DIM = EMBED_DIM // NUM_HEADS
        B, SQ, SK = (2, 512, 512)
        key = jax.random.key(seed)
        ks = jax.random.split(key, 10)
        s = 1.0 / np.sqrt(EMBED_DIM)
        return {'tgt': jax.random.normal(ks[0], (B, SQ, EMBED_DIM), jnp.float32), 'mem': jax.random.normal(ks[1], (B, SK, EMBED_DIM), jnp.float32), 'attn_bias': jax.random.normal(ks[2], (B, SK), jnp.float32), 'memory_key_padding_mask': jax.random.randint(ks[3], (B, SK), 0, 2).astype(bool), 'Wq_w': jax.random.normal(ks[4], (EMBED_DIM, EMBED_DIM), jnp.float32) * s, 'Wq_b': jnp.zeros((EMBED_DIM,), jnp.float32), 'Wkv_w': jax.random.normal(ks[5], (2 * EMBED_DIM, EMBED_DIM), jnp.float32) * s, 'Wkv_b': jnp.zeros((2 * EMBED_DIM,), jnp.float32), 'out_w': jax.random.normal(ks[6], (EMBED_DIM, EMBED_DIM), jnp.float32) * s, 'out_b': jnp.zeros((EMBED_DIM,), jnp.float32)}
    _L0_xattn_all = _L0_xattn_setup()
    _L0_xattn_in = {k: v for k, v in _L0_xattn_all.items() if k in ('Wq_w', 'Wq_b', 'Wkv_w', 'Wkv_b', 'out_w', 'out_b')}
    del _L0_xattn_all

    def _L0_ffn_setup():
        import jax, jax.numpy as jnp
        import numpy as np
        HIDDEN = 256
        INNER = 1024

        def _weight_quant(w):
            scale = 1.0 / jnp.clip(jnp.mean(jnp.abs(w)), 1e-05)
            wq = jnp.clip(jnp.round(w * scale), -1.0, 1.0) / scale
            return w + jax.lax.stop_gradient(wq - w)

        def _act_quant(x):
            scale = 127.0 / jnp.clip(jnp.max(jnp.abs(x), axis=-1, keepdims=True), 1e-05)
            xq = jnp.clip(jnp.round(x * scale), -128.0, 127.0) / scale
            return x + jax.lax.stop_gradient(xq - x)

        def _bitlinear(x, w):
            return jnp.einsum('bsi,oi->bso', _act_quant(x), _weight_quant(w))
        key = jax.random.key(seed)
        k0, k1, k2, k3 = jax.random.split(key, 4)
        x = jax.random.normal(k0, (4, 512, HIDDEN), dtype=jnp.float32)
        w_gate = jax.random.normal(k1, (INNER, HIDDEN), dtype=jnp.float32) / np.sqrt(HIDDEN)
        w_up = jax.random.normal(k2, (INNER, HIDDEN), dtype=jnp.float32) / np.sqrt(HIDDEN)
        w_down = jax.random.normal(k3, (HIDDEN, INNER), dtype=jnp.float32) / np.sqrt(INNER)
        return {'x': x, 'w_gate': w_gate, 'w_up': w_up, 'w_down': w_down}
    _L0_ffn_all = _L0_ffn_setup()
    _L0_ffn_in = {k: v for k, v in _L0_ffn_all.items() if k in ('w_gate', 'w_up', 'w_down')}
    del _L0_ffn_all

    def _L1_attn_setup():
        import jax, jax.numpy as jnp
        import numpy as np
        from functools import partial
        B, S, D, H, DK, DV, DFF = (4, 512, 256, 8, 128, 128, 1024)
        EPS = 1e-06

        def rms_norm(x):
            return x * jax.lax.rsqrt(jnp.mean(x * x, axis=-1, keepdims=True) + EPS)

        def l2norm(x):
            return x * jax.lax.rsqrt(jnp.sum(x * x, axis=-1, keepdims=True) + EPS)

        def gated_delta_net(h, Wq, Wk, Wv, Wb, Wa, A_log, dt_bias, Wg, o_norm_w, Wo):
            b, s, _ = h.shape
            q = l2norm(jax.nn.silu(h @ Wq).reshape(b, s, H, DK))
            k = l2norm(jax.nn.silu(h @ Wk).reshape(b, s, H, DK))
            v = jax.nn.silu(h @ Wv).reshape(b, s, H, DV)
            beta = jax.nn.sigmoid(h @ Wb)
            g = -jnp.exp(A_log) * jax.nn.softplus(h @ Wa + dt_bias)
            alpha = jnp.exp(g)
            scale = DK ** (-0.5)
            tm = lambda a: jnp.moveaxis(a, 1, 0)
            qs, ks_, vs, als, bts = (tm(q), tm(k), tm(v), tm(alpha), tm(beta))

            def step(Sst, inp):
                q_t, k_t, v_t, a_t, b_t = inp
                Sst = Sst * a_t[..., None, None]
                kv = jnp.einsum('bhd,bhde->bhe', k_t, Sst)
                delta = (v_t - kv) * b_t[..., None]
                Sst = Sst + jnp.einsum('bhd,bhe->bhde', k_t, delta)
                o_t = jnp.einsum('bhd,bhde->bhe', q_t, Sst) * scale
                return (Sst, o_t)
            S0 = jnp.zeros((b, H, DK, DV), dtype=h.dtype)
            _, o = jax.lax.scan(step, S0, (qs, ks_, vs, als, bts))
            o = jnp.moveaxis(o, 0, 1)
            gate = (h @ Wg).reshape(b, s, H, DV)
            o = rms_norm(o) * o_norm_w * jax.nn.silu(gate)
            return o.reshape(b, s, H * DV) @ Wo
        key = jax.random.key(seed)
        ks = jax.random.split(key, 16)
        w = lambda k, shp: jax.random.normal(k, shp, dtype=jnp.float32) * 0.02
        return {'x': jax.random.normal(ks[0], (B, S, D), dtype=jnp.float32), 'Wq': w(ks[1], (D, H * DK)), 'Wk': w(ks[2], (D, H * DK)), 'Wv': w(ks[3], (D, H * DV)), 'Wb': w(ks[4], (D, H)), 'Wa': w(ks[5], (D, H)), 'A_log': jnp.log(jnp.linspace(1.0, 8.0, H).astype(jnp.float32)), 'dt_bias': jax.random.normal(ks[6], (H,), dtype=jnp.float32) * 0.1, 'Wg': w(ks[7], (D, H * DV)), 'o_norm_w': jnp.ones((DV,), dtype=jnp.float32), 'Wo': w(ks[8], (H * DV, D)), 'W_fc': w(ks[9], (D, DFF)), 'W_proj': w(ks[10], (DFF, D))}
    _L1_attn_all = _L1_attn_setup()
    _L1_attn_in = {k: v for k, v in _L1_attn_all.items() if k in ('Wq', 'Wk', 'Wv', 'Wb', 'Wa', 'A_log', 'dt_bias', 'Wg', 'o_norm_w', 'Wo', 'W_fc', 'W_proj')}
    del _L1_attn_all

    def _L1_xattn_setup():
        import jax, jax.numpy as jnp
        import numpy as np
        D_MODEL = 256
        HEADS = 16
        DEPTH = D_MODEL // HEADS
        B, S = (4, 1024)
        EPS_K = 1e-06
        EPS_LN = 1e-06

        def _layernorm(x, g, b):
            m = jnp.mean(x, axis=-1, keepdims=True)
            var = jnp.var(x, axis=-1, keepdims=True)
            return (x - m) * jax.lax.rsqrt(var + EPS_LN) * g + b

        def _split_heads(x):
            bsz, sl, _ = x.shape
            return x.reshape(bsz, sl, HEADS, DEPTH).transpose(0, 2, 1, 3)
        key = jax.random.key(seed)
        ks = jax.random.split(key, 8)
        lecun = 1.0 / np.sqrt(D_MODEL)
        glorot = np.sqrt(2.0 / (D_MODEL + D_MODEL))
        return {'q': jax.random.normal(ks[0], (B, S, D_MODEL), jnp.float32), 'k': jax.random.normal(ks[1], (B, S, D_MODEL), jnp.float32), 'v': jax.random.normal(ks[2], (B, S, D_MODEL), jnp.float32), 'mask': jnp.ones((B, S), jnp.float32), 'wq': jax.random.normal(ks[3], (D_MODEL, D_MODEL), jnp.float32) * lecun, 'wk': jax.random.normal(ks[4], (D_MODEL, D_MODEL), jnp.float32) * lecun, 'wv': jax.random.normal(ks[5], (D_MODEL, D_MODEL), jnp.float32) * lecun, 'ln_gamma': jnp.ones((D_MODEL,), jnp.float32), 'ln_beta': jnp.zeros((D_MODEL,), jnp.float32), 'dense_w': jax.random.normal(ks[6], (D_MODEL, D_MODEL), jnp.float32) * glorot, 'dense_b': jnp.zeros((D_MODEL,), jnp.float32)}
    _L1_xattn_all = _L1_xattn_setup()
    _L1_xattn_in = {k: v for k, v in _L1_xattn_all.items() if k in ('wq', 'wk', 'wv', 'ln_gamma', 'ln_beta', 'dense_w', 'dense_b')}
    del _L1_xattn_all

    def _L1_ffn_setup():
        import jax, jax.numpy as jnp
        import numpy as np
        D = 256
        H = 16
        DH = D // H
        DC = D // 4
        HID = 512
        G = 2
        EPG = 4
        E = G * EPG
        TOPK = 2
        EPS = 1e-06
        B, T = (2, 512)

        def _rope_sincos(t, dh):
            inv_freq = 1.0 / 10000.0 ** (jnp.arange(0, dh, 2, dtype=jnp.float32) / dh)
            ang = jnp.arange(t, dtype=jnp.float32)[:, None] * inv_freq[None, :]
            return (jnp.sin(ang), jnp.cos(ang))

        def _apply_rope(x, sin, cos):
            x1 = x[..., ::2]
            x2 = x[..., 1::2]
            r = jnp.stack([x1 * cos - x2 * sin, x1 * sin + x2 * cos], axis=-1)
            return r.reshape(x.shape)

        def _swiglu(x):
            a, b = jnp.split(x, 2, axis=-1)
            return jax.nn.silu(a) * b

        def _rmsnorm(x, w):
            return x * jax.lax.rsqrt(jnp.mean(x * x, axis=-1, keepdims=True) + EPS) * w
        key = jax.random.key(seed)
        ks = jax.random.split(key, 14)
        s = 0.02
        return {'src': jax.random.normal(ks[0], (B, T, D), jnp.float32), 'Wq': jax.random.normal(ks[1], (D, D), jnp.float32) * s, 'Wk_c': jax.random.normal(ks[2], (D, DC), jnp.float32) * s, 'Wv_c': jax.random.normal(ks[3], (D, DC), jnp.float32) * s, 'Wk': jax.random.normal(ks[4], (DC, D), jnp.float32) * s, 'Wv': jax.random.normal(ks[5], (DC, D), jnp.float32) * s, 'Wo': jax.random.normal(ks[6], (D, D), jnp.float32) * s, 'W_shared_in': jax.random.normal(ks[7], (D, 2 * HID), jnp.float32) * s, 'W_shared_out': jax.random.normal(ks[8], (HID, D), jnp.float32) * s, 'W1_shared': jax.random.normal(ks[9], (D, 2 * HID), jnp.float32) * s, 'W2_experts': jax.random.normal(ks[10], (E, HID, D), jnp.float32) * s, 'Wg_gate': jax.random.normal(ks[11], (D, G), jnp.float32) * s, 'We_gate': jax.random.normal(ks[12], (D, E), jnp.float32) * s, 'group_bias': jnp.zeros((G,), jnp.float32), 'expert_bias': jnp.zeros((E,), jnp.float32), 'norm1_w': jnp.ones((D,), jnp.float32), 'norm2_w': jnp.ones((D,), jnp.float32)}
    _L1_ffn_all = _L1_ffn_setup()
    _L1_ffn_in = {k: v for k, v in _L1_ffn_all.items() if k in ('Wq', 'Wk_c', 'Wv_c', 'Wk', 'Wv', 'Wo', 'W_shared_in', 'W_shared_out', 'W1_shared', 'W2_experts', 'Wg_gate', 'We_gate', 'group_bias', 'expert_bias', 'norm1_w', 'norm2_w')}
    del _L1_ffn_all
    return {'x': x, 'ctx_1024': ctx_1024, 'fside_BxS2_0': fside_BxS2_0, 'mask_BxS2_bk0': mask_BxS2_bk0, 'mask_BxS2_ff1': mask_BxS2_ff1, 'L0_attn_Wq': _L0_attn_in['Wq'], 'L0_attn_bq': _L0_attn_in['bq'], 'L0_attn_Wk': _L0_attn_in['Wk'], 'L0_attn_bk': _L0_attn_in['bk'], 'L0_attn_Wv': _L0_attn_in['Wv'], 'L0_attn_bv': _L0_attn_in['bv'], 'L0_attn_Wo': _L0_attn_in['Wo'], 'L0_attn_bo': _L0_attn_in['bo'], 'L0_attn_rel_W': _L0_attn_in['rel_W'], 'L0_attn_rel_b': _L0_attn_in['rel_b'], 'L0_attn_logical_bias': _L0_attn_in['logical_bias'], 'L0_attn_gate_W': _L0_attn_in['gate_W'], 'L0_attn_gate_b': _L0_attn_in['gate_b'], 'L0_xattn_Wq_w': _L0_xattn_in['Wq_w'], 'L0_xattn_Wq_b': _L0_xattn_in['Wq_b'], 'L0_xattn_Wkv_w': _L0_xattn_in['Wkv_w'], 'L0_xattn_Wkv_b': _L0_xattn_in['Wkv_b'], 'L0_xattn_out_w': _L0_xattn_in['out_w'], 'L0_xattn_out_b': _L0_xattn_in['out_b'], 'L0_ffn_w_gate': _L0_ffn_in['w_gate'], 'L0_ffn_w_up': _L0_ffn_in['w_up'], 'L0_ffn_w_down': _L0_ffn_in['w_down'], 'L1_attn_Wq': _L1_attn_in['Wq'], 'L1_attn_Wk': _L1_attn_in['Wk'], 'L1_attn_Wv': _L1_attn_in['Wv'], 'L1_attn_Wb': _L1_attn_in['Wb'], 'L1_attn_Wa': _L1_attn_in['Wa'], 'L1_attn_A_log': _L1_attn_in['A_log'], 'L1_attn_dt_bias': _L1_attn_in['dt_bias'], 'L1_attn_Wg': _L1_attn_in['Wg'], 'L1_attn_o_norm_w': _L1_attn_in['o_norm_w'], 'L1_attn_Wo': _L1_attn_in['Wo'], 'L1_attn_W_fc': _L1_attn_in['W_fc'], 'L1_attn_W_proj': _L1_attn_in['W_proj'], 'L1_xattn_wq': _L1_xattn_in['wq'], 'L1_xattn_wk': _L1_xattn_in['wk'], 'L1_xattn_wv': _L1_xattn_in['wv'], 'L1_xattn_ln_gamma': _L1_xattn_in['ln_gamma'], 'L1_xattn_ln_beta': _L1_xattn_in['ln_beta'], 'L1_xattn_dense_w': _L1_xattn_in['dense_w'], 'L1_xattn_dense_b': _L1_xattn_in['dense_b'], 'L1_ffn_Wq': _L1_ffn_in['Wq'], 'L1_ffn_Wk_c': _L1_ffn_in['Wk_c'], 'L1_ffn_Wv_c': _L1_ffn_in['Wv_c'], 'L1_ffn_Wk': _L1_ffn_in['Wk'], 'L1_ffn_Wv': _L1_ffn_in['Wv'], 'L1_ffn_Wo': _L1_ffn_in['Wo'], 'L1_ffn_W_shared_in': _L1_ffn_in['W_shared_in'], 'L1_ffn_W_shared_out': _L1_ffn_in['W_shared_out'], 'L1_ffn_W1_shared': _L1_ffn_in['W1_shared'], 'L1_ffn_W2_experts': _L1_ffn_in['W2_experts'], 'L1_ffn_Wg_gate': _L1_ffn_in['Wg_gate'], 'L1_ffn_We_gate': _L1_ffn_in['We_gate'], 'L1_ffn_group_bias': _L1_ffn_in['group_bias'], 'L1_ffn_expert_bias': _L1_ffn_in['expert_bias'], 'L1_ffn_norm1_w': _L1_ffn_in['norm1_w'], 'L1_ffn_norm2_w': _L1_ffn_in['norm2_w']}

def reference(x, ctx_1024, fside_BxS2_0, mask_BxS2_bk0, mask_BxS2_ff1, L0_attn_Wq, L0_attn_bq, L0_attn_Wk, L0_attn_bk, L0_attn_Wv, L0_attn_bv, L0_attn_Wo, L0_attn_bo, L0_attn_rel_W, L0_attn_rel_b, L0_attn_logical_bias, L0_attn_gate_W, L0_attn_gate_b, L0_xattn_Wq_w, L0_xattn_Wq_b, L0_xattn_Wkv_w, L0_xattn_Wkv_b, L0_xattn_out_w, L0_xattn_out_b, L0_ffn_w_gate, L0_ffn_w_up, L0_ffn_w_down, L1_attn_Wq, L1_attn_Wk, L1_attn_Wv, L1_attn_Wb, L1_attn_Wa, L1_attn_A_log, L1_attn_dt_bias, L1_attn_Wg, L1_attn_o_norm_w, L1_attn_Wo, L1_attn_W_fc, L1_attn_W_proj, L1_xattn_wq, L1_xattn_wk, L1_xattn_wv, L1_xattn_ln_gamma, L1_xattn_ln_beta, L1_xattn_dense_w, L1_xattn_dense_b, L1_ffn_Wq, L1_ffn_Wk_c, L1_ffn_Wv_c, L1_ffn_Wk, L1_ffn_Wv, L1_ffn_Wo, L1_ffn_W_shared_in, L1_ffn_W_shared_out, L1_ffn_W1_shared, L1_ffn_W2_experts, L1_ffn_Wg_gate, L1_ffn_We_gate, L1_ffn_group_bias, L1_ffn_expert_bias, L1_ffn_norm1_w, L1_ffn_norm2_w):
    import jax
    import jax.numpy as jnp

    def _L0_attn_ref(hidden_states, Wq, bq, Wk, bk, Wv, bv, Wo, bo, rel_W, rel_b, logical_bias, gate_W, gate_b):
        import jax, jax.numpy as jnp
        import numpy as np
        B, S, D, H = (2, 512, 256, 16)
        HD = D // H
        x = hidden_states
        b, s, d = x.shape
        h = gate_W.shape[0]
        hd = d // h
        scale = hd ** 0.5
        q = (x @ Wq.T + bq).reshape(b, s, h, hd)
        k = (x @ Wk.T + bk).reshape(b, s, h, hd)
        v = (x @ Wv.T + bv).reshape(b, s, h, hd)
        attn_scores = jnp.einsum('bihd,bjhd->bhij', q, k) / scale
        li = x @ rel_W[:, :d].T
        lj = x @ rel_W[:, d:].T
        logits = li[:, :, None, :] + lj[:, None, :, :] + rel_b
        relation_probs = jax.nn.softmax(logits, axis=-1)
        bias = jnp.einsum('bijk,hk->bhij', relation_probs, logical_bias)
        gate = jax.nn.sigmoid(x @ gate_W.T + gate_b)
        gate = jnp.transpose(gate, (0, 2, 1))[..., None]
        attn_scores = attn_scores + gate * bias
        attn_weights = jax.nn.softmax(attn_scores, axis=-1)
        out = jnp.einsum('bhij,bjhd->bihd', attn_weights, v).reshape(b, s, d)
        return out @ Wo.T + bo

    def _L0_xattn_ref(tgt, mem, attn_bias, memory_key_padding_mask, Wq_w, Wq_b, Wkv_w, Wkv_b, out_w, out_b):
        import jax, jax.numpy as jnp
        import numpy as np
        EMBED_DIM = 256
        NUM_HEADS = 16
        HEAD_DIM = EMBED_DIM // NUM_HEADS
        B, SQ, SK = (2, 512, 512)
        b, sq, _ = tgt.shape
        sk = mem.shape[1]
        q = (tgt @ Wq_w.T + Wq_b).reshape(b, sq, NUM_HEADS, HEAD_DIM)
        kv = (mem @ Wkv_w.T + Wkv_b).reshape(b, sk, 2, NUM_HEADS, HEAD_DIM)
        k, v = (kv[:, :, 0], kv[:, :, 1])
        scale = 1.0 / np.sqrt(HEAD_DIM)
        scores = jnp.einsum('bthd,bshd->bhts', q, k * scale)
        scores = scores + attn_bias[:, None, None, :]
        pad = jnp.where(memory_key_padding_mask, 0.0, -jnp.inf).astype(scores.dtype)
        scores = scores + pad[:, None, None, :]
        attn = jax.nn.softmax(scores, axis=-1)
        ctx = jnp.einsum('bhts,bshd->bthd', attn, v)
        out = ctx.reshape(b, sq, EMBED_DIM) @ out_w.T + out_b
        return out

    def _L0_ffn_ref(x, w_gate, w_up, w_down):
        import jax, jax.numpy as jnp
        import numpy as np
        HIDDEN = 256
        INNER = 1024

        def _weight_quant(w):
            scale = 1.0 / jnp.clip(jnp.mean(jnp.abs(w)), 1e-05)
            wq = jnp.clip(jnp.round(w * scale), -1.0, 1.0) / scale
            return w + jax.lax.stop_gradient(wq - w)

        def _act_quant(x):
            scale = 127.0 / jnp.clip(jnp.max(jnp.abs(x), axis=-1, keepdims=True), 1e-05)
            xq = jnp.clip(jnp.round(x * scale), -128.0, 127.0) / scale
            return x + jax.lax.stop_gradient(xq - x)

        def _bitlinear(x, w):
            return jnp.einsum('bsi,oi->bso', _act_quant(x), _weight_quant(w))
        gate = jax.nn.silu(_bitlinear(x, w_gate))
        up = _bitlinear(x, w_up)
        return _bitlinear(gate * up, w_down)

    def _L1_attn_ref(x, Wq, Wk, Wv, Wb, Wa, A_log, dt_bias, Wg, o_norm_w, Wo, W_fc, W_proj):
        import jax, jax.numpy as jnp
        import numpy as np
        from functools import partial
        B, S, D, H, DK, DV, DFF = (4, 512, 256, 8, 128, 128, 1024)
        EPS = 1e-06

        def rms_norm(x):
            return x * jax.lax.rsqrt(jnp.mean(x * x, axis=-1, keepdims=True) + EPS)

        def l2norm(x):
            return x * jax.lax.rsqrt(jnp.sum(x * x, axis=-1, keepdims=True) + EPS)

        def gated_delta_net(h, Wq, Wk, Wv, Wb, Wa, A_log, dt_bias, Wg, o_norm_w, Wo):
            b, s, _ = h.shape
            q = l2norm(jax.nn.silu(h @ Wq).reshape(b, s, H, DK))
            k = l2norm(jax.nn.silu(h @ Wk).reshape(b, s, H, DK))
            v = jax.nn.silu(h @ Wv).reshape(b, s, H, DV)
            beta = jax.nn.sigmoid(h @ Wb)
            g = -jnp.exp(A_log) * jax.nn.softplus(h @ Wa + dt_bias)
            alpha = jnp.exp(g)
            scale = DK ** (-0.5)
            tm = lambda a: jnp.moveaxis(a, 1, 0)
            qs, ks_, vs, als, bts = (tm(q), tm(k), tm(v), tm(alpha), tm(beta))

            def step(Sst, inp):
                q_t, k_t, v_t, a_t, b_t = inp
                Sst = Sst * a_t[..., None, None]
                kv = jnp.einsum('bhd,bhde->bhe', k_t, Sst)
                delta = (v_t - kv) * b_t[..., None]
                Sst = Sst + jnp.einsum('bhd,bhe->bhde', k_t, delta)
                o_t = jnp.einsum('bhd,bhde->bhe', q_t, Sst) * scale
                return (Sst, o_t)
            S0 = jnp.zeros((b, H, DK, DV), dtype=h.dtype)
            _, o = jax.lax.scan(step, S0, (qs, ks_, vs, als, bts))
            o = jnp.moveaxis(o, 0, 1)
            gate = (h @ Wg).reshape(b, s, H, DV)
            o = rms_norm(o) * o_norm_w * jax.nn.silu(gate)
            return o.reshape(b, s, H * DV) @ Wo
        ln_scale = 1.0
        h = gated_delta_net(ln_scale * rms_norm(x), Wq, Wk, Wv, Wb, Wa, A_log, dt_bias, Wg, o_norm_w, Wo)
        x = x + h
        m = ln_scale * rms_norm(x)
        y = jnp.square(jax.nn.relu(m @ W_fc)) @ W_proj
        return x + y

    def _L1_xattn_ref(q, k, v, mask, wq, wk, wv, ln_gamma, ln_beta, dense_w, dense_b):
        import jax, jax.numpy as jnp
        import numpy as np
        D_MODEL = 256
        HEADS = 16
        DEPTH = D_MODEL // HEADS
        B, S = (4, 1024)
        EPS_K = 1e-06
        EPS_LN = 1e-06

        def _layernorm(x, g, b):
            m = jnp.mean(x, axis=-1, keepdims=True)
            var = jnp.var(x, axis=-1, keepdims=True)
            return (x - m) * jax.lax.rsqrt(var + EPS_LN) * g + b

        def _split_heads(x):
            bsz, sl, _ = x.shape
            return x.reshape(bsz, sl, HEADS, DEPTH).transpose(0, 2, 1, 3)
        bsz = q.shape[0]
        em = mask[:, None, :, None]
        qh = _split_heads(_layernorm(q @ wq, ln_gamma, ln_beta))
        kh = _split_heads(_layernorm(k @ wk, ln_gamma, ln_beta))
        vh = _split_heads(_layernorm(v @ wv, ln_gamma, ln_beta))
        q_prime = jax.nn.relu(qh) + EPS_K
        k_prime = (jax.nn.relu(kh) + EPS_K) * em
        vh = vh * em
        kv = jnp.einsum('bhnd,bhne->bhde', k_prime, vh)
        z = 1.0 / (jnp.einsum('bhnd,bhd->bhn', q_prime, k_prime.sum(axis=-2)) + EPS_K)
        att = jnp.einsum('bhnd,bhde,bhn->bhne', q_prime, kv, z)
        att = att.reshape(bsz, -1, D_MODEL)
        out = att @ dense_w + dense_b
        return _layernorm(out, ln_gamma, ln_beta)

    def _L1_ffn_ref(src, Wq, Wk_c, Wv_c, Wk, Wv, Wo, W_shared_in, W_shared_out, W1_shared, W2_experts, Wg_gate, We_gate, group_bias, expert_bias, norm1_w, norm2_w):
        import jax, jax.numpy as jnp
        import numpy as np
        D = 256
        H = 16
        DH = D // H
        DC = D // 4
        HID = 512
        G = 2
        EPG = 4
        E = G * EPG
        TOPK = 2
        EPS = 1e-06
        B, T = (2, 512)

        def _rope_sincos(t, dh):
            inv_freq = 1.0 / 10000.0 ** (jnp.arange(0, dh, 2, dtype=jnp.float32) / dh)
            ang = jnp.arange(t, dtype=jnp.float32)[:, None] * inv_freq[None, :]
            return (jnp.sin(ang), jnp.cos(ang))

        def _apply_rope(x, sin, cos):
            x1 = x[..., ::2]
            x2 = x[..., 1::2]
            r = jnp.stack([x1 * cos - x2 * sin, x1 * sin + x2 * cos], axis=-1)
            return r.reshape(x.shape)

        def _swiglu(x):
            a, b = jnp.split(x, 2, axis=-1)
            return jax.nn.silu(a) * b

        def _rmsnorm(x, w):
            return x * jax.lax.rsqrt(jnp.mean(x * x, axis=-1, keepdims=True) + EPS) * w
        Bb, Tt, C = src.shape
        q = (src @ Wq).reshape(Bb, Tt, H, DH).transpose(0, 2, 1, 3)
        k = (src @ Wk_c @ Wk).reshape(Bb, Tt, H, DH).transpose(0, 2, 1, 3)
        v = (src @ Wv_c @ Wv).reshape(Bb, Tt, H, DH).transpose(0, 2, 1, 3)
        sin, cos = _rope_sincos(Tt, DH)
        q = _apply_rope(q, sin, cos)
        k = _apply_rope(k, sin, cos)
        attn = jnp.einsum('bhqd,bhkd->bhqk', q, k) / np.sqrt(DH).astype(np.float32)
        attn = jax.nn.softmax(attn, axis=-1)
        sa = jnp.einsum('bhqk,bhkd->bhqd', attn, v)
        sa = sa.transpose(0, 2, 1, 3).reshape(Bb, Tt, C) @ Wo
        x = _rmsnorm(src + sa, norm1_w)
        S = Bb * Tt
        flat = x.reshape(S, C)
        shared = _swiglu(flat @ W_shared_in) @ W_shared_out
        g_probs = jax.nn.softmax(flat @ Wg_gate + group_bias, -1)
        g_idx = jnp.argmax(g_probs, axis=-1)
        e_logits = flat @ We_gate + expert_bias
        e_group = jnp.arange(E) // EPG
        in_group = e_group[None, :] == g_idx[:, None]
        e_probs = jax.nn.softmax(jnp.where(in_group, e_logits, -jnp.inf), -1)
        g_prob = jnp.take_along_axis(g_probs, g_idx[:, None], axis=1)
        p_expert = e_probs * g_prob
        topv, topi = jax.lax.top_k(p_expert, TOPK)
        w = jnp.zeros((S, E), flat.dtype).at[jnp.arange(S)[:, None], topi].set(topv)
        h = _swiglu(flat @ W1_shared)
        routed = jnp.zeros_like(shared)
        for e in range(E):
            routed = routed + h @ W2_experts[e] * w[:, e:e + 1]
        out = x + (shared + routed).reshape(Bb, Tt, C)
        return _rmsnorm(out, norm2_w)
    x = x + _L0_attn_ref(_layernorm(x, axis=-1), L0_attn_Wq, L0_attn_bq, L0_attn_Wk, L0_attn_bk, L0_attn_Wv, L0_attn_bv, L0_attn_Wo, L0_attn_bo, L0_attn_rel_W, L0_attn_rel_b, L0_attn_logical_bias, L0_attn_gate_W, L0_attn_gate_b)
    x = x + _L0_xattn_ref(_layernorm(x, axis=-1), ctx_1024, fside_BxS2_0, mask_BxS2_bk0, L0_xattn_Wq_w, L0_xattn_Wq_b, L0_xattn_Wkv_w, L0_xattn_Wkv_b, L0_xattn_out_w, L0_xattn_out_b)
    x = x + _L0_ffn_ref(_layernorm(x, axis=-1), L0_ffn_w_gate, L0_ffn_w_up, L0_ffn_w_down)
    x = x + _L1_attn_ref(_layernorm(x, axis=-1), L1_attn_Wq, L1_attn_Wk, L1_attn_Wv, L1_attn_Wb, L1_attn_Wa, L1_attn_A_log, L1_attn_dt_bias, L1_attn_Wg, L1_attn_o_norm_w, L1_attn_Wo, L1_attn_W_fc, L1_attn_W_proj)
    x = x + _L1_xattn_ref(_layernorm(x, axis=-1), ctx_1024, ctx_1024, mask_BxS2_ff1, L1_xattn_wq, L1_xattn_wk, L1_xattn_wv, L1_xattn_ln_gamma, L1_xattn_ln_beta, L1_xattn_dense_w, L1_xattn_dense_b)
    x = x + _L1_ffn_ref(_layernorm(x, axis=-1), L1_ffn_Wq, L1_ffn_Wk_c, L1_ffn_Wv_c, L1_ffn_Wk, L1_ffn_Wv, L1_ffn_Wo, L1_ffn_W_shared_in, L1_ffn_W_shared_out, L1_ffn_W1_shared, L1_ffn_W2_experts, L1_ffn_Wg_gate, L1_ffn_We_gate, L1_ffn_group_bias, L1_ffn_expert_bias, L1_ffn_norm1_w, L1_ffn_norm2_w)
    return x

_drawn_inputs = setup_inputs


def setup_inputs(seed=0):
    import zlib

    import numpy as np

    out = dict(_drawn_inputs(seed))
    spreads = {'L0_attn_bq': (0.0, 0.8),
     'L0_attn_bk': (0.0, 2.0),
     'L0_attn_bv': (0.0, 0.328),
     'L0_attn_bo': (0.0, 0.1),
     'L0_attn_rel_b': (0.0, 2.0),
     'L0_attn_gate_b': (0.0, 2.0),
     'L0_xattn_Wq_b': (0.0, 0.359),
     'L0_xattn_Wkv_b': (0.0, 0.1),
     'L0_xattn_out_b': (0.0, 0.1),
     'L1_attn_o_norm_w': (1.0, 0.6),
     'L1_xattn_ln_gamma': (1.0, 0.2),
     'L1_xattn_ln_beta': (0.0, 0.1),
     'L1_xattn_dense_b': (0.0, 0.1),
     'L1_ffn_group_bias': (0.0, 0.8),
     'L1_ffn_expert_bias': (0.0, 0.8),
     'L1_ffn_norm1_w': (1.0, 0.2),
     'L1_ffn_norm2_w': (1.0, 0.2)}
    factors = {'L0_attn_Wq': 8.0,
     'L0_attn_Wk': 8.0,
     'L0_attn_Wv': 8.0,
     'L0_attn_rel_W': 8.0,
     'L0_attn_logical_bias': 8.0,
     'L0_attn_gate_W': 22.598,
     'L1_attn_Wq': 2.676,
     'L1_attn_Wb': 8.0,
     'L1_attn_Wa': 97.076,
     'L1_attn_A_log': 22.178,
     'L1_attn_dt_bias': 122.904,
     'L1_ffn_Wq': 8.0,
     'L1_ffn_Wk_c': 8.0,
     'L1_ffn_Wv_c': 8.0,
     'L1_ffn_Wk': 8.0,
     'L1_ffn_Wv': 8.0,
     'L1_ffn_Wo': 8.0,
     'L1_ffn_W_shared_in': 7.537,
     'L1_ffn_W_shared_out': 7.635,
     'L1_ffn_W1_shared': 8.0,
     'L1_ffn_W2_experts': 8.0,
     'L1_ffn_Wg_gate': 8.0,
     'L1_ffn_We_gate': 8.0}
    for name, (base, spread) in spreads.items():
        noise = np.random.default_rng([zlib.crc32(name.encode()), seed]).standard_normal(out[name].shape)
        drawn = base * np.exp(spread * noise) if base else spread * noise
        out[name] = jnp.asarray(drawn.astype(out[name].dtype))
    for name, factor in factors.items():
        out[name] = (out[name] * factor).astype(out[name].dtype)
    return out
```

```python
import numpy as np
from contextlib import ExitStack

import concourse.bass as bass
from concourse import mybir

F32 = mybir.dt.float32
BF16 = mybir.dt.bfloat16
ALU = mybir.AluOpType
ACT = mybir.ActivationFunctionType
AX = mybir.AxisListType

P = 128
B, S, D = 4, 1024, 256
T = B * S
TILES = T // P
TPB = S // P
KD = D // P
NH = 16
HD = D // NH
SPLIT = 6
Q_PART = (0, 0, 1, 1, 0, 2)
K_PART = (0, 1, 0, 1, 2, 0)


class Link:

    def __init__(self, eng, sem, per, turn=None):
        self.eng, self.sem, self.per, self.turn, self.n = eng, sem, per, turn, 0

    def __call__(self, ins):
        self.n += 1
        ins.then_inc(self.sem, 1)
        self.eng.wait_ge(self.sem, self.n if self.turn is None else self.turn * self.per + self.n)

    def alone(self, ins, passed):
        self.n += 1
        ins.then_inc(self.sem, 1)
        hold(self.eng, passed, self.sem, self.n if self.turn is None else self.turn * self.per + self.n)

    def done(self):
        assert self.turn is None or self.n == self.per, (self.n, self.per)


def hold(eng, passed, sem, value):
    eng.wait_ge(sem, value)
    eng.sem_inc(passed, 1)


class Room:

    def __init__(self, nc, ctx, stage):
        self.nc, self.ctx, self.stage, self.sems = nc, ctx, stage, []
        ctx.callback(self.leave)
        self.passed = self.sem("passed")

    def sb(self, name, shape, dt=F32):
        return self.ctx.enter_context(self.nc.sbuf_tensor(f"{self.stage}_{name}", shape, dt))

    def ps(self, name, shape, dt=F32):
        return self.ctx.enter_context(self.nc.psum_tensor(f"{self.stage}_{name}", shape, dt))

    def sem(self, name):
        self.sems.append(self.nc.alloc_semaphore(f"{self.stage}_{name}"))
        return self.sems[-1]

    def leave(self):
        self.nc.all_engine_barrier()
        self.nc.clear_and_free_semaphores(self.sems)
        self.nc.all_engine_barrier()


def rows_in(w):
    return w.rearrange("(c p) n -> p c n", p=P)


def stage_pre0(nc, d):
    G = 4
    W = G * P
    NR = D + NH + 3
    with ExitStack() as ctx:
        r = Room(nc, ctx, "pre0")
        ident = r.sb("ident", [P, P])
        wq, wk = r.sb("wq", [P, KD, D]), r.sb("wk", [P, KD, D])
        wrow = r.sb("wrow", [P, KD, NR])
        wlj, wld = r.sb("wlj", [P, KD, 3]), r.sb("wld", [P, KD, 3])
        bq, bk = r.sb("bq", [P, KD]), r.sb("bk", [P, KD])
        bqs = r.sb("bqs", [P, KD])
        brow = r.sb("brow", [P, NR])
        lb = r.sb("lb", [P, 3, NH])
        x = r.sb("x", [P, G, D])
        st = r.sb("st", [P, G, 6])
        mv = r.sb("mv", [P, G, 2])
        var, rstd, half, eps = [r.sb(n, [P, G]) for n in ("var", "rstd", "half", "eps")]
        xn = r.sb("xn", [P, G, D])
        xt = r.sb("xt", [P, KD, W])
        qf, qr = r.sb("qf", [P, 2, W]), r.sb("qr", [P, 2, W])
        parts = r.sb("parts", [P, 2, 3, W], BF16)
        ljs = r.sb("ljs", [3, W])
        row = r.sb("row", [P, 2, NR])
        aux = r.sb("aux", [P, 2, 4 + 3 * NH])
        gate = r.sb("gate", [P, 2, NH])
        tp = [r.ps(f"tp{n}", [P, KD, P]) for n in range(2)]
        qk = [r.ps(f"qk{n}", [P, W]) for n in range(2)]
        ljp = r.ps("ljp", [3, W])
        rowp = [r.ps(f"rowp{n}", [P, NR]) for n in range(2)]

        w_in, consts, x_in, x_free = r.sem("w_in"), r.sem("consts"), r.sem("x_in"), r.sem("x_free")
        mv_done, rstd_done, xn_done = r.sem("mv_done"), r.sem("rstd_done"), r.sem("xn_done")
        tp_done, xt_done, mm_done = r.sem("tp_done"), r.sem("xt_done"), r.sem("mm_done")
        qk_done, qf_done, qk_free = r.sem("qk_done"), r.sem("qf_done"), r.sem("qk_free")
        parts_done, parts_out = r.sem("parts_done"), [r.sem(f"parts_out{n}") for n in range(2)]
        lj_done, lj_free, lj_out = r.sem("lj_done"), r.sem("lj_free"), r.sem("lj_out")
        row_done, row_free, gate_in, gate_done = r.sem("row_done"), r.sem("row_free"), r.sem("gate_in"), r.sem("gate_done")
        v_out, aux_out = [[r.sem(f"{a}{n}") for n in range(2)] for a in ("v_out", "aux_out")]
        aux_done = r.sem("aux_done")
        chain, pchain = r.sem("chain"), r.sem("pchain")
        block = ctx.enter_context(nc.Block())
        LOADS = 14

        @block.sync
        def _(sp):
            for dst, src in (
                (ident[:], d["ident"]), (wq[:], rows_in(d["L0_attn_WqT"])), (wk[:], rows_in(d["L0_attn_WkT"])),
                (wrow[:, :, 0:D], rows_in(d["L0_attn_WvT"])), (wrow[:, :, D:D + NH], rows_in(d["L0_attn_gate_WT"])),
                (wrow[:, :, D + NH:NR], rows_in(d["L0_attn_rel_WT"][0:D, :])),
                (wlj[:], rows_in(d["L0_attn_rel_WT"][D:2 * D, :])),
                (bq[:], d["L0_attn_bq_cols"]), (bk[:], d["L0_attn_bk_cols"]),
                (brow[:, 0:D], d["L0_attn_bv"].partition_broadcast(P)),
                (brow[:, D:D + NH], d["L0_attn_gate_b"].partition_broadcast(P)),
                (brow[:, D + NH:NR], d["L0_attn_rel_b"].partition_broadcast(P)),
                (lb[:], d["L0_attn_logical_biasT"].partition_broadcast(P)),
            ):
                sp.dma_start(dst, src).then_inc(w_in, 16)
            with sp.Fori(0, T // W) as i:
                hold(sp, r.passed, x_free, i + 1)
                sp.dma_start(x[:], d["x"][bass.ds(i * W, W), :].rearrange("(s p) c -> p s c", p=P)).then_inc(x_in, 16)
                for n in range(4):
                    dst = d["q3"] if n < 2 else d["k3"]
                    c = n % 2
                    hold(sp, r.passed, parts_done, i * 4 + n + 1)
                    sp.dma_start(dst[:, c * P:(c + 1) * P, bass.ds(i * W, W)].rearrange("a p t -> p a t"),
                                 parts[:, n % 2]).then_inc(parts_out[n % 2], 16)
                hold(sp, r.passed, lj_done, 2 * i + 2)
                sp.dma_start(d["ljd"][:, bass.ds(i * W, W)], ljs[:]).then_inc(lj_out, 16)
                for s in range(G):
                    hold(sp, r.passed, aux_done, i * G + s + 1)
                    sp.dma_start(d["v0"][bass.ds(i * W + s * P, P), :], row[:, s % 2, 0:D]).then_inc(v_out[s % 2], 16)
                    sp.dma_start(d["aux"][bass.ds(i * W + s * P, P), :], aux[:, s % 2]).then_inc(aux_out[s % 2], 16)
            sp.wait_ge(lj_out, 16 * (T // W))
            for n in range(2):
                sp.wait_ge(v_out[n], 16 * TILES // 2)
                sp.wait_ge(aux_out[n], 16 * TILES // 2)
                sp.wait_ge(parts_out[n], 16 * 2 * (T // W))

        @block.gpsimd
        def _(pool):
            pool.memset(eps[:], 1e-5)
            pool.memset(half[:], -0.5).then_inc(pchain, 1)
            pool.wait_ge(pchain, 1)
            with pool.Fori(0, T // W) as i:
                pool.wait_ge(mv_done, i + 1)
                pool.tensor_tensor(var[:], mv[:, :, 1], eps[:], ALU.add).then_inc(pchain, 1)
                pool.wait_ge(pchain, i + 2)
                pool.tensor_tensor(rstd[:], var[:], half[:], ALU.pow).then_inc(rstd_done, 1)

        @block.vector
        def _(dve):
            dve.wait_ge(w_in, 16 * 13)
            for c, (a, b) in enumerate(((1, 0), (2, 0), (2, 1))):
                dve.tensor_tensor(wld[:, :, c], wlj[:, :, a], wlj[:, :, b], ALU.subtract)
            dve.tensor_tensor(lb[:, 0:2], lb[:, 0:2], lb[:, 2:3].to_broadcast([P, 2, NH]), ALU.subtract)
            dve.tensor_scalar(bqs[:], bq[:], HD ** -0.5, None, ALU.mult).then_inc(consts, 1)
            dve.sem_inc(x_free, 1)
            dve.sem_inc(qk_free, 2)
            dve.sem_inc(row_free, 2)
            dve.sem_inc(lj_free, 1)
            with dve.Fori(0, T // W) as i:
                link = Link(dve, chain, 37, i)
                dve.wait_ge(x_in, i * 16 + 16)
                for s in range(G):
                    ins = dve.bn_stats(st[:, s], x[:, s])
                link.alone(ins, r.passed)
                for s in range(G):
                    ins = dve.bn_aggr(mv[:, s], st[:, s])
                ins.then_inc(mv_done, 1)
                dve.wait_ge(rstd_done, i + 1)
                for s in range(G):
                    ins = dve.tensor_scalar(xn[:, s], x[:, s], mv[:, s, 0:1], rstd[:, s:s + 1], ALU.subtract, ALU.mult)
                    ins.then_inc(xn_done, 1)
                dve.wait_ge(xn_done, i * G + G)
                dve.sem_inc(x_free, 1)
                for n in range(4):
                    h = n % 2
                    dve.wait_ge(qf_done, i * 4 + n + 1)
                    dve.wait_ge(parts_out[h], i * 32 + 16 * (n // 2))
                    link(dve.tensor_copy(parts[:, h, 0], qf[:, h]))
                    link(dve.tensor_tensor(qr[:, h], qf[:, h], parts[:, h, 0], ALU.subtract))
                    dve.sem_inc(qk_free, 1)
                    link(dve.tensor_copy(parts[:, h, 1], qr[:, h]))
                    link(dve.tensor_tensor(parts[:, h, 2], qr[:, h], parts[:, h, 1], ALU.subtract))
                    dve.sem_inc(parts_done, 1)
                dve.wait_ge(lj_done, 2 * i + 1)
                dve.wait_ge(lj_out, i * 16)
                dve.tensor_copy(ljs[:], ljp[:]).then_inc(lj_done, 1)
                for s in range(G):
                    h = s % 2
                    dve.wait_ge(row_done, i * G + s + 1)
                    dve.wait_ge(v_out[h], i * 32 + 16 * (s // 2))
                    dve.wait_ge(aux_out[h], i * 32 + 16 * (s // 2))
                    link(dve.tensor_tensor(row[:, h], rowp[h][:], brow[:], ALU.add))
                    dve.sem_inc(gate_in, 1)
                    link(dve.tensor_tensor(aux[:, h, 0:1], row[:, h, D + NH + 1:D + NH + 2], row[:, h, D + NH:D + NH + 1], ALU.subtract))
                    link(dve.tensor_tensor(aux[:, h, 1:3], row[:, h, D + NH + 2:D + NH + 3].to_broadcast([P, 2]), row[:, h, D + NH:D + NH + 2], ALU.subtract))
                    link(dve.memset(aux[:, h, 3:4], 0.0))
                    dve.wait_ge(gate_done, i * G + s + 1)
                    link(dve.tensor_tensor(aux[:, h, 4:].rearrange("p (a h) -> p a h", a=3), lb[:],
                                           gate[:, h:h + 1].to_broadcast([P, 3, NH]), ALU.mult))
                    dve.sem_inc(aux_done, 1)
                    dve.sem_inc(row_free, 1)
                link.done()

        @block.scalar
        def _(act):
            act.wait_ge(consts, 1)
            with act.Fori(0, T // W) as i:
                act.wait_ge(mm_done, i)
                for s in range(G):
                    act.wait_ge(tp_done, i * G + s + 1)
                    act.activation(xt[:, :, s * P:(s + 1) * P], tp[s % 2][:], ACT.Copy).then_inc(xt_done, 1)
                for n in range(4):
                    c, h = n % 2, n % 2
                    act.wait_ge(qk_done, i * 4 + n + 1)
                    act.wait_ge(qk_free, i * 4 + n + 1)
                    if n < 2:
                        act.activation(qf[:, h], qk[h][:], ACT.Identity, bias=bqs[:, c:c + 1], scale=HD ** -0.5).then_inc(qf_done, 1)
                    else:
                        act.activation(qf[:, h], qk[h][:], ACT.Identity, bias=bk[:, c:c + 1]).then_inc(qf_done, 1)
                for s in range(G):
                    h = s % 2
                    act.wait_ge(gate_in, i * G + s + 1)
                    act.activation(gate[:, h], row[:, h, D:D + NH], ACT.Sigmoid).then_inc(gate_done, 1)

        @block.tensor
        def _(pe):
            pe.wait_ge(w_in, 16 * 13)
            pe.wait_ge(consts, 1)
            pe.sem_inc(xt_done, 2)
            with pe.Fori(0, T // W) as i:
                for s in range(G):
                    pe.wait_ge(xn_done, i * G + s + 1)
                    pe.wait_ge(xt_done, i * G + s + 1)
                    for c in range(KD):
                        ins = pe.transpose(tp[s % 2][:, c], xn[:, s, c * P:(c + 1) * P], ident[:])
                    ins.then_inc(tp_done, 1)
                pe.wait_ge(xt_done, i * G + G + 2)
                for n in range(4):
                    w = wq if n < 2 else wk
                    c = n % 2
                    if n >= 2:
                        pe.wait_ge(qf_done, i * 4 + n - 1)
                    else:
                        pe.wait_ge(qf_done, i * 4)
                    for k in range(KD):
                        ins = pe.matmul(qk[n % 2][:], w[:, k, c * P:(c + 1) * P], xt[:, k], start=k == 0, stop=k == KD - 1)
                    ins.then_inc(qk_done, 1)
                pe.wait_ge(lj_done, 2 * i)
                for k in range(KD):
                    ins = pe.matmul(ljp[:], wld[:, k], xt[:, k], start=k == 0, stop=k == KD - 1)
                ins.then_inc(lj_done, 1)
                for s in range(G):
                    pe.wait_ge(row_free, i * G + s + 1)
                    for k in range(KD):
                        ins = pe.matmul(rowp[s % 2][:], xt[:, k, s * P:(s + 1) * P], wrow[:, k], start=k == 0, stop=k == KD - 1)
                    if s < G - 1:
                        ins.then_inc(row_done, 1)
                ins.then_inc(row_done, 1)
                pe.wait_ge(row_done, i * G + G)
                pe.sem_inc(mm_done, 1)




def stage_attn0(nc, d):
    NB = S // P
    GR = 4
    ROWS = SPLIT * HD
    with ExitStack() as ctx:
        r = Room(nc, ctx, "attn0")
        ident = r.sb("ident", [P, P])
        kt = r.sb("kt", [ROWS, NH, S], BF16)
        qt = r.sb("qt", [ROWS, 2, NH, P], BF16)
        vs = r.sb("vs", [P, NB, D])
        v32 = r.sb("v32", [P, NB, NH, 32])
        lj = r.sb("lj", [P, 3, S])
        aux = r.sb("aux", [P, 2, 4 + 3 * NH])
        dif = r.sb("dif", [P, 3, S])
        ex = r.sb("ex", [P, 4, S])
        rel = r.sb("rel", [P, 2, S])
        u = r.sb("u", [P, 4, S])
        ns = r.sb("ns", [P, 2, S])
        nm = r.sb("nm", [P, NH])
        pr = r.sb("pr", [P, 2, S])
        pt = r.sb("pt", [P, 2 * GR, NB, P])
        os_ = r.sb("os", [P, GR, P])
        rs = r.sb("rs", [P, NH])
        row = r.sb("row", [P, 2, D])
        sc = [r.ps(f"s{n}", [P, 2, 512]) for n in range(2)]
        tp = [r.ps(f"tp{n}", [P, 4, P]) for n in range(2)]
        op = r.ps("op", [P, GR, P])
        ot = r.ps("ot", [P, GR, P])
        names = ("id_in kv_in kv_free v_ready q_in0 q_in1 q_free dif_done ex_done rel_done "
                 "u_done u_free qk_done s_free ns_done exp_done tp_done "
                 "pt_done pv_done os_done ot_done row_done out0 out1 chain pchain")
        m = {n: r.sem(n) for n in names.split()}
        block = ctx.enter_context(nc.Block())

        def tiles(eng, before=None, after=None):
            with eng.Fori(0, B) as b:
                if before:
                    before(b)
                with eng.Fori(0, TPB // 2) as ih:
                    for z in range(2):
                        yield b, z, b * TPB + ih * 2 + z, b * (TPB // 2) + ih
                if after:
                    after(b)

        @block.sync
        def _(sp):
            sp.dma_start(ident[:], d["ident"]).then_inc(m["id_in"], 16)

            def load_batch(b):
                hold(sp, r.passed, m["kv_free"], b + 1)
                for slot in range(SPLIT):
                    sp.dma_start(kt[slot * HD:(slot + 1) * HD], d["k3"][K_PART[slot], :, bass.ds(b * S, S)]
                                 .rearrange("(h e) t -> e h t", e=HD)).then_inc(m["kv_in"], 16)
                sp.dma_start(vs[:], d["v0"][bass.ds(b * S, S), :].rearrange("(n p) c -> p n c", p=P)).then_inc(m["kv_in"], 16)
                sp.dma_start(lj[:], d["ljd"][:, bass.ds(b * S, S)].partition_broadcast(P)).then_inc(m["kv_in"], 16)

            for b, z, i, pair in tiles(sp, load_batch):
                hold(sp, r.passed, m["q_free"], i + 1)
                for slot in range(SPLIT):
                    sp.dma_start(qt[slot * HD:(slot + 1) * HD, z],
                                 d["q3"][Q_PART[slot], :, bass.ds(i * P, P)].rearrange("(h e) t -> e h t", e=HD)
                                 ).then_inc(m[f"q_in{z}"], 16)
                sp.dma_start(aux[:, z], d["aux"][bass.ds(i * P, P), :]).then_inc(m[f"q_in{z}"], 16)

        @block.gpsimd
        def _(pool):
            pool.memset(v32[:, :, :, HD + 1:], 0.0)
            pool.memset(v32[:, :, :, HD:HD + 1], 1.0).then_inc(m["pchain"], 1)

            def pad_values(b):
                pool.wait_ge(m["kv_in"], b * 128 + 128)
                hold(pool, r.passed, m["pv_done"], b * TPB * GR + 2)
                pool.tensor_copy(v32[:, :, :, 0:HD], vs[:].rearrange("p n (h e) -> p n h e", e=HD)).then_inc(m["v_ready"], 1)

            for b, z, i, pair in tiles(pool, pad_values):
                hold(pool, r.passed, m["rel_done"], i + 1)
                for h in range(NH):
                    hold(pool, r.passed, m["u_free"], i * NH + h + 1)
                    pool.tensor_scalar(u[:, h % 4], rel[:, 1], aux[:, z, 4 + NH + h:5 + NH + h],
                                       aux[:, z, 4 + 2 * NH + h:5 + 2 * NH + h], ALU.mult, ALU.add).then_inc(m["u_done"], 1)
            for z in range(2):
                pool.wait_ge(m[f"out{z}"], TILES // 2 * 16)

        @block.vector
        def _(dve):
            dve.sem_inc(m["kv_free"], 1)
            dve.sem_inc(m["q_free"], 2)
            dve.sem_inc(m["u_free"], 4)
            dve.sem_inc(m["s_free"], 2)

            def batch_done(b):
                dve.sem_inc(m["kv_free"], 1)

            for b, z, i, pair in tiles(dve, after=batch_done):
                link = Link(dve, m["chain"], 2 * NH + 9, i)
                dve.wait_ge(m[f"q_in{z}"], pair * 112 + 112)
                dve.wait_ge(m["kv_in"], b * 128 + 128)
                for c in range(3):
                    ins = dve.tensor_scalar(dif[:, c], lj[:, c], aux[:, z, c:c + 1], 80.0, ALU.add, ALU.min)
                link(ins)
                link(dve.tensor_scalar(dif[:], dif[:], -80.0, None, ALU.max))
                dve.sem_inc(m["dif_done"], 1)
                for c in range(2):
                    dve.wait_ge(m["ex_done"], i * 2 + c + 1)
                    link(dve.scalar_tensor_tensor(ex[:, 2 * c], ex[:, 2 * c], 1.0, ex[:, 2 * c + 1], ALU.add, ALU.add))
                    if c == 0:
                        dve.wait_ge(m["u_done"], i * NH)
                    link(dve.reciprocal(rel[:, c], ex[:, 2 * c]))
                dve.sem_inc(m["rel_done"], 1)
                for h in range(NH):
                    dve.wait_ge(m["u_done"], i * NH + h + 1)
                    link(dve.scalar_tensor_tensor(u[:, h % 4], rel[:, 0], aux[:, z, 4 + h:5 + h], u[:, h % 4], ALU.mult, ALU.add))
                    dve.wait_ge(m["qk_done"], i * NH + h + 1)
                    hold(dve, r.passed, m["exp_done"], i * NH + h + 1)
                    link(dve.tensor_tensor_reduce(ns[:, h % 2], u[:, h % 4], sc[h % 2][:].rearrange("p a n -> p (a n)"), -1.0, 3e38,
                                                  ALU.add, ALU.min, nm[:, h:h + 1]))
                    dve.sem_inc(m["u_free"], 1)
                    dve.sem_inc(m["s_free"], 1)
                    dve.sem_inc(m["ns_done"], 1)
                dve.sem_inc(m["q_free"], 1)
                dve.wait_ge(m["ot_done"], i + 1)
                dve.wait_ge(m[f"out{z}"], pair * 16)
                v = ot[:].rearrange("p g (h e) -> p (g h) e", e=32)
                link(dve.reciprocal(rs[:].rearrange("p (h o) -> p h o", o=1), v[:, :, HD:HD + 1]))
                link(dve.tensor_tensor(row[:, z].rearrange("p (h e) -> p h e", e=HD), v[:, :, 0:HD],
                                       rs[:].rearrange("p (h o) -> p h o", o=1).to_broadcast([P, NH, HD]), ALU.mult))
                dve.sem_inc(m["row_done"], 1)
                link(dve.memset(rs[:], 0.0))
                link.done()

        @block.scalar
        def _(act):
            act.sem_inc(m["exp_done"], 2)
            for b, z, i, pair in tiles(act):
                act.wait_ge(m["dif_done"], i + 1)
                for n, (c, sign) in enumerate(((0, 1.0), (1, 1.0), (0, -1.0), (2, 1.0))):
                    ins = act.activation(ex[:, n], dif[:, c], ACT.Exp, scale=sign)
                    if n % 2:
                        ins.then_inc(m["ex_done"], 1)
                for s in range(NH + 1):
                    if s < NH:
                        act.wait_ge(m["ns_done"], i * NH + s + 1)
                        if s >= 2:
                            act.wait_ge(m["tp_done"], i * 2 * NH + 2 * (s - 1))
                        act.activation(pr[:, s % 2], ns[:, s % 2], ACT.Exp, bias=nm[:, s:s + 1], scale=-1.0).then_inc(m["exp_done"], 1)
                    if s:
                        h = s - 1
                        for k in range(2):
                            act.wait_ge(m["tp_done"], i * 2 * NH + 2 * h + k + 1)
                            if k == 0:
                                if h % GR == 0:
                                    act.wait_ge(m["pv_done"], i * GR + h // GR + 1)
                            act.activation(pt[:, h % (2 * GR), 4 * k:4 * k + 4], tp[k][:], ACT.Copy).then_inc(m["pt_done"], 1)
                act.wait_ge(m["pv_done"], i * GR + GR + 2)
                act.wait_ge(m["ot_done"], i)
                act.activation(os_[:], op[:], ACT.Copy).then_inc(m["os_done"], 1)
                act.wait_ge(m["row_done"], i + 1)
                act.dma_start(d["attn"][bass.ds(i * P, P), :], row[:, z]).then_inc(m[f"out{z}"], 16)

        @block.tensor
        def _(pe):
            pe.wait_ge(m["id_in"], 16)
            pe.sem_inc(m["pv_done"], 2)
            for b, z, i, pair in tiles(pe):
                pe.wait_ge(m[f"q_in{z}"], pair * 112 + 112)
                pe.wait_ge(m["v_ready"], b + 1)
                for s in range(NH + 3):
                    if s < NH:
                        pe.wait_ge(m["s_free"], i * NH + s + 1)
                        for k in range(2):
                            ins = pe.matmul(sc[s % 2][:, k], qt[:, z, s], kt[:, s, k * 512:(k + 1) * 512], start=True, stop=True)
                        ins.then_inc(m["qk_done"], 1)
                    if 1 <= s <= NH:
                        h = s - 1
                        pe.wait_ge(m["exp_done"], i * NH + h + 3)
                        for k in range(2):
                            pe.wait_ge(m["pt_done"], i * 2 * NH + 2 * h + k - 1) if h else pe.wait_ge(m["pt_done"], i * 2 * NH)
                            for n in range(4):
                                ins = pe.transpose(tp[k][:, n], pr[:, h % 2, (4 * k + n) * P:(4 * k + n + 1) * P], ident[:])
                            ins.then_inc(m["tp_done"], 1)
                    if s >= GR + 1 and (s - 2) % GR == GR - 1:
                        g = (s - 2) // GR
                        pe.wait_ge(m["pt_done"], i * 2 * NH + 2 * GR * (g + 1))
                        if g == 0:
                            pe.wait_ge(m["os_done"], i)
                        for n in range(NB):
                            for h4 in range(GR):
                                h = g * GR + h4
                                ins = pe.matmul(op[32 * h4:32 * h4 + 32, g], v32[:, n, h], pt[:, h % (2 * GR), n],
                                                start=n == 0, stop=n == NB - 1)
                        ins.then_inc(m["pv_done"], 1)
                pe.wait_ge(m["os_done"], i + 1)
                pe.wait_ge(m["row_done"], i)
                for g in range(GR):
                    ins = pe.transpose(ot[:, g], os_[:, g], ident[:])
                ins.then_inc(m["ot_done"], 1)


def stage_mid0(nc, d):
    SK = 77
    GR = 4
    with ExitStack() as ctx:
        r = Room(nc, ctx, "mid0")
        ident = r.sb("ident", [P, P])
        wo, wq, wk, wv = [r.sb(n, [P, KD, D]) for n in ("wo", "wq", "wk", "wv")]
        wx = r.sb("wx", [P, GR, D])
        bo, bx = r.sb("bo", [P, D]), r.sb("bx", [P, D])
        bq, bk, bks = r.sb("bq", [P, KD]), r.sb("bk", [P, KD]), r.sb("bks", [P, KD])
        bv = r.sb("bv", [SK, D])
        hm = r.sb("hm", [P, NH // 2])
        cx, cxt = r.sb("cx", [SK, D]), r.sb("cxt", [P, KD, SK])
        kt = r.sb("kt", [P, KD, SK])
        kbd = r.sb("kbd", [P, KD, NH // 2, SK])
        v32 = r.sb("v32", [SK, NH, 32])
        mski, mskf = r.sb("mski", [P, SK], mybir.dt.int32), r.sb("mskf", [P, SK])
        fb = r.sb("fb", [P, SK])
        a, x = r.sb("a", [P, 2, D]), r.sb("x", [P, 2, D])
        at = r.sb("at", [P, 2, D])
        x1 = r.sb("x1", [P, 2, D])
        st, mv = r.sb("st", [P, 2, 6]), r.sb("mv", [P, 2, 2])
        var, rstd, half, eps = [r.sb(n, [P, 2]) for n in ("var", "rstd", "half", "eps")]
        xn, xt, qt = r.sb("xn", [P, 2, D]), r.sb("xt", [P, 2, D]), r.sb("qt", [P, 2, D])
        pr = r.sb("pr", [P, 2, NH, SK])
        mx, sm = r.sb("mx", [P, 2, NH]), r.sb("sm", [P, 2, NH])
        pt = r.sb("pt", [SK, NH, P])
        ot = r.sb("ot", [P, GR, P])
        x2 = r.sb("x2", [P, 2, D])
        ps = [r.ps(f"ps{z}", [P, 2, D]) for z in range(2)]
        sc = r.ps("sc", [P, 4, 512])
        op = r.ps("op", [P, GR, P])
        names = ("w_in consts chain pchain ctx_in ctx_free ctx_t ctx_c kv_mm kv_done kv_ready kv_used")
        m = {n: r.sem(n) for n in names.split()}
        steps = ("in free at_mm at_c wo_mm wo_c mv rstd xn xt_mm xt_c q_mm q_c sc_mm sub ex pr pt_mm pt_c pv_mm pv_c out_mm x2_done out")
        e = {n: [r.sem(f"{n}{z}") for z in range(2)] for n in steps.split()}
        block = ctx.enter_context(nc.Block())
        LOADS = 17

        def pairs(eng, before, after=None):
            with eng.Fori(0, B) as b:
                before(b)
                with eng.Fori(0, TPB // 2) as ih:
                    yield b * (TPB // 2) + ih
                if after:
                    after(b)

        @block.sync
        def _(sp):
            for dst, src in (
                (ident[:], d["ident"]), (wo[:], rows_in(d["L0_attn_WoT"])), (wq[:], rows_in(d["L0_xattn_Wq_wT"])),
                (wk[:], rows_in(d["L0_xattn_Wkv_wT"][:, 0:D])), (wv[:], rows_in(d["L0_xattn_Wkv_wT"][:, D:2 * D])),
                (bo[:], d["L0_attn_bo"].partition_broadcast(P)), (bx[:], d["L0_xattn_out_b"].partition_broadcast(P)),
                (bq[:], d["L0_xattn_Wq_b_cols"]), (bk[:], d["L0_xattn_Wkv_b_cols"][:, 0:KD]),
                (bv[:], d["L0_xattn_Wkv_b"][D:2 * D].partition_broadcast(SK)), (hm[:], d["head_mask"]),
            ):
                sp.dma_start(dst, src).then_inc(m["w_in"], 16)
            sp.wait_ge(m["consts"], 1)
            wxd = d["L0_xattn_out_wT"].rearrange("(g a e) n -> a e g n", g=GR, e=HD)
            for h in range(GR):
                sp.dma_start(wx[32 * h:32 * h + HD], wxd[h]).then_inc(m["w_in"], 16)

            def context(b):
                hold(sp, r.passed, m["ctx_free"], b + 1)
                sp.dma_start(cx[:], d["ctx"][bass.ds(b * SK, SK), :]).then_inc(m["ctx_in"], 16)
                sp.dma_start(mski[:], d["mask_words"][bass.ds(b, 1), :].partition_broadcast(P).rearrange("p a k -> p (a k)")).then_inc(m["ctx_in"], 16)
                sp.dma_start(fb[:], d["fside_BxS2_0"][bass.ds(b, 1), :].partition_broadcast(P).rearrange("p a k -> p (a k)")).then_inc(m["ctx_in"], 16)

            for p in pairs(sp, context):
                for z in range(2):
                    hold(sp, r.passed, e["free"][z], p + 1)
                    sp.dma_start(a[:, z], d["attn"][bass.ds((p * 2 + z) * P, P), :]).then_inc(e["in"][z], 16)
                    sp.dma_start(x[:, z], d["x"][bass.ds((p * 2 + z) * P, P), :]).then_inc(e["in"][z], 16)
                for z in range(2):
                    hold(sp, r.passed, e["x2_done"][z], p + 1)
                    sp.dma_start(d["x2"][bass.ds((p * 2 + z) * P, P), :], x2[:, z]).then_inc(e["out"][z], 16)
            for z in range(2):
                sp.wait_ge(e["out"][z], 16 * TILES // 2)

        @block.gpsimd
        def _(pool):
            pool.memset(eps[:], 1e-5)
            pool.memset(half[:], -0.5)
            pool.memset(v32[:], 0.0)
            pool.memset(wx[:], 0.0).then_inc(m["consts"], 1)
            pool.wait_ge(m["consts"], 1)

            for p in pairs(pool, lambda b: None):
                for z in range(2):
                    pool.wait_ge(e["mv"][z], p + 1)
                    pool.tensor_tensor(var[:, z:z + 1], mv[:, z, 1:2], eps[:, z:z + 1], ALU.add).then_inc(m["pchain"], 1)
                    pool.wait_ge(m["pchain"], p * 2 + z + 1)
                    pool.tensor_tensor(rstd[:, z:z + 1], var[:, z:z + 1], half[:, z:z + 1], ALU.pow).then_inc(e["rstd"][z], 1)

        @block.vector
        def _(dve):
            dve.wait_ge(m["w_in"], 16 * 15)
            dve.tensor_scalar(bks[:], bk[:], HD ** -0.5, None, ALU.mult).then_inc(m["consts"], 1)
            dve.sem_inc(m["ctx_free"], 1)
            for z in range(2):
                dve.sem_inc(e["free"][z], 1)

            def context(b):
                dve.wait_ge(m["kv_done"], KD * b + KD)
                dve.wait_ge(m["ctx_in"], 48 * b + 48)
                for c in range(KD):
                    dve.tensor_tensor(kbd[:, c], kt[:, c:c + 1].to_broadcast([P, NH // 2, SK]),
                                      hm[:].rearrange("p (h o) -> p h o", o=1).to_broadcast([P, NH // 2, SK]), ALU.mult)
                dve.tensor_tensor(v32[:, :, 0:HD], ps[0][0:SK, 1].rearrange("k (h e) -> k h e", e=HD),
                                  bv[:].rearrange("k (h e) -> k h e", e=HD), ALU.add)
                dve.tensor_scalar(mskf[:], mski[:], 1.0, None, ALU.min).then_inc(m["kv_used"], 1)
                dve.wait_ge(m["kv_used"], 3 * b + 1)
                dve.tensor_scalar(mskf[:], mskf[:], 1.0, 1e30, ALU.subtract, ALU.mult).then_inc(m["kv_used"], 1)
                dve.wait_ge(m["kv_used"], 3 * b + 2)
                dve.tensor_tensor(fb[:], fb[:], mskf[:], ALU.add).then_inc(m["kv_used"], 1)
                hold(dve, r.passed, m["kv_used"], 3 * b + 3)
                dve.sem_inc(m["kv_ready"], 1)

            for p in pairs(dve, context, lambda b: dve.sem_inc(m["ctx_free"], 1)):
                link = Link(dve, m["chain"], 2 * 9, p)
                for z in range(2):
                    dve.wait_ge(e["in"][z], 32 * p + 32)
                    dve.wait_ge(e["wo_mm"][z], p + 1)
                    link(dve.tensor_tensor(x1[:, z], x[:, z], ps[z][:, 1], ALU.add))
                    dve.sem_inc(e["free"][z], 1)
                    link(dve.tensor_tensor(x1[:, z], x1[:, z], bo[:], ALU.add))
                    link.alone(dve.bn_stats(st[:, z], x1[:, z]), r.passed)
                    dve.bn_aggr(mv[:, z], st[:, z]).then_inc(e["mv"][z], 1)
                for z in range(2):
                    dve.wait_ge(e["rstd"][z], p + 1)
                    dve.tensor_scalar(xn[:, z], x1[:, z], mv[:, z, 0:1], rstd[:, z:z + 1], ALU.subtract, ALU.mult).then_inc(e["xn"][z], 1)
                for z in range(2):
                    s4 = pr[:, z].rearrange("p (g h) k -> p g h k", g=GR)
                    dve.wait_ge(e["sc_mm"][z], p + 1)
                    link(dve.tensor_tensor(s4, sc[:, :, 0:GR * SK].rearrange("p g (h k) -> p g h k", k=SK),
                                           fb[:].rearrange("p (o q k) -> p o q k", o=1, q=1).to_broadcast([P, GR, GR, SK]), ALU.add))
                    dve.sem_inc(e["sub"][z], 1)
                    link(dve.reduce_max(mx[:, z], pr[:, z], AX.X))
                    link(dve.tensor_tensor(pr[:, z], pr[:, z], mx[:, z].rearrange("p (h o) -> p h o", o=1).to_broadcast([P, NH, SK]), ALU.subtract))
                    dve.sem_inc(e["ex"][z], 1)
                    dve.wait_ge(e["ex"][z], 2 * p + 2)
                    link(dve.reduce_sum(sm[:, z], pr[:, z], AX.X))
                    link(dve.reciprocal(sm[:, z], sm[:, z]))
                    dve.tensor_tensor(pr[:, z], pr[:, z], sm[:, z].rearrange("p (h o) -> p h o", o=1).to_broadcast([P, NH, SK]),
                                      ALU.mult).then_inc(e["pr"][z], 1)
                for z in range(2):
                    dve.wait_ge(e["out"][z], 16 * p)
                    dve.wait_ge(e["out_mm"][z], p + 1)
                    link(dve.tensor_tensor(x2[:, z], x1[:, z], ps[z][:, 0], ALU.add))
                    dve.tensor_tensor(x2[:, z], x2[:, z], bx[:], ALU.add).then_inc(e["x2_done"][z], 1)
                link.done()

        @block.scalar
        def _(act):
            act.wait_ge(m["w_in"], 16 * 15)
            act.wait_ge(m["consts"], 2)

            def context(b):
                act.wait_ge(m["ctx_t"], b + 1)
                act.activation(cxt[:], ps[0][:, 0, 0:KD * SK].rearrange("p (c k) -> p c k", c=KD), ACT.Copy).then_inc(m["ctx_c"], 1)
                act.wait_ge(m["kv_mm"], b + 1)
                for c in range(KD):
                    act.activation(kt[:, c], ps[0][:, 0, c * SK:(c + 1) * SK], ACT.Identity, bias=bks[:, c:c + 1],
                                   scale=HD ** -0.5).then_inc(m["kv_done"], 1)

            for p in pairs(act, context):
                for z in range(2):
                    act.wait_ge(e["at_mm"][z], p + 1)
                    act.activation(at[:, z], ps[z][:, 0], ACT.Copy).then_inc(e["at_c"][z], 1)
                for z in range(2):
                    act.wait_ge(e["xt_mm"][z], p + 1)
                    act.activation(xt[:, z], ps[z][:, 0], ACT.Copy).then_inc(e["xt_c"][z], 1)
                for z in range(2):
                    act.wait_ge(e["q_mm"][z], p + 1)
                    for c in range(KD):
                        ins = act.activation(qt[:, z, c * P:(c + 1) * P], ps[z][:, 1, c * P:(c + 1) * P], ACT.Identity, bias=bq[:, c:c + 1])
                    ins.then_inc(e["q_c"][z], 1)
                for z in range(2):
                    act.wait_ge(e["ex"][z], 2 * p + 1)
                    act.activation(pr[:, z], pr[:, z], ACT.Exp).then_inc(e["ex"][z], 1)
                    act.wait_ge(e["pt_mm"][z], p + 1)
                    for g in range(GR):
                        ins = act.activation(pt[:, g * GR:(g + 1) * GR], sc[0:SK, g].rearrange("k (h n) -> k h n", h=GR), ACT.Copy)
                    ins.then_inc(e["pt_c"][z], 1)
                    act.wait_ge(e["pv_mm"][z], p + 1)
                    act.activation(ot[:], op[:], ACT.Copy).then_inc(e["pv_c"][z], 1)

        @block.tensor
        def _(pe):
            pe.wait_ge(m["w_in"], 16 * 15)

            def context(b):
                pe.wait_ge(m["ctx_in"], 48 * b + 48)
                pe.wait_ge(e["x2_done"][0], b * (TPB // 2))
                for c in range(KD):
                    ins = pe.transpose(ps[0][:, 0, c * SK:(c + 1) * SK], cx[:, c * P:(c + 1) * P], ident[0:SK, 0:SK])
                ins.then_inc(m["ctx_t"], 1)
                pe.wait_ge(m["ctx_c"], b + 1)
                for c in range(KD):
                    for k in range(KD):
                        pe.matmul(ps[0][:, 0, c * SK:(c + 1) * SK], wk[:, k, c * P:(c + 1) * P], cxt[:, k], start=k == 0, stop=k == KD - 1)
                for k in range(KD):
                    ins = pe.matmul(ps[0][0:SK, 1], cxt[:, k], wv[:, k], start=k == 0, stop=k == KD - 1)
                ins.then_inc(m["kv_mm"], 1)
                hold(pe, r.passed, m["kv_ready"], b + 1)

            for p in pairs(pe, context):
                for z in range(2):
                    pe.wait_ge(e["in"][z], 32 * p + 32)
                    pe.wait_ge(e["x2_done"][z], p)
                    for c in range(KD):
                        ins = pe.transpose(ps[z][:, 0, c * P:(c + 1) * P], a[:, z, c * P:(c + 1) * P], ident[:])
                    ins.then_inc(e["at_mm"][z], 1)
                for z in range(2):
                    pe.wait_ge(e["at_c"][z], p + 1)
                    for k in range(KD):
                        ins = pe.matmul(ps[z][:, 1], at[:, z, k * P:(k + 1) * P], wo[:, k], start=k == 0, stop=k == KD - 1)
                    ins.then_inc(e["wo_mm"][z], 1)
                for z in range(2):
                    pe.wait_ge(e["xn"][z], p + 1)
                    for c in range(KD):
                        ins = pe.transpose(ps[z][:, 0, c * P:(c + 1) * P], xn[:, z, c * P:(c + 1) * P], ident[:])
                    ins.then_inc(e["xt_mm"][z], 1)
                for z in range(2):
                    pe.wait_ge(e["xt_c"][z], p + 1)
                    for c in range(KD):
                        for k in range(KD):
                            ins = pe.matmul(ps[z][:, 1, c * P:(c + 1) * P], wq[:, k, c * P:(c + 1) * P], xt[:, z, k * P:(k + 1) * P],
                                            start=k == 0, stop=k == KD - 1)
                    ins.then_inc(e["q_mm"][z], 1)
                for z in range(2):
                    pe.wait_ge(e["q_c"][z], p + 1)
                    if z:
                        pe.wait_ge(e["pt_c"][0], p + 1)
                    for g in range(GR):
                        c, h = g // 2, g % 2
                        ins = pe.matmul(sc[:, g, 0:GR * SK], qt[:, z, c * P:(c + 1) * P], kbd[:, c, h * GR:(h + 1) * GR], start=True, stop=True)
                    ins.then_inc(e["sc_mm"][z], 1)
                    pe.wait_ge(e["pr"][z], p + 1)
                    for h in range(NH):
                        ins = pe.transpose(sc[0:SK, h // GR, (h % GR) * P:(h % GR + 1) * P], pr[:, z, h], ident[:])
                    ins.then_inc(e["pt_mm"][z], 1)
                    pe.wait_ge(e["pt_c"][z], p + 1)
                    for g in range(GR):
                        for h4 in range(GR):
                            h = g * GR + h4
                            ins = pe.matmul(op[32 * h4:32 * h4 + 32, g], v32[:, h], pt[:, h], start=True, stop=True)
                    ins.then_inc(e["pv_mm"][z], 1)
                    pe.wait_ge(e["pv_c"][z], p + 1)
                    for g in range(GR):
                        ins = pe.matmul(ps[z][:, 0], ot[:, g], wx[:, g], start=g == 0, stop=g == GR - 1)
                    ins.then_inc(e["out_mm"][z], 1)


def stage_ffn0(nc, d):
    INNER = 1024
    KI = INNER // P
    ROUND = 12582912.0
    with ExitStack() as ctx:
        r = Room(nc, ctx, "ffn0")
        identb = r.sb("identb", [P, P], BF16)
        ident = r.sb("ident", [P, P])
        wf = [r.sb(f"wf{n}", [P, 2 * INNER]) for n in range(3)]
        wt = [r.sb(f"wt{n}", [P, 2 * INNER], BF16) for n in range(3)]
        ones = r.sb("ones", [P, P])
        wsum, wscale, winv = r.sb("wsum", [P, 3]), r.sb("wscale", [P, 3]), r.sb("winv", [P, 3])
        x = r.sb("x", [P, 2, D])
        st, mv = r.sb("st", [P, 2, 6]), r.sb("mv", [P, 2, 2])
        var, rstd, half, eps = [r.sb(n, [P, 2]) for n in ("var", "rstd", "half", "eps")]
        xn = r.sb("xn", [P, 2, D])
        xq, xqt = r.sb("xq", [P, 2, D], BF16), r.sb("xqt", [P, 2, KD, P], BF16)
        am, asc, ainv = r.sb("am", [P, 2, 2]), r.sb("asc", [P, 2, 2]), r.sb("ainv", [P, 2, 2])
        so = r.sb("so", [P, 2, 3])
        hg, hh = r.sb("hg", [P, 2, INNER]), r.sb("hh", [P, 2, INNER])
        hq, hqt = r.sb("hq", [P, 2, INNER], BF16), r.sb("hqt", [P, 2, KI, P], BF16)
        x3 = r.sb("x3", [P, 2, D])
        pg, pu = r.ps("pg", [P, 2, 512]), r.ps("pu", [P, 2, 512])
        tp = [r.ps(f"tp{z}", [P, KI, P], BF16) for z in range(2)]
        po = [r.ps(f"po{z}", [P, D]) for z in range(2)]
        m = {n: r.sem(n) for n in "w_in consts wsum_done wtot_done w_ready chain pchain".split()}
        steps = "in free mv rstd xq xt_mm xt_c gu_mm g_c h_done hq ht_mm ht_c out_mm x3_done out"
        e = {n: [r.sem(f"{n}{z}") for z in range(2)] for n in steps.split()}
        block = ctx.enter_context(nc.Block())
        PAIRS = TILES // 2

        @block.sync
        def _(sp):
            sp.dma_start(ident[:], d["ident"]).then_inc(m["w_in"], 16)
            for n, w in enumerate(("L0_ffn_w_gateT", "L0_ffn_w_upT", "L0_ffn_w_downT")):
                c = D // P if n < 2 else KI
                sp.dma_start(wf[n][:].rearrange("p (c n) -> p c n", c=c), rows_in(d[w])).then_inc(m["w_in"], 16)
            with sp.Fori(0, PAIRS) as p:
                for z in range(2):
                    hold(sp, r.passed, e["free"][z], p + 1)
                    sp.dma_start(x[:, z], d["x2"][bass.ds((p * 2 + z) * P, P), :]).then_inc(e["in"][z], 16)
                for z in range(2):
                    hold(sp, r.passed, e["x3_done"][z], p + 1)
                    sp.dma_start(d["x3"][bass.ds((p * 2 + z) * P, P), :], x3[:, z]).then_inc(e["out"][z], 16)
            for z in range(2):
                sp.wait_ge(e["out"][z], 16 * PAIRS)

        @block.gpsimd
        def _(pool):
            pool.memset(eps[:], 1e-5)
            pool.memset(ones[:], 1.0)
            pool.memset(half[:], -0.5).then_inc(m["consts"], 1)
            pool.wait_ge(m["consts"], 1)
            with pool.Fori(0, PAIRS) as p:
                for z in range(2):
                    pool.wait_ge(e["mv"][z], p + 1)
                    pool.tensor_tensor(var[:, z:z + 1], mv[:, z, 1:2], eps[:, z:z + 1], ALU.add).then_inc(m["pchain"], 1)
                    pool.wait_ge(m["pchain"], p * 2 + z + 1)
                    pool.tensor_tensor(rstd[:, z:z + 1], var[:, z:z + 1], half[:, z:z + 1], ALU.pow).then_inc(e["rstd"][z], 1)

        @block.vector
        def _(dve):
            link = Link(dve, m["w_ready"], 0)
            dve.wait_ge(m["w_in"], 64)
            link(dve.tensor_copy(identb[:], ident[:]))
            dve.wait_ge(m["wtot_done"], 1)
            link(dve.tensor_scalar(wscale[:], po[0][:, 0:3], 1.0 / (D * INNER), 1e-5, ALU.mult, ALU.max))
            link(dve.reciprocal(wscale[:], wscale[:]))
            link(dve.reciprocal(winv[:], wscale[:]))
            for n in range(3):
                link(dve.tensor_scalar(wf[n][:], wf[n][:], wscale[:, n:n + 1], ROUND, ALU.mult, ALU.add))
                link(dve.tensor_scalar(wf[n][:], wf[n][:], ROUND, 1.0, ALU.subtract, ALU.min))
                link(dve.tensor_scalar(wt[n][:], wf[n][:], -1.0, None, ALU.max))
            prepared = link.n
            assert prepared == 13
            for z in range(2):
                dve.sem_inc(e["free"][z], 1)

            def quantise(link, q, f, z, k):
                link(dve.tensor_reduce(am[:, z, k:k + 1], f, AX.X, ALU.max, apply_absolute_value=True))
                link(dve.tensor_scalar(am[:, z, k:k + 1], am[:, z, k:k + 1], 1e-5, None, ALU.max))
                link(dve.reciprocal(asc[:, z, k:k + 1], am[:, z, k:k + 1]))
                link(dve.tensor_scalar(asc[:, z, k:k + 1], asc[:, z, k:k + 1], 127.0, None, ALU.mult))
                link(dve.reciprocal(ainv[:, z, k:k + 1], asc[:, z, k:k + 1]))
                link(dve.tensor_scalar(f, f, asc[:, z, k:k + 1], ROUND, ALU.mult, ALU.add))
                link(dve.tensor_scalar(q, f, ROUND, 127.0, ALU.subtract, ALU.min))
                link(dve.tensor_scalar(q, q, -128.0, None, ALU.max))

            with dve.Fori(0, PAIRS) as p:
                link = Link(dve, m["chain"], 2 * (1 + 10 + 9 + 1), p)
                for z in range(2):
                    dve.wait_ge(e["in"][z], 16 * p + 16)
                    link.alone(dve.bn_stats(st[:, z], x[:, z]), r.passed)
                    dve.bn_aggr(mv[:, z], st[:, z]).then_inc(e["mv"][z], 1)
                for z in range(2):
                    dve.wait_ge(e["rstd"][z], p + 1)
                    link(dve.tensor_scalar(xn[:, z], x[:, z], mv[:, z, 0:1], rstd[:, z:z + 1], ALU.subtract, ALU.mult))
                    quantise(link, xq[:, z], xn[:, z], z, 0)
                    dve.sem_inc(e["xq"][z], 1)
                    link(dve.tensor_scalar(so[:, z, 0:2], winv[:, 0:2], ainv[:, z, 0:1], None, ALU.mult))
                    dve.sem_inc(e["xq"][z], 1)
                for z in range(2):
                    dve.wait_ge(e["g_c"][z], p + 1)
                    link(dve.scalar_tensor_tensor(hh[:, z].rearrange("p (c n) -> p c n", c=2), pu[:], so[:, z, 1:2],
                                                  hg[:, z].rearrange("p (c n) -> p c n", c=2), ALU.mult, ALU.mult))
                    dve.sem_inc(e["h_done"][z], 1)
                    quantise(link, hq[:, z], hh[:, z], z, 1)
                    dve.sem_inc(e["hq"][z], 1)
                for z in range(2):
                    link(dve.tensor_tensor(so[:, z, 2:3], winv[:, 2:3], ainv[:, z, 1:2], ALU.mult))
                    dve.wait_ge(e["out"][z], 16 * p)
                    dve.wait_ge(e["out_mm"][z], p + 1)
                    dve.scalar_tensor_tensor(x3[:, z], po[z][:], so[:, z, 2:3], x[:, z], ALU.mult, ALU.add).then_inc(e["x3_done"][z], 1)
                    dve.wait_ge(e["x3_done"][z], p + 1)
                    dve.sem_inc(e["free"][z], 1)
                link.done()

        @block.scalar
        def _(act):
            act.wait_ge(m["w_in"], 64)
            for n in range(3):
                ins = act.activation((hh, hg, hq)[n][:].rearrange("p z n -> p (z n)"), wf[n][:], ACT.Abs, accum_out=wsum[:, n:n + 1])
            ins.then_inc(m["wsum_done"], 1)
            with act.Fori(0, PAIRS) as p:
                for z in range(2):
                    act.wait_ge(e["xt_mm"][z], p + 1)
                    act.activation(xqt[:, z], tp[z][:, 0:KD], ACT.Copy).then_inc(e["xt_c"][z], 1)
                for z in range(2):
                    act.wait_ge(e["xq"][z], 2 * p + 2)
                    act.wait_ge(e["gu_mm"][z], p + 1)
                    act.activation(hg[:, z].rearrange("p (c n) -> p c n", c=2), pg[:], ACT.Silu, scale=so[:, z, 0:1]).then_inc(e["g_c"][z], 1)
                for z in range(2):
                    act.wait_ge(e["ht_mm"][z], p + 1)
                    act.activation(hqt[:, z], tp[z][:], ACT.Copy).then_inc(e["ht_c"][z], 1)

        @block.tensor
        def _(pe):
            pe.wait_ge(m["consts"], 1)
            pe.wait_ge(m["wsum_done"], 1)
            pe.matmul(po[0][:, 0:3], ones[:], wsum[:], start=True, stop=True).then_inc(m["wtot_done"], 1)
            pe.wait_ge(m["w_ready"], 13)
            wg, wu = [wt[n][:].rearrange("p (c n) -> p c n", c=KD) for n in range(2)]
            wd = wt[2][:].rearrange("p (c n) -> p c n", c=KI)
            with pe.Fori(0, PAIRS) as p:
                for z in range(2):
                    pe.wait_ge(e["xq"][z], 2 * p + 1)
                    for c in range(KD):
                        ins = pe.transpose(tp[z][:, c], xq[:, z, c * P:(c + 1) * P], identb[:])
                    ins.then_inc(e["xt_mm"][z], 1)
                for z in range(2):
                    pe.wait_ge(e["xt_c"][z], p + 1)
                    if z:
                        pe.wait_ge(e["h_done"][0], p + 1)
                    for w, acc in ((wg, pg), (wu, pu)):
                        for n in range(2):
                            for k in range(KD):
                                ins = pe.matmul(acc[:, n], xqt[:, z, k], w[:, k, n * 512:(n + 1) * 512], start=k == 0, stop=k == KD - 1)
                    ins.then_inc(e["gu_mm"][z], 1)
                for z in range(2):
                    pe.wait_ge(e["hq"][z], p + 1)
                    for c in range(KI):
                        ins = pe.transpose(tp[z][:, c], hq[:, z, c * P:(c + 1) * P], identb[:])
                    ins.then_inc(e["ht_mm"][z], 1)
                for z in range(2):
                    pe.wait_ge(e["ht_c"][z], p + 1)
                    for k in range(KI):
                        ins = pe.matmul(po[z][:], hqt[:, z, k], wd[:, k], start=k == 0, stop=k == KI - 1)
                    ins.then_inc(e["out_mm"][z], 1)


GH = 8
DK = 128
GD = GH * DK


def stage_gdn_in(nc, d):
    NC = 3 * GD // 512
    with ExitStack() as ctx:
        r = Room(nc, ctx, "gin")
        ident = r.sb("ident", [P, P])
        w = r.sb("w", [P, KD, 3 * GD])
        wab = r.sb("wab", [P, KD, 2 * GH])
        x = r.sb("x", [P, 2, D])
        st, mv = r.sb("st", [P, 2, 6]), r.sb("mv", [P, 2, 2])
        va, rstd = r.sb("va", [P, 2, 2]), r.sb("rstd", [P, 2, 2])
        half = r.sb("half", [P, 2 * GH])
        ssq, junk = r.sb("ssq", [P, 2]), r.sb("junk", [P, 2, D])
        xn, xt = r.sb("xn", [P, 2, D]), r.sb("xt", [P, 2, KD, P])
        qkv = r.sb("qkv", [P, 2, 3 * GD])
        sq = r.sb("sq", [P, 2, 2 * GD])
        nq, rq = r.sb("nq", [P, 2, 2 * GH]), r.sb("rq", [P, 2, 2 * GH])
        ab = r.sb("ab", [P, 2, 2 * GH])
        tp = [r.ps(f"tp{z}", [P, KD, P]) for z in range(2)]
        pw = [r.ps(f"pw{n}", [P, 512]) for n in range(4)]
        pab = [r.ps(f"pab{z}", [P, 2 * GH]) for z in range(2)]
        m = {n: r.sem(n) for n in "w_in consts chain pw_done pw_c0 pw_c1 pw_c2 pw_c3".split()}
        steps = "in free va rstd sq va2 rstd2 xn xt_mm xt_c ab_mm ab_done qk_sq nq rq qkv_done out"
        e = {n: [r.sem(f"{n}{z}") for z in range(2)] for n in steps.split()}
        block = ctx.enter_context(nc.Block())
        PAIRS = TILES // 2
        PER = 2 * NC // 4

        @block.sync
        def _(sp):
            for dst, src in ((ident[:], d["ident"]), (w[:, :, 0:GD], rows_in(d["L1_attn_Wq"])),
                             (w[:, :, GD:2 * GD], rows_in(d["L1_attn_Wk"])), (w[:, :, 2 * GD:], rows_in(d["L1_attn_Wv"])),
                             (wab[:, :, 0:GH], rows_in(d["L1_attn_Wa"])), (wab[:, :, GH:], rows_in(d["L1_attn_Wb"]))):
                sp.dma_start(dst, src).then_inc(m["w_in"], 16)
            with sp.Fori(0, PAIRS) as p:
                for z in range(2):
                    hold(sp, r.passed, e["free"][z], p + 1)
                    sp.dma_start(x[:, z], d["x3"][bass.ds((p * 2 + z) * P, P), :]).then_inc(e["in"][z], 16)
                for z in range(2):
                    for k in (z * NC + NC - 2, z * NC + NC - 1):
                        hold(sp, r.passed, m[f"pw_c{k % 4}"], p * PER + k // 4 + 1)
                    hold(sp, r.passed, e["qkv_done"][z], p + 1)
                    sp.dma_start(d["qkv"][bass.ds((p * 2 + z) * P, P), :], qkv[:, z]).then_inc(e["out"][z], 16)
                    sp.dma_start(d["ab"][bass.ds((p * 2 + z) * P, P), :], ab[:, z]).then_inc(e["out"][z], 16)
            for z in range(2):
                sp.wait_ge(e["out"][z], 32 * PAIRS)

        @block.gpsimd
        def _(pool):
            pool.memset(half[:], -0.5).then_inc(m["consts"], 1)
            pool.wait_ge(m["consts"], 1)
            with pool.Fori(0, PAIRS) as p:
                for z in range(2):
                    pool.wait_ge(e["va"][z], p + 1)
                    pool.tensor_tensor(rstd[:, z, 0:1], va[:, z, 0:1], half[:, 0:1], ALU.pow).then_inc(e["rstd"][z], 1)
                for z in range(2):
                    pool.wait_ge(e["va2"][z], p + 1)
                    pool.tensor_tensor(rstd[:, z, 1:2], va[:, z, 1:2], half[:, 0:1], ALU.pow).then_inc(e["rstd2"][z], 1)
                for z in range(2):
                    pool.wait_ge(e["nq"][z], p + 1)
                    pool.tensor_tensor(rq[:, z], nq[:, z], half[:], ALU.pow).then_inc(e["rq"][z], 1)

        @block.vector
        def _(dve):
            for z in range(2):
                dve.sem_inc(e["free"][z], 1)
            with dve.Fori(0, PAIRS) as p:
                link = Link(dve, m["chain"], 2 * 5, p)
                for z in range(2):
                    dve.wait_ge(e["in"][z], 16 * p + 16)
                    link.alone(dve.bn_stats(st[:, z], x[:, z]), r.passed)
                    link(dve.bn_aggr(mv[:, z], st[:, z]))
                    dve.tensor_scalar(va[:, z, 0:1], mv[:, z, 1:2], 1e-5, None, ALU.add).then_inc(e["va"][z], 1)
                for z in range(2):
                    dve.wait_ge(e["rstd"][z], p + 1)
                    link(dve.tensor_scalar(xn[:, z], x[:, z], mv[:, z, 0:1], rstd[:, z, 0:1], ALU.subtract, ALU.mult))
                    dve.sem_inc(e["free"][z], 1)
                    dve.sem_inc(e["sq"][z], 1)
                for z in range(2):
                    dve.wait_ge(e["sq"][z], 2 * p + 2)
                    dve.tensor_scalar(va[:, z, 1:2], ssq[:, z:z + 1], 1.0 / D, 1e-6, ALU.mult, ALU.add).then_inc(e["va2"][z], 1)
                for z in range(2):
                    dve.wait_ge(e["rstd2"][z], p + 1)
                    dve.tensor_scalar(xn[:, z], xn[:, z], rstd[:, z, 1:2], None, ALU.mult).then_inc(e["xn"][z], 1)
                for z in range(2):
                    dve.wait_ge(e["ab_mm"][z], p + 1)
                    dve.wait_ge(e["out"][z], 32 * p)
                    dve.tensor_copy(ab[:, z], pab[z][:]).then_inc(e["ab_done"][z], 1)
                    dve.wait_ge(e["qk_sq"][z], p + 1)
                    link(dve.reduce_sum(nq[:, z], sq[:, z].rearrange("p (h e) -> p h e", e=DK), AX.X))
                    dve.tensor_scalar(nq[:, z], nq[:, z], 1e-6, None, ALU.add).then_inc(e["nq"][z], 1)
                for z in range(2):
                    dve.wait_ge(e["rq"][z], p + 1)
                    link(dve.tensor_scalar(rq[:, z, 0:GH], rq[:, z, 0:GH], DK ** -0.5, None, ALU.mult))
                    v = qkv[:, z, 0:2 * GD].rearrange("p (h e) -> p h e", e=DK)
                    dve.tensor_tensor(v, v, rq[:, z].rearrange("p (h o) -> p h o", o=1).to_broadcast([P, 2 * GH, DK]),
                                      ALU.mult).then_inc(e["qkv_done"][z], 1)
                link.done()

        @block.scalar
        def _(act):
            with act.Fori(0, PAIRS) as p:
                for z in range(2):
                    act.wait_ge(e["sq"][z], 2 * p + 1)
                    act.activation(junk[:, z], xn[:, z], ACT.Square, accum_out=ssq[:, z:z + 1]).then_inc(e["sq"][z], 1)
                for z in range(2):
                    act.wait_ge(e["xt_mm"][z], p + 1)
                    act.activation(xt[:, z], tp[z][:], ACT.Copy).then_inc(e["xt_c"][z], 1)
                for z in range(2):
                    act.wait_ge(e["out"][z], 32 * p)
                    for n in range(NC):
                        k = z * NC + n
                        act.wait_ge(m["pw_done"], p * 2 * NC + k + 1)
                        act.activation(qkv[:, z, n * 512:(n + 1) * 512], pw[k % 4][:], ACT.Silu).then_inc(m[f"pw_c{k % 4}"], 1)
                        if n == 3:
                            act.wait_ge(m[f"pw_c{k % 4}"], p * PER + k // 4 + 1)
                            act.activation(sq[:, z], qkv[:, z, 0:2 * GD], ACT.Square).then_inc(e["qk_sq"][z], 1)

        @block.tensor
        def _(pe):
            pe.wait_ge(m["w_in"], 96)
            with pe.Fori(0, PAIRS) as p:
                for z in range(2):
                    pe.wait_ge(e["xn"][z], p + 1)
                    for c in range(KD):
                        ins = pe.transpose(tp[z][:, c], xn[:, z, c * P:(c + 1) * P], ident[:])
                    ins.then_inc(e["xt_mm"][z], 1)
                for z in range(2):
                    pe.wait_ge(e["xt_c"][z], p + 1)
                    pe.wait_ge(e["ab_done"][z], p)
                    for k in range(KD):
                        ins = pe.matmul(pab[z][:], xt[:, z, k], wab[:, k], start=k == 0, stop=k == KD - 1)
                    ins.then_inc(e["ab_mm"][z], 1)
                    for n in range(NC):
                        u = z * NC + n
                        if u < 4:
                            pe.wait_ge(m[f"pw_c{u % 4}"], p * PER)
                        else:
                            pe.wait_ge(m[f"pw_c{u % 4}"], p * PER + u // 4)
                        for k in range(KD):
                            ins = pe.matmul(pw[u % 4][:], xt[:, z, k], w[:, k, n * 512:(n + 1) * 512], start=k == 0, stop=k == KD - 1)
                        ins.then_inc(m["pw_done"], 1)




def stage_gdn_core(nc, d):
    HG = 4
    NG = GH // HG
    LV = 6
    C = P
    USES = 22
    (A_T, GAMMA, ABC0, ABC1, KQ, _1, _2, _3, GK, _5, _6, _7, KS0, KS1, QS0, QS1, W0, W1, O0, O1, DS0, DS1) = range(USES)
    with ExitStack() as ctx:
        r = Room(nc, ctx, "core")
        ident = r.sb("ident", [P, P])
        i4 = r.sb("i4", [P, HG, C])
        lvl = r.sb("lvl", [P, LV, C])
        m0t = r.sb("m0t", [P, C])
        amask, eye8, ones8 = r.sb("amask", [GH, GH, C]), r.sb("eye8", [GH, GH]), r.sb("ones8", [GH, P])
        alog, dtb = r.sb("alog", [P, GH]), r.sb("dtb", [P, GH])
        ab = r.sb("ab", [P, TILES, 2 * GH])
        al_all, be_all = r.sb("al_all", [P, TILES, GH]), r.sb("be_all", [P, TILES, GH])
        t1, t2, t3 = [r.sb(f"t{n}", [P, TILES, GH]) for n in range(3)]
        rows = r.sb("rows", [P, 2, 3, GH, DK])
        al, be = r.sb("al", [P, 2, GH]), r.sb("be", [P, 2, GH])
        at_, gt, gx = r.sb("aT", [GH, C]), r.sb("gT", [GH, C]), r.sb("gX", [GH, GH])
        ax = r.sb("aX", [GH, GH, C])
        zero8 = r.sb("zero8", [GH, C])
        ga, ng, gc = r.sb("ga", [P, GH]), r.sb("ng", [P, GH]), r.sb("gc", [P, GH])
        dt = r.sb("DT", [P, GH, C])
        db = r.sb("DB", [P, GH, C])
        kp = r.sb("KP", [P, GH, DK])
        kqt = r.sb("KQT", [P, GH, 2, C])
        att = r.sb("At", [P, GH, C])
        attn = r.sb("attn", [P, GH, C])
        bt = r.sb("Bt", [P, GH, C])
        tm, um, xm = r.sb("Tm", [P, GH, C]), r.sb("Um", [P, GH, C]), r.sb("Xm", [P, GH, C])
        rr, dl, o1 = r.sb("R", [P, GH, DK]), r.sb("delta", [P, GH, DK]), r.sb("o1", [P, GH, DK])
        st = r.sb("S", [P, GH, DK])
        o = r.sb("o", [P, 2, GH, DK])
        mb = [r.ps(f"m{n}", [P, HG, C]) for n in range(2)]
        px, pt, pu = [[r.ps(f"p{a}{g}", [P, HG, C]) for g in range(NG)] for a in "xtu"]
        m = {n: r.sem(n) for n in ("w_in ab_in prep consts chain ab_done a_c g_done ax_done g_c dt_done db_done kq_c at_done kp_done "
                                   "r_done o1_c delta_c s_zero s_done full0 full1 free0 free1").split()}
        e = {n: [r.sem(f"{n}{g}") for g in range(2)] for n in "in rows_free o_done out bt u1 x_mm x_c t_mm t_c u_mm u_c".split()}
        block = ctx.enter_context(nc.Block())
        gs = lambda g: slice(g * HG, (g + 1) * HG)
        bc = lambda v, n, w: v.rearrange("p (h o) -> p h o", o=1).to_broadcast([P, n, w])
        lv4 = lambda v: v.rearrange("p (o n) -> p o n", o=1).to_broadcast([P, HG, C])

        def wait_full(eng, i, k):
            eng.wait_ge(m[f"full{k % 2}"], i * (USES // 2) + k // 2 + 1)

        def wait_free(eng, i, k):
            eng.wait_ge(m[f"free{k % 2}"], i * (USES // 2) + k // 2 + 1)

        def chunks(eng, before=None):
            with eng.Fori(0, B) as b:
                if before:
                    before(b)
                with eng.Fori(0, TPB // 2) as ih:
                    for z in range(2):
                        yield b, z, b * TPB + ih * 2 + z, b * (TPB // 2) + ih

        @block.sync
        def _(sp):
            for dst, src in ((ident[:], d["ident"]), (i4[:], d["eye4"]), (lvl[:], d["levels"]), (m0t[:], d["level0t"]),
                             (amask[:], d["alpha_mask"]), (eye8[:], d["eye8"]),
                             (alog[:], d["L1_attn_A_log"].partition_broadcast(P)), (dtb[:], d["L1_attn_dt_bias"].partition_broadcast(P)),
                             (ab[:], d["ab"].rearrange("(i p) c -> p i c", p=P))):
                sp.dma_start(dst, src).then_inc(m["w_in"], 16)
            for b, z, i, pair in chunks(sp):
                hold(sp, r.passed, e["rows_free"][z], pair + 1)
                sp.dma_start(rows[:, z].rearrange("p a h e -> p (a h e)"), d["qkv"][bass.ds(i * P, P), :]).then_inc(e["in"][z], 16)

        @block.gpsimd
        def _(pool):
            pool.memset(zero8[:], 0.0)
            pool.memset(ones8[:], 1.0).then_inc(m["consts"], 1)
            for b, z, i, pair in chunks(pool):
                for g in range(NG):
                    hold(pool, r.passed, m["dt_done"], i * NG + g + 1)
                    pool.tensor_tensor(db[:, gs(g)], dt[:, gs(g)], bc(be[:, z, gs(g)], HG, C), ALU.mult).then_inc(m["db_done"], 1)
                for g in range(NG):
                    hold(pool, r.passed, m["at_done"], i * 4 + 2 * g + 2)
                    pool.affine_select(out=bt[:, gs(g)], in_=att[:, gs(g)], compare_op=ALU.not_equal, fill=1.0, base=0,
                                       pattern=[[0, HG], [-1, C]], channel_multiplier=1).then_inc(e["bt"][g], 1)
                hold(pool, r.passed, e["in"][z], 16 * pair + 16)
                pool.tensor_tensor(kp[:], rows[:, z, 1], dt[:, :, C - 1:C].to_broadcast([P, GH, DK]), ALU.mult).then_inc(m["kp_done"], 1)

        @block.scalar
        def _(act):
            act.wait_ge(m["prep"], 1)
            act.activation(t1[:], ab[:, :, 0:GH], ACT.Abs).then_inc(m["prep"], 1)
            act.wait_ge(m["prep"], 2)
            act.activation(t2[:], t1[:], ACT.Exp, scale=-1.0).then_inc(m["prep"], 1)
            act.activation(be_all[:], ab[:, :, GH:], ACT.Exp, scale=-1.0)
            act.activation(alog[:], alog[:], ACT.Exp).then_inc(m["prep"], 1)
            act.wait_ge(m["prep"], PREP - 1)
            act.activation(al_all[:], t1[:], ACT.Exp, scale=-1.0).then_inc(m["prep"], 1)
            for b, z, i, pair in chunks(act):
                wait_full(act, i, A_T)
                act.activation(at_[:], mb[0][0:GH, 0], ACT.Copy).then_inc(m["a_c"], 1)
                act.wait_ge(m["a_c"], i + 1)
                act.sem_inc(m["free0"], 1)
                wait_full(act, i, GAMMA)
                act.activation(ga[:], mb[1][:, 0, 0:GH], ACT.Copy)
                act.activation(ng[:], mb[1][:, 0, 0:GH], ACT.Copy, scale=-1.0)
                act.activation(gc[:], mb[1][:, 0, GH:2 * GH], ACT.Copy).then_inc(m["g_c"], 1)
                act.wait_ge(m["g_c"], i + 1)
                act.sem_inc(m["free1"], 1)
                for k in range(4):
                    wait_full(act, i, KQ + k)
                    act.activation(kqt[:, 2 * k:2 * k + 2].rearrange("p h a t -> p (h a) t"), mb[k % 2][:], ACT.Copy).then_inc(m["kq_c"], 1)
                    act.wait_ge(m["kq_c"], i * 4 + k + 1)
                    act.sem_inc(m[f"free{k % 2}"], 1)
                for g in range(NG):
                    act.wait_ge(e["t_mm"][g], i * LV + 1)
                    act.activation(tm[:, gs(g)], pt[g][:], ACT.Copy).then_inc(e["t_c"][g], 1)
                for g in range(NG):
                    wait_full(act, i, QS0 + g)
                    for h in range(HG):
                        ins = act.activation(o1[:, g * HG + h], mb[g][:, h], ACT.Copy, scale=ga[:, g * HG + h:g * HG + h + 1])
                    ins.then_inc(m["o1_c"], 1)
                    act.wait_ge(m["o1_c"], i * NG + g + 1)
                    act.sem_inc(m[f"free{g}"], 1)
                for l in range(1, LV + 1):
                    for g in range(NG):
                        if l < LV:
                            act.wait_ge(e["t_mm"][g], i * LV + l + 1)
                            act.activation(tm[:, gs(g)], pt[g][:], ACT.Copy).then_inc(e["t_c"][g], 1)
                        act.wait_ge(e["u_mm"][g], i * LV + l)
                        act.activation(um[:, gs(g)], pu[g][:], ACT.Copy).then_inc(e["u_c"][g], 1)
                for g in range(NG):
                    wait_full(act, i, W0 + g)
                    for h in range(HG):
                        ins = act.activation(dl[:, g * HG + h], mb[g][:, h], ACT.Copy, scale=be[:, z, g * HG + h:g * HG + h + 1])
                    ins.then_inc(m["delta_c"], 1)
                    act.wait_ge(m["delta_c"], i * NG + g + 1)
                    act.sem_inc(m[f"free{g}"], 1)
                for g in range(NG):
                    act.wait_ge(e["o_done"][z], pair * NG + g + 1)
                act.dma_start(d["o"][bass.ds(i * P, P), :], o[:, z].rearrange("p h e -> p (h e)")).then_inc(e["out"][z], 16)
            for z in range(2):
                act.wait_ge(e["out"][z], 16 * TILES // 2)

        @block.vector
        def _(dve):
            link = Link(dve, m["prep"], 0)
            b8 = lambda v: v.rearrange("p (o h) -> p o h", o=1).to_broadcast([P, TILES, GH])
            dve.wait_ge(m["w_in"], 16 * 9)
            link(dve.tensor_tensor(ab[:, :, 0:GH], ab[:, :, 0:GH], b8(dtb[:]), ALU.add))
            link.n += 3
            dve.wait_ge(m["prep"], 4)
            link(dve.tensor_scalar(t1[:], t2[:], 2.0, None, ALU.add))
            link(dve.reciprocal(t1[:], t1[:]))
            link(dve.tensor_tensor(t2[:], t2[:], t1[:], ALU.mult))
            link(dve.tensor_tensor(t3[:], t2[:], t2[:], ALU.mult))
            link(dve.tensor_scalar(t1[:], t3[:], 1.0 / 19, None, ALU.mult))
            for odd in (17, 15, 13, 11, 9, 7, 5, 3):
                link(dve.scalar_tensor_tensor(t1[:], t1[:], 1.0 / odd, t3[:], ALU.add, ALU.mult))
            link(dve.scalar_tensor_tensor(t1[:], t1[:], 1.0, t2[:], ALU.add, ALU.mult))
            link(dve.tensor_scalar(t1[:], t1[:], 2.0, None, ALU.mult))
            link(dve.tensor_scalar(ab[:, :, 0:GH], ab[:, :, 0:GH], 0.0, None, ALU.max))
            link(dve.tensor_tensor(t1[:], t1[:], ab[:, :, 0:GH], ALU.add))
            link(dve.tensor_tensor(t1[:], t1[:], b8(alog[:]), ALU.mult))
            link(dve.tensor_scalar(be_all[:], be_all[:], 1.0, None, ALU.add))
            link(dve.reciprocal(be_all[:], be_all[:]))
            assert link.n == PREP - 1
            dve.wait_ge(m["prep"], PREP)
            dve.wait_ge(m["consts"], 1)
            for z in range(2):
                dve.sem_inc(e["rows_free"][z], 1)
                dve.sem_inc(m[f"free{z}"], 1)

            def clear_state(b):
                dve.memset(st[:], 0.0).then_inc(m["s_zero"], 1)

            for b, z, i, pair in chunks(dve, clear_state):
                link = Link(dve, m["chain"], CHAIN, i)
                dve.tensor_copy(al[:, z], al_all[:, bass.ds(i, 1)].rearrange("p o h -> p (o h)"))
                link(dve.tensor_copy(be[:, z], be_all[:, bass.ds(i, 1)].rearrange("p o h -> p (o h)")))
                dve.sem_inc(m["ab_done"], 1)
                dve.wait_ge(m["a_c"], i + 1)
                link(dve.tensor_tensor_scan(gt[:], at_[:], zero8[:], 1.0, ALU.mult, ALU.add))
                dve.tensor_scalar(gx[:], eye8[:], gt[:, C - 1:C], None, ALU.mult).then_inc(m["g_done"], 1)
                dve.tensor_tensor(ax[:], at_[:].rearrange("p (o t) -> p o t", o=1).to_broadcast([GH, GH, C]), amask[:], ALU.mult
                                  ).then_inc(m["ax_done"], 1)
                for g in range(NG):
                    wait_full(dve, i, ABC0 + g)
                    link(dve.tensor_tensor_scan(dt[:, gs(g)].rearrange("p h t -> p (h t)"), mb[g][:].rearrange("p h t -> p (h t)"),
                                                i4[:].rearrange("p h t -> p (h t)"), 0.0, ALU.mult, ALU.add))
                    dve.sem_inc(m["dt_done"], 1)
                    dve.sem_inc(m[f"free{g}"], 1)
                for k in range(4):
                    wait_full(dve, i, GK + k)
                    dve.wait_ge(m["db_done"], i * NG + k // 2 + 1)
                    v = mb[k % 2][:].rearrange("p (h a) t -> p h a t", a=2)
                    dve.tensor_tensor(att[:, 2 * k:2 * k + 2], v[:, :, 0], db[:, 2 * k:2 * k + 2], ALU.mult).then_inc(m["at_done"], 1)
                    link(dve.tensor_tensor(attn[:, 2 * k:2 * k + 2], v[:, :, 1], dt[:, 2 * k:2 * k + 2], ALU.mult))
                    dve.sem_inc(m[f"free{k % 2}"], 1)
                for g in range(NG):
                    link(dve.tensor_tensor(xm[:, gs(g)], att[:, gs(g)], lv4(m0t[:]), ALU.mult))
                    dve.tensor_tensor(um[:, gs(g)], xm[:, gs(g)], i4[:], ALU.add).then_inc(e["u1"][g], 1)
                for g in range(NG):
                    wait_full(dve, i, KS0 + g)
                    for h in range(HG):
                        hh = g * HG + h
                        ins = dve.scalar_tensor_tensor(rr[:, hh], mb[g][:, h], ng[:, hh:hh + 1], rows[:, z, 2, hh], ALU.mult, ALU.add)
                    link(ins)
                    dve.sem_inc(m["r_done"], 1)
                    dve.sem_inc(m[f"free{g}"], 1)
                for l in range(1, LV + 1):
                    for g in range(NG):
                        dve.wait_ge(e["x_mm"][g], i * LV + l)
                        dve.tensor_tensor(xm[:, gs(g)], px[g][:], lv4(lvl[:, l - 1]), ALU.mult).then_inc(e["x_c"][g], 1)
                dve.wait_ge(e["out"][z], 16 * pair)
                for g in range(NG):
                    wait_full(dve, i, O0 + g)
                    dve.wait_ge(m["o1_c"], i * NG + g + 1)
                    link(dve.tensor_tensor(o[:, z, gs(g)], mb[g][:], o1[:, gs(g)], ALU.add))
                    dve.sem_inc(e["o_done"][z], 1)
                    dve.sem_inc(m[f"free{g}"], 1)
                for g in range(NG):
                    wait_full(dve, i, DS0 + g)
                    for h in range(HG):
                        hh = g * HG + h
                        ins = dve.scalar_tensor_tensor(st[:, hh], st[:, hh], gc[:, hh:hh + 1], mb[g][:, h], ALU.mult, ALU.add)
                    link(ins)
                    dve.sem_inc(m["s_done"], 1)
                    dve.sem_inc(m[f"free{g}"], 1)
                dve.sem_inc(e["rows_free"][z], 1)
                link.done()

        @block.tensor
        def _(pe):
            pe.wait_ge(m["w_in"], 16 * 9)
            pe.wait_ge(m["consts"], 1)

            def use(i, k):
                wait_free(pe, i, k)
                return mb[k % 2]

            def wrote(ins, k):
                ins.then_inc(m[f"full{k % 2}"], 1)

            for b, z, i, pair in chunks(pe):
                pe.wait_ge(m["ab_done"], i + 1)
                q = use(i, A_T)
                wrote(pe.transpose(q[0:GH, 0], al[:, z], ident[:]), A_T)
                q = use(i, GAMMA)
                hold(pe, r.passed, m["g_done"], i + 1)
                pe.transpose(q[:, 0, 0:GH], gt[:], ident[0:GH, 0:GH])
                wrote(pe.matmul(q[:, 0, GH:2 * GH], ones8[:], gx[:], start=True, stop=True), GAMMA)
                pe.wait_ge(m["ax_done"], i + 1)
                for g in range(NG):
                    q = use(i, ABC0 + g)
                    wrote(pe.matmul(q[:], ones8[:], ax[:, gs(g)], start=True, stop=True), ABC0 + g)
                pe.wait_ge(e["in"][z], 16 * pair + 16)
                for k in range(4):
                    q = use(i, KQ + k)
                    for h in range(2):
                        pe.transpose(q[:, 2 * h], rows[:, z, 1, 2 * k + h], ident[:])
                        ins = pe.transpose(q[:, 2 * h + 1], rows[:, z, 0, 2 * k + h], ident[:])
                    wrote(ins, KQ + k)
                for k in range(4):
                    pe.wait_ge(m["kq_c"], i * 4 + k + 1)
                    q = use(i, GK + k)
                    for h in range(2):
                        ins = pe.matmul(q[:, 2 * h:2 * h + 2], kqt[:, 2 * k + h, 0], kqt[:, 2 * k + h], start=True, stop=True)
                    wrote(ins, GK + k)
                pe.wait_ge(m["s_zero"], b + 1)
                pe.wait_ge(m["s_done"], i * NG)
                for a, first in ((0, KS0), (1, QS0)):
                    for g in range(NG):
                        q = use(i, first + g)
                        for h in range(HG):
                            ins = pe.matmul(q[:, h], kqt[:, g * HG + h, a], st[:, g * HG + h], start=True, stop=True)
                        wrote(ins, first + g)
                for g in range(NG):
                    pe.wait_ge(e["u1"][g], i + 1)
                    for h in range(HG):
                        ins = pe.transpose(pt[g][:, h], um[:, g * HG + h], ident[:])
                    ins.then_inc(e["t_mm"][g], 1)
                for l in range(1, LV + 1):
                    for g in range(NG):
                        if l == 1:
                            pe.wait_ge(e["bt"][g], i + 1)
                        pe.wait_ge(e["t_c"][g], i * LV + l)
                        for h in range(HG):
                            hh = g * HG + h
                            ins = pe.matmul(px[g][:, h], bt[:, hh], tm[:, hh], start=True, stop=True)
                        ins.then_inc(e["x_mm"][g], 1)
                    for g in range(NG):
                        pe.wait_ge(e["x_c"][g], i * LV + l)
                        if l > 1:
                            pe.wait_ge(e["u_c"][g], i * LV + l - 1)
                        if l < LV:
                            for h in range(HG):
                                hh = g * HG + h
                                ins = pe.matmul(pt[g][:, h], um[:, hh], xm[:, hh], start=True, stop=True)
                            ins.then_inc(e["t_mm"][g], 1)
                        for h in range(HG):
                            hh = g * HG + h
                            ins = pe.matmul(pu[g][:, h], xm[:, hh], um[:, hh], start=True, stop=True)
                        ins.then_inc(e["u_mm"][g], 1)
                for g in range(NG):
                    pe.wait_ge(e["u_c"][g], i * LV + LV)
                    pe.wait_ge(m["r_done"], i * NG + g + 1)
                    q = use(i, W0 + g)
                    for h in range(HG):
                        hh = g * HG + h
                        ins = pe.matmul(q[:, h], um[:, hh], rr[:, hh], start=True, stop=True)
                    wrote(ins, W0 + g)
                pe.wait_ge(m["kp_done"], i + 1)
                for left, first in ((attn, O0), (kp, DS0)):
                    for g in range(NG):
                        pe.wait_ge(m["delta_c"], i * NG + g + 1)
                        q = use(i, first + g)
                        for h in range(HG):
                            hh = g * HG + h
                            ins = pe.matmul(q[:, h], left[:, hh], dl[:, hh], start=True, stop=True)
                        wrote(ins, first + g)


PREP = 25
CHAIN = 2 + 2 + 4 + 2 + 2 + 2 + 2


def stage_gdn_out(nc, d):
    FF = 1024
    KF = FF // P
    PAIRS = TILES // 2
    with ExitStack() as ctx:
        r = Room(nc, ctx, "gout")
        ident = r.sb("ident", [P, P])
        wg, wfc = r.sb("wg", [P, KD, GD]), r.sb("wfc", [P, KD, FF])
        wo, wp = r.sb("wo", [P, GD // P, D]), r.sb("wp", [P, KF, D])
        onw = r.sb("onw", [P, DK])
        x, o = r.sb("x", [P, 2, D]), r.sb("o", [P, 2, GD])
        st, mv = r.sb("st", [P, 2, 6]), r.sb("mv", [P, 2, 2])
        va, rstd = r.sb("va", [P, 2, 3]), r.sb("rstd", [P, 2, 3])
        half = r.sb("half", [P, GH])
        ssq, junk = r.sb("ssq", [P, 2, 2]), r.sb("junk", [P, 2, D])
        xin, xn, xt = r.sb("xin", [P, 2, D]), r.sb("xn", [P, 2, D]), r.sb("xt", [P, 2, D])
        sq = r.sb("sq", [P, 2, GD])
        no, ro = r.sb("no", [P, 2, GH]), r.sb("ro", [P, 2, GH])
        gate = r.sb("gate", [P, 2, GD])
        big = r.sb("big", [P, 2, 8, P])
        x5 = r.sb("xm", [P, 2, D])
        mn, mt = r.sb("mn", [P, 2, D]), r.sb("mt", [P, 2, D])
        y = r.sb("y", [P, 2, D])
        ps = [r.ps(f"ps{z}", [P, 2, 512]) for z in range(2)]
        tp = [r.ps(f"tp{z}", [P, 2, D]) for z in range(2)]
        m = {n: r.sem(n) for n in "w_in consts chain".split()}
        steps = ("in rows_free va rstd sq1 sq1_c va2 rstd2 xn xt_mm xt_c g_mm g_c osq no ro on gated ot_mm ot_c wo_mm xm sq2 va3 rstd3 "
                 "mn mt_mm mt_c f_mm f_c f_sq ft_mm ft_c p_mm y_done out")
        e = {n: [r.sem(f"{n}{z}") for z in range(2)] for n in steps.split()}
        block = ctx.enter_context(nc.Block())

        @block.sync
        def _(sp):
            for dst, src in ((ident[:], d["ident"]), (wg[:], rows_in(d["L1_attn_Wg"])), (wfc[:], rows_in(d["L1_attn_W_fc"])),
                             (wo[:], rows_in(d["L1_attn_Wo"])), (wp[:], rows_in(d["L1_attn_W_proj"])),
                             (onw[:], d["L1_attn_o_norm_w"].partition_broadcast(P))):
                sp.dma_start(dst, src).then_inc(m["w_in"], 16)
            with sp.Fori(0, PAIRS) as p:
                for z in range(2):
                    hold(sp, r.passed, e["rows_free"][z], p + 1)
                    sp.dma_start(x[:, z], d["x3"][bass.ds((p * 2 + z) * P, P), :]).then_inc(e["in"][z], 16)
                    sp.dma_start(o[:, z], d["o"][bass.ds((p * 2 + z) * P, P), :]).then_inc(e["in"][z], 16)
                for z in range(2):
                    hold(sp, r.passed, e["y_done"][z], p + 1)
                    sp.dma_start(d["x4"][bass.ds((p * 2 + z) * P, P), :], y[:, z]).then_inc(e["out"][z], 16)
            for z in range(2):
                sp.wait_ge(e["out"][z], 16 * PAIRS)

        @block.gpsimd
        def _(pool):
            pool.memset(half[:], -0.5).then_inc(m["consts"], 1)
            pool.wait_ge(m["consts"], 1)
            with pool.Fori(0, PAIRS) as p:
                for a, b, k in (("va", "rstd", 0), ("va2", "rstd2", 1), ("no", "ro", None), ("va3", "rstd3", 2)):
                    for z in range(2):
                        pool.wait_ge(e[a][z], p + 1)
                        if k is None:
                            pool.tensor_tensor(ro[:, z], no[:, z], half[:], ALU.pow).then_inc(e[b][z], 1)
                        else:
                            pool.tensor_tensor(rstd[:, z, k:k + 1], va[:, z, k:k + 1], half[:, 0:1], ALU.pow).then_inc(e[b][z], 1)

        @block.vector
        def _(dve):
            for z in range(2):
                dve.sem_inc(e["rows_free"][z], 1)
            with dve.Fori(0, PAIRS) as p:
                link = Link(dve, m["chain"], 2 * 8, p)
                for z in range(2):
                    dve.wait_ge(e["in"][z], 32 * p + 32)
                    link.alone(dve.bn_stats(st[:, z], x[:, z]), r.passed)
                    link(dve.bn_aggr(mv[:, z], st[:, z]))
                    dve.tensor_scalar(va[:, z, 0:1], mv[:, z, 1:2], 1e-5, None, ALU.add).then_inc(e["va"][z], 1)
                for z in range(2):
                    dve.wait_ge(e["rstd"][z], p + 1)
                    dve.tensor_scalar(xin[:, z], x[:, z], mv[:, z, 0:1], rstd[:, z, 0:1], ALU.subtract, ALU.mult).then_inc(e["sq1"][z], 1)
                for z in range(2):
                    dve.wait_ge(e["sq1_c"][z], p + 1)
                    dve.tensor_scalar(va[:, z, 1:2], ssq[:, z, 0:1], 1.0 / D, 1e-6, ALU.mult, ALU.add).then_inc(e["va2"][z], 1)
                for z in range(2):
                    dve.wait_ge(e["rstd2"][z], p + 1)
                    dve.tensor_scalar(xn[:, z], xin[:, z], rstd[:, z, 1:2], None, ALU.mult).then_inc(e["xn"][z], 1)
                for z in range(2):
                    dve.wait_ge(e["osq"][z], p + 1)
                    link(dve.reduce_sum(no[:, z], sq[:, z].rearrange("p (h e) -> p h e", e=DK), AX.X))
                    dve.tensor_scalar(no[:, z], no[:, z], 1.0 / DK, 1e-6, ALU.mult, ALU.add).then_inc(e["no"][z], 1)
                for z in range(2):
                    dve.wait_ge(e["ro"][z], p + 1)
                    for h in range(GH):
                        v = o[:, z, h * DK:(h + 1) * DK]
                        ins = dve.scalar_tensor_tensor(v, v, ro[:, z, h:h + 1], onw[:], ALU.mult, ALU.mult)
                    link(ins)
                    dve.wait_ge(e["g_c"][z], p + 1)
                    dve.tensor_tensor(o[:, z], o[:, z], gate[:, z], ALU.mult).then_inc(e["gated"][z], 1)
                for z in range(2):
                    dve.wait_ge(e["wo_mm"][z], p + 1)
                    dve.tensor_tensor(x5[:, z], xin[:, z], tp[z][:, 1], ALU.add).then_inc(e["xm"][z], 1)
                for z in range(2):
                    dve.wait_ge(e["sq2"][z], p + 1)
                    dve.tensor_scalar(va[:, z, 2:3], ssq[:, z, 1:2], 1.0 / D, 1e-6, ALU.mult, ALU.add).then_inc(e["va3"][z], 1)
                for z in range(2):
                    dve.wait_ge(e["rstd3"][z], p + 1)
                    dve.tensor_scalar(mn[:, z], x5[:, z], rstd[:, z, 2:3], None, ALU.mult).then_inc(e["mn"][z], 1)
                for z in range(2):
                    dve.wait_ge(e["out"][z], 16 * p)
                    link(dve.tensor_tensor(y[:, z], x[:, z], x5[:, z], ALU.add))
                    dve.wait_ge(e["f_c"][z], p + 1)
                    link(dve.tensor_tensor(gate[:, z], gate[:, z], gate[:, z], ALU.mult))
                    dve.sem_inc(e["f_sq"][z], 1)
                    dve.sem_inc(e["rows_free"][z], 1)
                for z in range(2):
                    dve.wait_ge(e["p_mm"][z], p + 1)
                    link(dve.tensor_tensor(y[:, z], y[:, z], tp[z][:, 1], ALU.add))
                    link(dve.memset(ssq[:, z], 0.0))
                    dve.sem_inc(e["y_done"][z], 1)
                link.done()

        @block.scalar
        def _(act):
            act.wait_ge(m["w_in"], 96)
            with act.Fori(0, PAIRS) as p:
                for z in range(2):
                    act.wait_ge(e["in"][z], 32 * p + 32)
                    act.activation(sq[:, z], o[:, z], ACT.Square).then_inc(e["osq"][z], 1)
                for z in range(2):
                    act.wait_ge(e["sq1"][z], p + 1)
                    act.activation(junk[:, z], xin[:, z], ACT.Square, accum_out=ssq[:, z, 0:1]).then_inc(e["sq1_c"][z], 1)
                for z in range(2):
                    act.wait_ge(e["xt_mm"][z], p + 1)
                    act.activation(xt[:, z], tp[z][:, 0], ACT.Copy).then_inc(e["xt_c"][z], 1)
                for z in range(2):
                    act.wait_ge(e["g_mm"][z], p + 1)
                    act.activation(gate[:, z].rearrange("p (a n) -> p a n", a=2), ps[z][:], ACT.Silu).then_inc(e["g_c"][z], 1)
                for z in range(2):
                    act.wait_ge(e["ot_mm"][z], p + 1)
                    act.activation(big[:, z].rearrange("p (a h) n -> p a (h n)", a=2), ps[z][:], ACT.Copy).then_inc(e["ot_c"][z], 1)
                for z in range(2):
                    act.wait_ge(e["xm"][z], p + 1)
                    act.activation(junk[:, z], x5[:, z], ACT.Square, accum_out=ssq[:, z, 1:2]).then_inc(e["sq2"][z], 1)
                for z in range(2):
                    act.wait_ge(e["mt_mm"][z], p + 1)
                    act.activation(mt[:, z], tp[z][:, 0], ACT.Copy).then_inc(e["mt_c"][z], 1)
                for z in range(2):
                    act.wait_ge(e["f_mm"][z], p + 1)
                    act.activation(gate[:, z].rearrange("p (a n) -> p a n", a=2), ps[z][:], ACT.Relu).then_inc(e["f_c"][z], 1)
                for z in range(2):
                    act.wait_ge(e["ft_mm"][z], p + 1)
                    act.activation(big[:, z].rearrange("p (a h) n -> p a (h n)", a=2), ps[z][:], ACT.Copy).then_inc(e["ft_c"][z], 1)

        @block.tensor
        def _(pe):
            pe.wait_ge(m["w_in"], 96)

            def transposes(dst, src, n):
                for c in range(n):
                    ins = pe.transpose(dst[:, c], src[:, c * P:(c + 1) * P], ident[:])
                return ins

            def product(dst, left, w, n):
                chunks = w.shape[1]
                for k in range(chunks):
                    ins = pe.matmul(dst, left[:, k * P:(k + 1) * P], w[:, k, n[0]:n[1]],
                                    start=k == 0, stop=k == chunks - 1)
                return ins

            split = lambda v: v.rearrange("p (c n) -> p c n", n=P)
            with pe.Fori(0, PAIRS) as p:
                for z in range(2):
                    pe.wait_ge(e["xn"][z], p + 1)
                    pe.wait_ge(e["y_done"][z], p)
                    transposes(split(tp[z][:, 0]), xn[:, z], KD).then_inc(e["xt_mm"][z], 1)
                for z in range(2):
                    pe.wait_ge(e["xt_c"][z], p + 1)
                    for a in range(2):
                        ins = product(ps[z][:, a], xt[:, z], wg, (a * 512, a * 512 + 512))
                    ins.then_inc(e["g_mm"][z], 1)
                for z in range(2):
                    pe.wait_ge(e["gated"][z], p + 1)
                    transposes(ps[z][:].rearrange("p a (h n) -> p (a h) n", n=P), o[:, z], GH).then_inc(e["ot_mm"][z], 1)
                for z in range(2):
                    pe.wait_ge(e["ot_c"][z], p + 1)
                    product(tp[z][:, 1], big[:, z].rearrange("p h n -> p (h n)"), wo, (0, D)).then_inc(e["wo_mm"][z], 1)
                for z in range(2):
                    pe.wait_ge(e["mn"][z], p + 1)
                    transposes(split(tp[z][:, 0]), mn[:, z], KD).then_inc(e["mt_mm"][z], 1)
                for z in range(2):
                    pe.wait_ge(e["mt_c"][z], p + 1)
                    for a in range(2):
                        ins = product(ps[z][:, a], mt[:, z], wfc, (a * 512, a * 512 + 512))
                    ins.then_inc(e["f_mm"][z], 1)
                for z in range(2):
                    pe.wait_ge(e["f_sq"][z], p + 1)
                    transposes(ps[z][:].rearrange("p a (h n) -> p (a h) n", n=P), gate[:, z], KF).then_inc(e["ft_mm"][z], 1)
                for z in range(2):
                    pe.wait_ge(e["ft_c"][z], p + 1)
                    product(tp[z][:, 1], big[:, z].rearrange("p h n -> p (h n)"), wp, (0, D)).then_inc(e["p_mm"][z], 1)


def stage_lin(nc, d):
    SK = 77
    PAIRS = TILES // 2
    NKV = D + NH
    STEPS = 14
    with ExitStack() as ctx:
        r = Room(nc, ctx, "lin")
        ident = r.sb("ident", [P, P])
        wq, wk, wv = [r.sb(n, [P, KD, D]) for n in ("wq", "wk", "wv")]
        lg, lb = r.sb("lg", [P, D]), r.sb("lb", [P, D])
        same = r.sb("same", [P, KD, NKV])
        cx, cxt, em = r.sb("cx", [SK, D]), r.sb("cxt", [P, KD, SK]), r.sb("em", [SK, 1])
        cst, cmv, cva, crs = [r.sb(n, s) for n, s in (("cst", [SK, 2, 6]), ("cmv", [SK, 2, 2]), ("cva", [SK, 2]), ("crs", [SK, 2]))]
        kv = r.sb("kv", [SK, 2, D])
        ones = r.sb("ones", [SK, 1])
        kvb = r.sb("kvb", [P, KD, NKV])
        half = r.sb("half", [P, 2])
        x = r.sb("x", [P, 2, D])
        st, mv = r.sb("st", [P, 2, 2, 6]), r.sb("mv", [P, 2, 2, 2])
        va, rs = r.sb("va", [P, 2, 2]), r.sb("rs", [P, 2, 2])
        xn, xt, q, qt = [r.sb(n, [P, 2, D]) for n in ("xn", "xt", "q", "qt")]
        den = r.sb("den", [P, 2, NH])
        att = r.sb("att", [P, 2, D])
        tp, mm = [[r.ps(f"{a}{z}", [P, 512]) for z in range(2)] for a in ("tp", "mm")]
        m = {n: r.sem(n) for n in "w_in consts chain cx_in cx_free cx".split()}
        steps = "in x_free va rstd xn xt_mm xt_c q_mm va2 rstd2 q_done qt_mm qt_c a_mm att_done out"
        e = {n: [r.sem(f"{n}{z}") for z in range(2)] for n in steps.split()}
        block = ctx.enter_context(nc.Block())
        split = lambda v: v.rearrange("p (c n) -> p c n", n=P)

        def pairs(eng, before):
            with eng.Fori(0, B) as b:
                before(b)
                with eng.Fori(0, TPB // 2) as ih:
                    yield b, ih, b * (TPB // 2) + ih

        @block.sync
        def _(sp):
            for dst, src in (
                (ident[:], d["ident"]), (wq[:], rows_in(d["L1_xattn_wq"])), (wk[:], rows_in(d["L1_xattn_wk"])),
                (wv[:], rows_in(d["L1_xattn_wv"])), (same[:], d["same_head"]),
                (lg[:], d["L1_xattn_ln_gamma"].partition_broadcast(P)), (lb[:], d["L1_xattn_ln_beta"].partition_broadcast(P)),
            ):
                sp.dma_start(dst, src).then_inc(m["w_in"], 16)

            def context(b):
                hold(sp, r.passed, m["cx"], b * STEPS)
                sp.dma_start(cx[:], d["ctx"][bass.ds(b * SK, SK), :]).then_inc(m["cx_in"], 16)
                sp.dma_start(em[:], d["mask_ff"][bass.ds(b * SK, SK), :]).then_inc(m["cx_in"], 16)

            for b, ih, p in pairs(sp, context):
                for z in range(2):
                    hold(sp, r.passed, e["x_free"][z], p + 1)
                    sp.dma_start(x[:, z], d["x4"][bass.ds((p * 2 + z) * P, P), :]).then_inc(e["in"][z], 16)
                for z in range(2):
                    hold(sp, r.passed, e["att_done"][z], p + 1)
                    sp.dma_start(d["latt"][bass.ds(b * NH, NH), bass.ds(ih * 2 * P + z * P, P), :].rearrange("h n e -> n h e"),
                                 att[:, z].rearrange("p (h e) -> p h e", e=HD)).then_inc(e["out"][z], 16)
            for z in range(2):
                sp.wait_ge(e["out"][z], 16 * PAIRS)

        @block.gpsimd
        def _(pool):
            pool.memset(ones[:], 1.0)
            pool.memset(half[:], -0.5).then_inc(m["consts"], 1)
            pool.wait_ge(m["consts"], 1)

            def context(b):
                pool.wait_ge(m["cx"], b * STEPS + 6)
                pool.tensor_tensor(crs[:], cva[:], half[0:SK], ALU.pow).then_inc(m["cx"], 1)

            for b, ih, p in pairs(pool, context):
                for k, (signal, done) in enumerate((("va", "rstd"), ("va2", "rstd2"))):
                    for z in range(2):
                        pool.wait_ge(e[signal][z], p + 1)
                        pool.tensor_tensor(rs[:, z, k:k + 1], va[:, z, k:k + 1], half[:, 0:1], ALU.pow).then_inc(e[done][z], 1)

        @block.vector
        def _(dve):
            dve.wait_ge(m["w_in"], 16 * 7)
            for z in range(2):
                dve.sem_inc(e["x_free"][z], 1)

            def context(b):
                step = lambda ins: ins.then_inc(m["cx"], 1)
                at_step = lambda k: hold(dve, r.passed, m["cx"], b * STEPS + k)
                two = lambda v: v.rearrange("k (o c) -> k o c", o=1).to_broadcast([SK, 2, D])
                at_step(3)
                for a in range(2):
                    ins = dve.bn_stats(cst[:, a], mm[a][0:SK, 0:D])
                step(ins)
                at_step(4)
                for a in range(2):
                    ins = dve.bn_aggr(cmv[:, a], cst[:, a])
                step(ins)
                at_step(5)
                step(dve.tensor_scalar(cva[:], cmv[:, :, 1], 1e-6, None, ALU.add))
                at_step(7)
                for a in range(2):
                    ins = dve.tensor_scalar(kv[:, a], mm[a][0:SK, 0:D], cmv[:, a, 0:1], crs[:, a:a + 1], ALU.subtract, ALU.mult)
                step(ins)
                at_step(8)
                step(dve.tensor_tensor(kv[:], kv[:], two(lg[0:SK]), ALU.mult))
                at_step(9)
                step(dve.tensor_tensor(kv[:], kv[:], two(lb[0:SK]), ALU.add))
                at_step(10)
                step(dve.tensor_scalar(kv[:, 0], kv[:, 0], 0.0, 1e-6, ALU.max, ALU.add))
                dve.wait_ge(m["cx_in"], 32 * b + 32)
                at_step(11)
                step(dve.tensor_scalar(kv[:], kv[:], em[:], None, ALU.mult))
                at_step(13)
                for c in range(KD):
                    dve.tensor_tensor(kvb[:, c, 0:D], tp[c][:, 0:D], same[:, c, 0:D], ALU.mult)
                    ins = dve.tensor_tensor(kvb[:, c, D:], tp[c][:, D:D + 1].to_broadcast([P, NH]), same[:, c, D:], ALU.mult)
                step(ins)

            def scaled(link, v):
                link(dve.tensor_tensor(v, v, lg[:], ALU.mult))
                link(dve.tensor_tensor(v, v, lb[:], ALU.add))

            for b, ih, p in pairs(dve, context):
                link = Link(dve, m["chain"], 2 * (2 + 2 + 3 + 2), p)

                def stats(v, z, k, eps, signal):
                    link.alone(dve.bn_stats(st[:, z, k], v), r.passed)
                    link(dve.bn_aggr(mv[:, z, k], st[:, z, k]))
                    dve.tensor_scalar(va[:, z, k:k + 1], mv[:, z, k, 1:2], eps, None, ALU.add).then_inc(e[signal][z], 1)

                for z in range(2):
                    dve.wait_ge(e["in"][z], 16 * p + 16)
                    stats(x[:, z], z, 0, 1e-5, "va")
                for z in range(2):
                    dve.wait_ge(e["rstd"][z], p + 1)
                    dve.tensor_scalar(xn[:, z], x[:, z], mv[:, z, 0, 0:1], rs[:, z, 0:1], ALU.subtract, ALU.mult).then_inc(e["xn"][z], 1)
                    dve.wait_ge(e["xn"][z], p + 1)
                    dve.sem_inc(e["x_free"][z], 1)
                for z in range(2):
                    hold(dve, r.passed, e["q_mm"][z], p + 1)
                    stats(mm[z][:, 0:D], z, 1, 1e-6, "va2")
                for z in range(2):
                    dve.wait_ge(e["rstd2"][z], p + 1)
                    link(dve.tensor_scalar(q[:, z], mm[z][:, 0:D], mv[:, z, 1, 0:1], rs[:, z, 1:2], ALU.subtract, ALU.mult))
                    scaled(link, q[:, z])
                    dve.tensor_scalar(q[:, z], q[:, z], 0.0, 1e-6, ALU.max, ALU.add).then_inc(e["q_done"][z], 1)
                for z in range(2):
                    dve.wait_ge(e["a_mm"][z], p + 1)
                    link(dve.tensor_scalar(den[:, z], mm[z][:, D:NKV], 1e-6, None, ALU.add))
                    link(dve.reciprocal(den[:, z], den[:, z]))
                    dve.wait_ge(e["out"][z], 16 * p)
                    dve.tensor_tensor(att[:, z].rearrange("p (h e) -> p h e", e=HD), mm[z][:, 0:D].rearrange("p (h e) -> p h e", e=HD),
                                      den[:, z].rearrange("p (h o) -> p h o", o=1).to_broadcast([P, NH, HD]), ALU.mult
                                      ).then_inc(e["att_done"][z], 1)
                link.done()

        @block.scalar
        def _(act):
            def context(b):
                act.wait_ge(m["cx"], b * STEPS + 1)
                act.activation(cxt[:], tp[0][:, 0:KD * SK].rearrange("p (c k) -> p c k", c=KD), ACT.Copy).then_inc(m["cx"], 1)

            for b, ih, p in pairs(act, context):
                for signal, done, dst in (("xt_mm", "xt_c", xt), ("qt_mm", "qt_c", qt)):
                    for z in range(2):
                        act.wait_ge(e[signal][z], p + 1)
                        act.activation(dst[:, z], tp[z][:, 0:D], ACT.Copy).then_inc(e[done][z], 1)

        @block.tensor
        def _(pe):
            pe.wait_ge(m["w_in"], 16 * 7)
            pe.wait_ge(m["consts"], 1)

            def context(b):
                step = lambda ins: ins.then_inc(m["cx"], 1)
                pe.wait_ge(m["cx_in"], 32 * b + 32)
                for z in range(2):
                    pe.wait_ge(e["att_done"][z], b * (TPB // 2))
                for c in range(KD):
                    ins = pe.transpose(tp[0][:, c * SK:(c + 1) * SK], cx[:, c * P:(c + 1) * P], ident[0:SK, 0:SK])
                step(ins)
                pe.wait_ge(m["cx"], b * STEPS + 2)
                for a, w in enumerate((wk, wv)):
                    for k in range(KD):
                        ins = pe.matmul(mm[a][0:SK, 0:D], cxt[:, k], w[:, k], start=k == 0, stop=k == KD - 1)
                step(ins)
                pe.wait_ge(m["cx"], b * STEPS + 12)
                for c in range(KD):
                    pe.matmul(tp[c][:, 0:D], kv[:, 0, c * P:(c + 1) * P], kv[:, 1], start=True, stop=True)
                    ins = pe.matmul(tp[c][:, D:D + 1], kv[:, 0, c * P:(c + 1) * P], ones[:], start=True, stop=True)
                step(ins)
                hold(pe, r.passed, m["cx"], b * STEPS + 14)

            def turn(p, signal, src, done):
                for z in range(2):
                    pe.wait_ge(e[signal][z], p + 1)
                    for c in range(KD):
                        ins = pe.transpose(tp[z][:, c * P:(c + 1) * P], src[:, z, c * P:(c + 1) * P], ident[:])
                    ins.then_inc(e[done][z], 1)

            def product(p, signal, left, w, n, done):
                for z in range(2):
                    pe.wait_ge(e[signal][z], p + 1)
                    for k in range(KD):
                        ins = pe.matmul(mm[z][:, 0:n], left[:, z, k * P:(k + 1) * P], w[:, k], start=k == 0, stop=k == KD - 1)
                    ins.then_inc(e[done][z], 1)

            for b, ih, p in pairs(pe, context):
                turn(p, "xn", xn, "xt_mm")
                product(p, "xt_c", xt, wq, D, "q_mm")
                turn(p, "q_done", q, "qt_mm")
                product(p, "qt_c", qt, kvb, NKV, "a_mm")


def stage_lin_out(nc, d):
    PAIRS = TILES // 2
    with ExitStack() as ctx:
        r = Room(nc, ctx, "linout")
        ident = r.sb("ident", [P, P])
        wd = r.sb("wd", [P, KD, D])
        lg, lb, bd = r.sb("lg", [P, D]), r.sb("lb", [P, D]), r.sb("bd", [P, D])
        half = r.sb("half", [P, 2])
        a, at, x, y, src = [r.sb(n, [P, 2, D]) for n in ("a", "at", "x", "y", "src")]
        st, mv = r.sb("st", [P, 2, 2, 6]), r.sb("mv", [P, 2, 2, 2])
        va, rs = r.sb("va", [P, 2, 2]), r.sb("rs", [P, 2, 2])
        tp, mm = [[r.ps(f"{n}{z}", [P, KD, P]) for z in range(2)] for n in ("tp", "mm")]
        m = {n: r.sem(n) for n in "w_in consts chain".split()}
        steps = "a_in x_in a_free x_free at_mm at_c d_mm va rstd y_done va2 rstd2 src_done out"
        e = {n: [r.sem(f"{n}{z}") for z in range(2)] for n in steps.split()}
        block = ctx.enter_context(nc.Block())

        @block.sync
        def _(sp):
            for dst, src_d in (
                (ident[:], d["ident"]), (wd[:], rows_in(d["L1_xattn_dense_w"])),
                (lg[:], d["L1_xattn_ln_gamma"].partition_broadcast(P)), (lb[:], d["L1_xattn_ln_beta"].partition_broadcast(P)),
                (bd[:], d["L1_xattn_dense_b"].partition_broadcast(P)),
            ):
                sp.dma_start(dst, src_d).then_inc(m["w_in"], 16)
            rows = d["latt"].rearrange("h (t m) e -> (h t) (m e)", m=NH)
            with sp.Fori(0, PAIRS) as p:
                for z in range(2):
                    hold(sp, r.passed, e["a_free"][z], p + 1)
                    sp.dma_start(a[:, z], rows[bass.ds((p * 2 + z) * P, P), :]).then_inc(e["a_in"][z], 16)
                    hold(sp, r.passed, e["x_free"][z], p + 1)
                    sp.dma_start(x[:, z], d["x4"][bass.ds((p * 2 + z) * P, P), :]).then_inc(e["x_in"][z], 16)
                for z in range(2):
                    hold(sp, r.passed, e["src_done"][z], p + 1)
                    sp.dma_start(d["x5"][bass.ds((p * 2 + z) * P, P), :], y[:, z]).then_inc(e["out"][z], 16)
                    sp.dma_start(d["src1"][bass.ds((p * 2 + z) * P, P), :], src[:, z]).then_inc(e["out"][z], 16)
            for z in range(2):
                sp.wait_ge(e["out"][z], 32 * PAIRS)

        @block.gpsimd
        def _(pool):
            pool.memset(half[:], -0.5).then_inc(m["consts"], 1)
            pool.wait_ge(m["consts"], 1)
            with pool.Fori(0, PAIRS) as p:
                for k, (signal, done) in enumerate((("va", "rstd"), ("va2", "rstd2"))):
                    for z in range(2):
                        pool.wait_ge(e[signal][z], p + 1)
                        pool.tensor_tensor(rs[:, z, k:k + 1], va[:, z, k:k + 1], half[:, 0:1], ALU.pow).then_inc(e[done][z], 1)

        @block.vector
        def _(dve):
            dve.wait_ge(m["w_in"], 16 * 5)
            for z in range(2):
                dve.sem_inc(e["x_free"][z], 1)
            with dve.Fori(0, PAIRS) as p:
                link = Link(dve, m["chain"], 2 * (3 + 4 + 2), p)

                def stats(v, z, k, eps, signal):
                    link.alone(dve.bn_stats(st[:, z, k], v), r.passed)
                    link(dve.bn_aggr(mv[:, z, k], st[:, z, k]))
                    dve.tensor_scalar(va[:, z, k:k + 1], mv[:, z, k, 1:2], eps, None, ALU.add).then_inc(e[signal][z], 1)

                for z in range(2):
                    dve.wait_ge(e["out"][z], 32 * p)
                    dve.wait_ge(e["d_mm"][z], p + 1)
                    link(dve.tensor_tensor(y[:, z], mm[z][:].rearrange("p c n -> p (c n)"), bd[:], ALU.add))
                    stats(y[:, z], z, 0, 1e-6, "va")
                for z in range(2):
                    dve.wait_ge(e["rstd"][z], p + 1)
                    link(dve.tensor_scalar(y[:, z], y[:, z], mv[:, z, 0, 0:1], rs[:, z, 0:1], ALU.subtract, ALU.mult))
                    link(dve.tensor_tensor(y[:, z], y[:, z], lg[:], ALU.mult))
                    link(dve.tensor_tensor(y[:, z], y[:, z], lb[:], ALU.add))
                    dve.wait_ge(e["x_in"][z], 16 * p + 16)
                    link(dve.tensor_tensor(y[:, z], y[:, z], x[:, z], ALU.add))
                    dve.sem_inc(e["x_free"][z], 1)
                    stats(y[:, z], z, 1, 1e-5, "va2")
                for z in range(2):
                    dve.wait_ge(e["rstd2"][z], p + 1)
                    dve.tensor_scalar(src[:, z], y[:, z], mv[:, z, 1, 0:1], rs[:, z, 1:2], ALU.subtract, ALU.mult).then_inc(e["src_done"][z], 1)
                link.done()

        @block.scalar
        def _(act):
            with act.Fori(0, PAIRS) as p:
                for z in range(2):
                    act.wait_ge(e["at_mm"][z], p + 1)
                    act.activation(at[:, z], tp[z][:].rearrange("p c n -> p (c n)"), ACT.Copy).then_inc(e["at_c"][z], 1)

        @block.tensor
        def _(pe):
            pe.wait_ge(m["w_in"], 16 * 5)
            for z in range(2):
                pe.sem_inc(e["a_free"][z], 1)
            with pe.Fori(0, PAIRS) as p:
                for z in range(2):
                    pe.wait_ge(e["a_in"][z], 16 * p + 16)
                    for c in range(KD):
                        ins = pe.transpose(tp[z][:, c], a[:, z, c * P:(c + 1) * P], ident[:])
                    ins.then_inc(e["at_mm"][z], 1)
                    pe.wait_ge(e["at_mm"][z], p + 1)
                    pe.sem_inc(e["a_free"][z], 1)
                for z in range(2):
                    pe.wait_ge(e["at_c"][z], p + 1)
                    pe.wait_ge(e["va"][z], p)
                    for k in range(KD):
                        ins = pe.matmul(mm[z][:].rearrange("p c n -> p (c n)"), at[:, z, k * P:(k + 1) * P], wd[:, k], start=k == 0, stop=k == KD - 1)
                    ins.then_inc(e["d_mm"][z], 1)


def stage_pre1(nc, d):
    G = 4
    W = G * P
    DC = D // 4
    HALVES = S // W
    GROUPS = B * HALVES
    with ExitStack() as ctx:
        r = Room(nc, ctx, "pre1")
        ident = r.sb("ident", [P, P])
        wq = [r.sb(f"wq{n}", [P, KD, D]) for n in range(2)]
        wc = r.sb("wc", [P, KD, 2 * DC])
        wk = [r.sb(f"wk{n}", [DC, D]) for n in range(2)]
        wv = r.sb("wv", [2 * DC, D])
        cos, sin = r.sb("cos", [P, S]), r.sb("sin", [P, S])
        x = r.sb("x", [P, G, D])
        xt = r.sb("xt", [P, KD, W])
        kvc = r.sb("kvc", [2 * DC, W])
        t1, t2, qf, qr = [r.sb(n, [P, 2, W]) for n in ("t1", "t2", "qf", "qr")]
        parts = r.sb("parts", [P, 2, 3, W], BF16)
        row = r.sb("row", [P, G, D])
        tp = [r.ps(f"tp{n}", [P, KD, P]) for n in range(2)]
        qk = [[r.ps(f"qk{n}_{a}", [P, W]) for a in range(2)] for n in range(2)]
        kvp = r.ps("kvp", [2 * DC, W])
        rowp = r.ps("rowp", [P, D])
        names = ("w_in x_in x_free tp_done xt_done kvc_mm kvc_done qk_done qk_free parts_done "
                 "row_mm row_done chain parts_out0 parts_out1 v_out")
        m = {n: r.sem(n) for n in names.split()}
        block = ctx.enter_context(nc.Block())

        def groups(eng):
            with eng.Fori(0, B) as b:
                for g in range(HALVES):
                    yield b, g, b * HALVES + g

        @block.sync
        def _(sp):
            for dst, src in (
                (ident[:], d["ident"]), (wq[0][:], rows_in(d["L1_ffn_Wq"])), (wq[1][:], rows_in(d["L1_ffn_Wq_swapped"])),
                (wc[:, :, 0:DC], rows_in(d["L1_ffn_Wk_c"])), (wc[:, :, DC:], rows_in(d["L1_ffn_Wv_c"])),
                (wk[0][:], d["L1_ffn_Wk"]), (wk[1][:], d["L1_ffn_Wk_swapped"]), (wv[DC:], d["L1_ffn_Wv"]),
                (cos[:], d["rope_cos"]), (sin[:], d["rope_sin"]),
            ):
                sp.dma_start(dst, src).then_inc(m["w_in"], 16)
            for b, g, i in groups(sp):
                hold(sp, r.passed, m["x_free"], i + 1)
                sp.dma_start(x[:], d["src1"][bass.ds(i * W, W), :].rearrange("(s p) c -> p s c", p=P)).then_inc(m["x_in"], 16)
                for n in range(4):
                    dst = d["q1"] if n < 2 else d["k1"]
                    c = n % 2
                    hold(sp, r.passed, m["parts_done"], i * 4 + n + 1)
                    sp.dma_start(dst[:, bass.ds(b * D + c * P, P), g * W:(g + 1) * W].rearrange("a p t -> p a t"),
                                 parts[:, n % 2]).then_inc(m[f"parts_out{n % 2}"], 16)
                hold(sp, r.passed, m["row_done"], i * G + G)
                for n in range(4):
                    sp.dma_start(d["v1"][bass.ds((b * 4 + n) * S + g * W, W), :].rearrange("(s p) c -> p s c", p=P),
                                 row[:, :, n * D // 4:(n + 1) * D // 4]).then_inc(m["v_out"], 16)
            sp.wait_ge(m["v_out"], 64 * GROUPS)
            for n in range(2):
                sp.wait_ge(m[f"parts_out{n}"], 32 * GROUPS)

        @block.vector
        def _(dve):
            dve.wait_ge(m["w_in"], 16 * 10)
            dve.sem_inc(m["x_free"], 1)
            dve.sem_inc(m["qk_free"], 2)
            for b, g, i in groups(dve):
                link = Link(dve, m["chain"], 4 * 7, i)
                at = slice(g * W, (g + 1) * W)
                for n in range(4):
                    h = n % 2
                    scale = HD ** -0.5 if n < 2 else 1.0
                    dve.wait_ge(m["qk_done"], i * 4 + n + 1)
                    dve.wait_ge(m[f"parts_out{h}"], i * 32 + 16 * (n // 2))
                    link(dve.scalar_tensor_tensor(t1[:, h], qk[h][0][:], scale, cos[:, at], ALU.mult, ALU.mult))
                    link(dve.scalar_tensor_tensor(t2[:, h], qk[h][1][:], scale, sin[:, at], ALU.mult, ALU.mult))
                    dve.sem_inc(m["qk_free"], 1)
                    link(dve.tensor_tensor(qf[:, h], t1[:, h], t2[:, h], ALU.add))
                    link(dve.tensor_copy(parts[:, h, 0], qf[:, h]))
                    link(dve.tensor_tensor(qr[:, h], qf[:, h], parts[:, h, 0], ALU.subtract))
                    link(dve.tensor_copy(parts[:, h, 1], qr[:, h]))
                    link(dve.tensor_tensor(parts[:, h, 2], qr[:, h], parts[:, h, 1], ALU.subtract))
                    dve.sem_inc(m["parts_done"], 1)
                link.done()

        @block.scalar
        def _(act):
            for b, g, i in groups(act):
                act.wait_ge(m["row_mm"], i * G)
                for s in range(G):
                    act.wait_ge(m["tp_done"], i * G + s + 1)
                    act.activation(xt[:, :, s * P:(s + 1) * P], tp[s % 2][:], ACT.Copy).then_inc(m["xt_done"], 1)
                act.wait_ge(m["kvc_mm"], i + 1)
                act.activation(kvc[:], kvp[:], ACT.Copy).then_inc(m["kvc_done"], 1)
                act.wait_ge(m["v_out"], 64 * i)
                for s in range(G):
                    act.wait_ge(m["row_mm"], i * G + s + 1)
                    act.activation(row[:, s], rowp[:], ACT.Copy).then_inc(m["row_done"], 1)

        @block.tensor
        def _(pe):
            pe.wait_ge(m["w_in"], 16 * 10)
            pe.sem_inc(m["xt_done"], 2)
            for b, g, i in groups(pe):
                pe.wait_ge(m["x_in"], 16 * i + 16)
                for s in range(G):
                    pe.wait_ge(m["xt_done"], i * G + s + 1)
                    for c in range(KD):
                        ins = pe.transpose(tp[s % 2][:, c], x[:, s, c * P:(c + 1) * P], ident[:])
                    ins.then_inc(m["tp_done"], 1)
                pe.wait_ge(m["tp_done"], i * G + G)
                pe.sem_inc(m["x_free"], 1)
                pe.wait_ge(m["xt_done"], i * G + G + 2)
                for k in range(KD):
                    ins = pe.matmul(kvp[:], wc[:, k], xt[:, k], start=k == 0, stop=k == KD - 1)
                ins.then_inc(m["kvc_mm"], 1)
                for n in range(4):
                    c = n % 2
                    pe.wait_ge(m["qk_free"], i * 4 + n + 1)
                    if n == 2:
                        pe.wait_ge(m["kvc_done"], i + 1)
                    for a in range(2):
                        if n < 2:
                            for k in range(KD):
                                ins = pe.matmul(qk[c][a][:], wq[a][:, k, c * P:(c + 1) * P], xt[:, k], start=k == 0, stop=k == KD - 1)
                        else:
                            ins = pe.matmul(qk[c][a][:], wk[a][:, c * P:(c + 1) * P], kvc[0:DC], start=True, stop=True)
                    ins.then_inc(m["qk_done"], 1)
                for s in range(G):
                    pe.wait_ge(m["row_done"], i * G + s)
                    pe.matmul(rowp[:], kvc[DC:, s * P:(s + 1) * P], wv[DC:], start=True, stop=True).then_inc(m["row_mm"], 1)


def stage_attn1(nc, d):
    NB = S // P
    GR = 4
    W = 512
    QT = W // P
    GC = GR * HD
    ROWS = SPLIT * HD
    STEPS = B * (NH // GR) * (S // W)
    BODY = 4
    BODIES = STEPS // BODY
    AHEAD = 4
    LAG = 2
    with ExitStack() as ctx:
        r = Room(nc, ctx, "attn1")
        ident = r.sb("ident", [P, P])
        kt = [r.sb(f"kt{n}", [ROWS + 3, GR, S], BF16) for n in range(2)]
        qt = [r.sb(f"qt{n}", [ROWS + 3, GR, W], BF16) for n in range(BODY)]
        vs = r.sb("vs", [P, NB, GC])
        v32 = [r.sb(f"v32_{n}", [P, NB, GR, 32]) for n in range(2)]
        mx = [r.sb(f"mx{n}", [P, GR, QT, 2]) for n in range(2)]
        nm = r.sb("nm", [P, GR * QT])
        nf, nr = r.sb("nf", [GR * QT, P]), r.sb("nr", [GR * QT, P])
        nt = r.sb("nt", [GR * QT, 3, P], BF16)
        pt = r.sb("pt", [P, 4, GR, W])
        os_ = r.sb("os", [P, W])
        rs = r.sb("rs", [P, QT, GR, 1])
        row = r.sb("row", [P, 2, QT, GC])
        mp = [r.ps(f"mp{n}", [P, W]) for n in range(2)]
        st = [r.ps(f"st{n}", [P, 2, W]) for n in range(2)]
        op = r.ps("op", [P, W])
        tb = r.ps("tb", [P, QT, P])
        names = ("id_in vs_in v_ready ones max_mm max_done nm_done nm_mm nt_done nt_out nm_in "
                 "st_mm exp_done pv_mm os_done ot_mm row_done chain schain out0 out1 k_in0 k_in1 q_in0 q_in1 q_in2 q_in3")
        m = {n: r.sem(n) for n in names.split()}
        block = ctx.enter_context(nc.Block())

        def bodies(eng):
            with eng.Fori(0, BODIES - 1) as v:
                yield v, False
            yield BODIES - 1, True

        def maxima(w, n, last):
            w, n = (w + 1, n + AHEAD) if n < NB - AHEAD else (w + 2, n + AHEAD - NB)
            return None if last and w >= BODY else (w, n)

        FIRST = [(0, n) for n in range(NB)] + [(1, n) for n in range(AHEAD)]

        def load_k(sp, v, w):
            u = v * 2 + w // 2
            n = w // 2 % 2
            for slot in range(SPLIT):
                sp.dma_start(kt[n][slot * HD:(slot + 1) * HD], d["k1"][K_PART[slot], bass.ds(u * GC, GC), :]
                             .rearrange("(h e) t -> e h t", e=HD)).then_inc(m[f"k_in{n}"], 16)

        def load_q(sp, v, w):
            u = v * 2 + w // 2
            for slot in range(SPLIT):
                sp.dma_start(qt[w % 4][slot * HD:(slot + 1) * HD], d["q1"][Q_PART[slot], bass.ds(u * GC, GC), (w % 2) * W:(w % 2 + 1) * W]
                             .rearrange("(h e) t -> e h t", e=HD)).then_inc(m[f"q_in{w % 4}"], 16)

        @block.sync
        def _(sp):
            def load_v(v, w):
                sp.dma_start(vs[:], d["v1"][bass.ds((v * 2 + w // 2) * S, S), :].rearrange("(n p) c -> p n c", p=P)).then_inc(m["vs_in"], 16)

            def negated_maxima(v, w):
                it = v * BODY + w
                hold(sp, r.passed, m["nt_done"], it + 1)
                sp.dma_start(d["mx1"][bass.ds(it * 3, 3)].rearrange("a s i -> s a i"), nt[:]).then_inc(m["nt_out"], 16)
                hold(sp, r.passed, m["nt_out"], it * 16 + 16)
                sp.dma_start(qt[w % 4][ROWS:ROWS + 3], d["mx1"][bass.ds(it * 3, 3)].rearrange("a (h t) i -> a h (t i)", h=GR)
                             ).then_inc(m["nm_in"], 16)

            def store(v, w):
                it = v * BODY + w
                hold(sp, r.passed, m["row_done"], it + 1)
                u = v * 2 + w // 2
                sp.dma_start(d["at1"][bass.ds(u * S + (w % 2) * W, W), :].rearrange("(t p) c -> p t c", p=P),
                             row[:, w % 2]).then_inc(m[f"out{w % 2}"], 16)

            sp.dma_start(ident[:], d["ident"]).then_inc(m["id_in"], 16)
            load_k(sp, 0, 0)
            for w in range(3):
                load_q(sp, 0, w)
            load_v(0, 0)
            negated_maxima(0, 0)
            for v, last in bodies(sp):
                for w in range(BODY):
                    hold(sp, r.passed, m["st_mm"], (v * BODY + w) * 2 * NB)
                    if w % 2 == 0 and not (last and w + 2 >= BODY):
                        load_k(sp, v, w + 2)
                    if not (last and w + 3 >= BODY):
                        load_q(sp, v, w + 3)
                    if w % 2 == 0 and not (last and w + 2 >= BODY):
                        hold(sp, r.passed, m["v_ready"], v * 2 + w // 2 + 1)
                        load_v(v, w + 2)
                    if w:
                        store(v, w - 1)
                    if not (last and w + 1 >= BODY):
                        negated_maxima(v, w + 1)
                store(v, BODY - 1)
            for z in range(2):
                sp.wait_ge(m[f"out{z}"], STEPS // 2 * 16)

        @block.gpsimd
        def _(pool):
            for n in range(2):
                pool.memset(v32[n][:, :, :, HD + 1:], 0.0)
                ins = pool.memset(v32[n][:, :, :, HD:HD + 1], 1.0)
            ins.then_inc(m["ones"], 1)

            def values(v, w):
                hold(pool, r.passed, m["vs_in"], (v * 2 + w // 2) * 16 + 16)
                pool.tensor_copy(v32[w // 2 % 2][:, :, :, 0:HD], vs[:].rearrange("p n (h e) -> p n h e", e=HD)).then_inc(m["v_ready"], 1)

            values(0, 0)
            for v, last in bodies(pool):
                for w in (0, 2):
                    if not (last and w + 2 >= BODY):
                        hold(pool, r.passed, m["pv_mm"], (v * BODY + w) * NB)
                        values(v, w + 2)

        @block.vector
        def _(dve):
            def row_maxima(v, w, n):
                for j in range(4 * n, 4 * n + 4):
                    dve.wait_ge(m["max_mm"], (v * BODY + w) * 4 * NB + j + 1)
                    dve.reduce_max(mx[w % 2][:].rearrange("p h t a -> p (h t a)")[:, j:j + 1], mp[j % 2][:], AX.X).then_inc(m["max_done"], 1)

            def negate(v, w):
                dve.wait_ge(m["max_done"], (v * BODY + w + 1) * 4 * NB)
                dve.tensor_reduce(nm[:].rearrange("p (h t) -> p h t", h=GR), mx[w % 2][:], AX.X, ALU.max, negate=True).then_inc(m["nm_done"], 1)

            def split(v, w):
                it = v * BODY + w
                link = Link(dve, m["schain"], 4, it)
                hold(dve, r.passed, m["nm_mm"], it + 1)
                link(dve.tensor_copy(nf[:], tb[0:GR * QT, 0]))
                dve.wait_ge(m["nt_out"], it * 16)
                link(dve.tensor_copy(nt[:, 0], nf[:]))
                link(dve.tensor_tensor(nr[:], nf[:], nt[:, 0], ALU.subtract))
                link(dve.tensor_copy(nt[:, 1], nr[:]))
                dve.tensor_tensor(nt[:, 2], nr[:], nt[:, 1], ALU.subtract).then_inc(m["nt_done"], 1)
                link.done()

            def normalise(v, w):
                it = v * BODY + w
                link = Link(dve, m["chain"], 1, it)
                dve.wait_ge(m["ot_mm"], it + 1)
                o = tb[:].rearrange("p t (h e) -> p t h e", e=32)
                link(dve.reciprocal(rs[:], o[:, :, :, HD:HD + 1]))
                dve.wait_ge(m[f"out{w % 2}"], (v * 2 + w // 2) * 16)
                dve.tensor_tensor(row[:, w % 2].rearrange("p t (h e) -> p t h e", e=HD), o[:, :, :, 0:HD],
                                  rs[:].to_broadcast([P, QT, GR, HD]), ALU.mult).then_inc(m["row_done"], 1)
                link.done()

            for n in range(2):
                ins = dve.memset(kt[n][ROWS:ROWS + 3], 1.0)
            ins.then_inc(m["ones"], 1)
            for w, n in FIRST:
                row_maxima(0, w, n)
                if (w, n) == (0, NB - 1):
                    negate(0, 0)
                    split(0, 0)
            for v, last in bodies(dve):
                for w in range(BODY):
                    for n in range(NB):
                        at = maxima(w, n, last)
                        if at:
                            row_maxima(v, *at)
                        if n == 3 and w:
                            normalise(v, w - 1)
                        if n == 3 and at:
                            negate(v, w + 1)
                        if n == 4 and not (last and w + 1 >= BODY):
                            split(v, w + 1)
                normalise(v, BODY - 1)

        @block.scalar
        def _(act):
            act.sem_inc(m["exp_done"], 2)

            def evacuate(v, w):
                it = v * BODY + w
                act.wait_ge(m["pv_mm"], it * NB + NB)
                act.wait_ge(m["ot_mm"], it)
                act.activation(os_[:], op[:], ACT.Copy).then_inc(m["os_done"], 1)

            for v, last in bodies(act):
                for x in range(BODY * NB):
                    slot = v * BODY * NB + x
                    for a in range(2):
                        act.wait_ge(m["st_mm"], slot * 2 + a + 1)
                        if a == 0:
                            if x >= 4:
                                act.wait_ge(m["pv_mm"], slot - 3)
                            else:
                                act.wait_ge(m["pv_mm"], v * BODY * NB)
                        act.activation(pt[:, x % 4, 2 * a:2 * a + 2], st[a][:], ACT.Exp).then_inc(m["exp_done"], 1)
                    if x % NB == 1 and x >= NB:
                        evacuate(v, x // NB - 1)
                evacuate(v, BODY - 1)

        @block.tensor
        def _(pe):
            def score_rows(v, w, j):
                if j == 0:
                    hold(pe, r.passed, m[f"q_in{w % 4}"], (v + w // 4) * 96 + 96)
                    hold(pe, r.passed, m[f"k_in{w // 2 % 2}"], (v + w // 4) * 96 + 96)
                for j in range(j, j + 2):
                    h, t, a = j // 8, j // 2 % 4, j % 2
                    if isinstance(v, int) and v == 0 and w == 0 and j < 2:
                        pass
                    else:
                        pe.wait_ge(m["max_done"], (v * BODY + w) * 4 * NB + j - 1)
                    pe.matmul(mp[a][:], qt[w % 4][0:ROWS, h, t * P:(t + 1) * P], kt[w // 2 % 2][0:ROWS, h, a * W:(a + 1) * W],
                              start=True, stop=True).then_inc(m["max_mm"], 1)

            def transpose_maxima(v, w):
                hold(pe, r.passed, m["nm_done"], v * BODY + w + 1)
                pe.transpose(tb[0:GR * QT, 0], nm[:], ident[:]).then_inc(m["nm_mm"], 1)

            def score_columns(v, w, n, a):
                pe.wait_ge(m["exp_done"], ((v * BODY + w) * NB + n) * 2 + a + 1)
                for h in (2 * a, 2 * a + 1):
                    ins = pe.matmul(st[a][:, h % 2], kt[w // 2 % 2][:, h, n * P:(n + 1) * P], qt[w % 4][:, h], start=True, stop=True)
                ins.then_inc(m["st_mm"], 1)

            def weigh(v, x):
                w, n = x // NB, x % NB
                slot = v * BODY * NB + x
                pe.wait_ge(m["exp_done"], slot * 2 + 4)
                if n == 0:
                    pe.wait_ge(m["os_done"], v * BODY + w)
                for h in range(GR):
                    ins = pe.matmul(op[32 * h:32 * h + 32], v32[w // 2 % 2][:, n, h], pt[:, x % 4, h], start=n == 0, stop=n == NB - 1)
                ins.then_inc(m["pv_mm"], 1)

            def transpose_sums(v, w):
                pe.wait_ge(m["os_done"], v * BODY + w + 1)
                for t in range(QT):
                    ins = pe.transpose(tb[:, t], os_[:, t * P:(t + 1) * P], ident[:])
                ins.then_inc(m["ot_mm"], 1)

            pe.wait_ge(m["id_in"], 16)
            pe.wait_ge(m["ones"], 2)
            for w, n in FIRST:
                for j in (4 * n, 4 * n + 2):
                    score_rows(0, w, j)
                if (w, n) == (0, NB - 1):
                    transpose_maxima(0, 0)
            for v, last in bodies(pe):
                for w in range(BODY):
                    for n in range(NB):
                        x = w * NB + n
                        at = maxima(w, n, last)
                        if n == 0:
                            hold(pe, r.passed, m["nm_in"], (v * BODY + w) * 16 + 16)
                            hold(pe, r.passed, m["v_ready"], v * 2 + w // 2 + 1)
                        for a in range(2):
                            score_columns(v, w, n, a)
                            if at:
                                score_rows(v, at[0], 4 * at[1] + 2 * a)
                            if a == 0 and x >= LAG:
                                weigh(v, x - LAG)
                        if n == 3 and w:
                            pe.wait_ge(m["nt_done"], v * BODY + w)
                            transpose_sums(v, w - 1)
                        if n == 4 and not (last and w + 1 >= BODY):
                            pe.wait_ge(m["row_done"], v * BODY + w)
                            transpose_maxima(v, w + 1)
                for x in range(BODY * NB - LAG, BODY * NB):
                    weigh(v, x)
                if last:
                    pe.wait_ge(m["row_done"], v * BODY + BODY - 1)
                else:
                    pe.wait_ge(m["nt_done"], v * BODY + BODY + 1)
                transpose_sums(v, BODY - 1)


def stage_moe(nc, d):
    HID = 512
    KH = HID // P
    NG, NE = 2, 8
    NL = NG + NE
    TOPK = 2
    BIG = 1e30
    PAIRS = TILES // 2
    PAIR_E = HID // D
    SLOTS = NE // PAIR_E
    with ExitStack() as ctx:
        r = Room(nc, ctx, "moe")
        ident = r.sb("ident", [P, P])
        wo = r.sb("wo", [P, KD, D])
        wi = [r.sb(f"wi{n}", [P, KD, 2 * HID]) for n in range(2)]
        wso = r.sb("wso", [P, KH, D])
        w2 = r.sb("w2", [P, KH, NE, D])
        wl, bl = r.sb("wl", [P, KD, NL]), r.sb("bl", [P, NL])
        n1, n2 = r.sb("n1", [P, D]), r.sb("n2", [P, D])
        before = r.sb("before", [P, NE, NE])
        half = r.sb("half", [P, 1])
        a, src, x5, at, xs, x, xt, acc, y = [r.sb(n, [P, 2, D]) for n in "a src x5 at xs x xt acc y".split()]
        junk = r.sb("junk", [P, 4, D])
        ssq, va, rs = [r.sb(n, [P, 2, 2]) for n in ("ssq", "va", "rs")]
        sil, hid, hidt = [[r.sb(f"{n}{k}", [P, 2, HID]) for k in range(2)] for n in ("sil", "hid", "hidt")]
        lg, gm, em, dif, ex = r.sb("lg", [P, 2, NL]), r.sb("gm", [P, 2, 1]), r.sb("em", [P, 2, 1]), r.sb("dif", [P, 2, NL]), r.sb("ex", [P, 2, NL])
        ing, sm, pe_, w = r.sb("ing", [P, 2, NE]), r.sb("sm", [P, 2, 2]), r.sb("pe", [P, 2, NE]), r.sb("w", [P, 2, NE])
        gt, eq, rank = r.sb("gt", [P, 2, NE, NE]), r.sb("eq", [P, 2, NE, NE]), r.sb("rank", [P, 2, NE])
        ps = [[r.ps(f"ps{z}{a_}", [P, HID]) for a_ in range(2)] for z in range(2)]
        tp = [r.ps(f"tp{z}", [P, HID]) for z in range(2)]
        so = r.ps("so", [P, 2, D])
        lp = r.ps("lp", [P, 2, NL])
        m = {n: r.sem(n) for n in "w_in consts chain fchain dif_done ex_done w_done so_used".split()}
        steps = ("a_in x5_in a_free x5_free at_mm at_c wo_mm xs_done sqf vaf rsf x_done xt_mm xt_c l_mm in_mm0 in_mm1 sil0 sil1 "
                 "hid0 hid1 ht_mm0 ht_mm1 ht_c0 ht_c1 so_mm acc0 e_mm e_used acc_done sqt vat rst y_done out")
        e = {n: [r.sem(f"{n}_{z}") for z in range(2)] for n in steps.split()}
        block = ctx.enter_context(nc.Block())

        def pairs(eng):
            with eng.Fori(0, PAIRS - 1) as p:
                yield p, False
            yield PAIRS - 1, True

        @block.sync
        def _(sp):
            loads = [(ident[:], d["ident"]), (wo[:], rows_in(d["L1_ffn_Wo"])), (wi[0][:], rows_in(d["L1_ffn_W_shared_in"])),
                     (wi[1][:], rows_in(d["L1_ffn_W1_shared"])), (wso[:], rows_in(d["L1_ffn_W_shared_out"])),
                     (wl[:, :, 0:NG], rows_in(d["L1_ffn_Wg_gate"])), (wl[:, :, NG:], rows_in(d["L1_ffn_We_gate"])),
                     (bl[:, 0:NG], d["L1_ffn_group_bias"].partition_broadcast(P)), (bl[:, NG:], d["L1_ffn_expert_bias"].partition_broadcast(P)),
                     (n1[:], d["L1_ffn_norm1_w"].partition_broadcast(P)), (n2[:], d["L1_ffn_norm2_w"].partition_broadcast(P)),
                     (before[:], d["before"].partition_broadcast(P))]
            loads += [(w2[:, :, n], rows_in(d["L1_ffn_W2_experts"][n])) for n in range(NE)]
            assert len(loads) == 20
            for dst, s in loads:
                sp.dma_start(dst, s).then_inc(m["w_in"], 16)
            with sp.Fori(0, B) as b:
                with sp.Fori(0, TPB // 2) as ih:
                    p = b * (TPB // 2) + ih
                    for z in range(2):
                        hold(sp, r.passed, e["a_free"][z], p + 1)
                        sp.dma_start(a[:, z].rearrange("p (h c) -> p h c", h=4), d["at1"].rearrange("(u s) c -> u s c", s=S)
                                     [bass.ds(b * 4, 4), bass.ds((ih * 2 + z) * P, P), :].rearrange("h p c -> p h c")).then_inc(e["a_in"][z], 16)
                        sp.dma_start(src[:, z], d["src1"][bass.ds((p * 2 + z) * P, P), :]).then_inc(e["a_in"][z], 16)
                    for z in range(2):
                        hold(sp, r.passed, e["x5_free"][z], p + 1)
                        sp.dma_start(x5[:, z], d["x5"][bass.ds((p * 2 + z) * P, P), :]).then_inc(e["x5_in"][z], 16)

        @block.gpsimd
        def _(pool):
            pool.memset(half[:], -0.5).then_inc(m["consts"], 1)
            pool.wait_ge(m["consts"], 1)

            def root(p, k, signal, done, z):
                pool.wait_ge(e[signal][z], p + 1)
                pool.tensor_tensor(rs[:, z, k:k + 1], va[:, z, k:k + 1], half[:], ALU.pow).then_inc(e[done][z], 1)

            for z in range(2):
                root(0, 0, "vaf", "rsf", z)
            for p, last in pairs(pool):
                if not last:
                    for z in range(2):
                        root(p + 1, 0, "vaf", "rsf", z)
                for z in range(2):
                    root(p, 1, "vat", "rst", z)

        @block.vector
        def _(dve):
            dve.wait_ge(m["w_in"], 16 * 20)
            for z in range(2):
                dve.sem_inc(e["x5_free"][z], 1)
                dve.sem_inc(e["a_free"][z], 1)

            def first_sum(p, z):
                dve.wait_ge(e["a_in"][z], 32 * p + 32)
                dve.wait_ge(e["wo_mm"][z], p + 1)
                dve.tensor_tensor(xs[:, z], src[:, z], tp[z][:, D:2 * D], ALU.add).then_inc(e["xs_done"][z], 1)
                dve.wait_ge(e["xs_done"][z], p + 1)
                dve.sem_inc(e["a_free"][z], 1)

            def variance(p, z, k, signal, done):
                dve.wait_ge(e[signal][z], p + 1)
                dve.tensor_scalar(va[:, z, k:k + 1], ssq[:, z, k:k + 1], 1.0 / D, 1e-6, ALU.mult, ALU.add).then_inc(e[done][z], 1)

            def first_norm(p, z):
                dve.wait_ge(e["rsf"][z], p + 1)
                dve.scalar_tensor_tensor(x[:, z], xs[:, z], rs[:, z, 0:1], n1[:], ALU.mult, ALU.mult).then_inc(e["x_done"][z], 1)

            def last_norm(p, z):
                link = Link(dve, e["chain"][z], 1, p)
                dve.wait_ge(e["rst"][z], p + 1)
                dve.wait_ge(e["out"][z], 16 * p)
                link(dve.scalar_tensor_tensor(y[:, z], acc[:, z], rs[:, z, 1:2], n2[:], ALU.mult, ALU.mult))
                dve.wait_ge(e["x5_in"][z], 16 * p + 16)
                dve.tensor_tensor(y[:, z], y[:, z], x5[:, z], ALU.add).then_inc(e["y_done"][z], 1)
                dve.wait_ge(e["y_done"][z], p + 1)
                dve.sem_inc(e["x5_free"][z], 1)
                link.done()

            e["chain"] = [r.sem(f"last_chain{z}") for z in range(2)]
            wide = lambda v, n: v.to_broadcast([P, 2, n])

            def route(p):
                link = Link(dve, m["chain"], 19, p)
                for z in range(2):
                    dve.wait_ge(e["l_mm"][z], p + 1)
                for z in range(2):
                    ins = dve.tensor_tensor(lg[:, z], lp[:, z], bl[:], ALU.add)
                link(ins)
                link(dve.reduce_max(gm[:], lg[:, :, 0:NG], AX.X))
                link(dve.tensor_tensor(ing[:, :, NE // 2:], wide(lg[:, :, 1:2], NE // 2), wide(lg[:, :, 0:1], NE // 2), ALU.is_gt))
                link(dve.tensor_scalar(ing[:, :, 0:NE // 2], ing[:, :, NE // 2:], -1.0, 1.0, ALU.mult, ALU.add))
                link(dve.tensor_tensor(lg[:, :, NG:], lg[:, :, NG:], ing[:], ALU.mult))
                link(dve.tensor_scalar(ing[:], ing[:], 1.0, BIG, ALU.subtract, ALU.mult))
                link(dve.tensor_tensor(lg[:, :, NG:], lg[:, :, NG:], ing[:], ALU.add))
                link(dve.reduce_max(em[:], lg[:, :, NG:], AX.X))
                link(dve.tensor_tensor(dif[:, :, 0:NG], lg[:, :, 0:NG], wide(gm[:], NG), ALU.subtract))
                link(dve.tensor_tensor(dif[:, :, NG:], lg[:, :, NG:], wide(em[:], NE), ALU.subtract))
                dve.sem_inc(m["dif_done"], 1)
                dve.wait_ge(m["ex_done"], p + 1)
                for n, (lo, hi) in enumerate(((0, NG), (NG, NL))):
                    ins = dve.reduce_sum(sm[:, :, n:n + 1].rearrange("p z o -> p (z o)"), ex[:, :, lo:hi], AX.X)
                link(ins)
                link(dve.reciprocal(sm[:], sm[:]))
                link(dve.tensor_tensor(pe_[:], ex[:, :, NG:], wide(sm[:, :, 1:2], NE), ALU.mult))
                link(dve.tensor_tensor(pe_[:], pe_[:], wide(sm[:, :, 0:1], NE), ALU.mult))
                for z in range(2):
                    mine = pe_[:, z].rearrange("p (e o) -> p e o", o=1).to_broadcast([P, NE, NE])
                    other = pe_[:, z].rearrange("p (o f) -> p o f", o=1).to_broadcast([P, NE, NE])
                    dve.tensor_tensor(gt[:, z], other, mine, ALU.is_gt)
                    ins = dve.tensor_tensor(eq[:, z], other, mine, ALU.is_equal)
                link(ins)
                for z in range(2):
                    ins = dve.tensor_tensor(eq[:, z], eq[:, z], before[:], ALU.mult)
                link(ins)
                link(dve.tensor_tensor(gt[:], gt[:], eq[:], ALU.add))
                link(dve.reduce_sum(rank[:], gt[:], AX.X))
                link(dve.tensor_scalar(rank[:], rank[:], float(TOPK), None, ALU.is_lt))
                dve.tensor_tensor(w[:], rank[:], pe_[:], ALU.mult).then_inc(m["w_done"], 1)
                link.done()

            for z in range(2):
                first_sum(0, z)
            for z in range(2):
                variance(0, z, 0, "sqf", "vaf")
            for z in range(2):
                first_norm(0, z)
            for p, last in pairs(dve):
                route(p)
                for k in range(2):
                    for z in range(2):
                        dve.wait_ge(e[f"sil{k}"][z], p + 1)
                        dve.tensor_tensor(hid[k][:, z], sil[k][:, z], ps[z][1][:], ALU.mult).then_inc(e[f"hid{k}"][z], 1)
                for z in range(2):
                    dve.wait_ge(e["so_mm"][z], p + 1)
                    dve.tensor_tensor(acc[:, z], x[:, z], so[:, z], ALU.add).then_inc(e["acc0"][z], 1)
                dve.wait_ge(m["w_done"], p + 1)
                for s in range(2 * SLOTS):
                    z, q = s // SLOTS, s % SLOTS
                    dve.wait_ge(e["e_mm"][z], p * SLOTS + q + 1)
                    for n in range(PAIR_E):
                        k = q * PAIR_E + n
                        if k == 0:
                            dve.wait_ge(e["acc0"][z], p + 1)
                        else:
                            dve.wait_ge(e["acc_done"][z], p * NE + k)
                        dve.scalar_tensor_tensor(acc[:, z], ps[z][q % 2][:, n * D:(n + 1) * D], w[:, z, k:k + 1], acc[:, z],
                                                 ALU.mult, ALU.add).then_inc(e["acc_done"][z], 1)
                    if s == 2 and not last:
                        for y_ in range(2):
                            first_sum(p + 1, y_)
                    if s == 3 and not last:
                        for y_ in range(2):
                            variance(p + 1, y_, 0, "sqf", "vaf")
                    if s == 4:
                        if not last:
                            for y_ in range(2):
                                first_norm(p + 1, y_)
                        variance(p, 0, 1, "sqt", "vat")
                    if s == 5:
                        last_norm(p, 0)
                variance(p, 1, 1, "sqt", "vat")
                last_norm(p, 1)

        @block.scalar
        def _(act):
            def copy(p, z, signal, done, dst, source):
                act.wait_ge(e[signal][z], p + 1)
                act.activation(dst[:, z], source, ACT.Copy).then_inc(e[done][z], 1)

            def first(p):
                for z in range(2):
                    copy(p, z, "at_mm", "at_c", at, tp[z][:, 0:D])
                for z in range(2):
                    act.wait_ge(e["xs_done"][z], p + 1)
                    act.activation(junk[:, z], xs[:, z], ACT.Square, accum_out=ssq[:, z, 0:1]).then_inc(e["sqf"][z], 1)

            def first_end(p):
                for z in range(2):
                    copy(p, z, "xt_mm", "xt_c", xt, tp[z][:, 0:D])

            def last_square(p, z):
                act.wait_ge(e["acc_done"][z], p * NE + NE)
                act.activation(junk[:, 2 + z], acc[:, z], ACT.Square, accum_out=ssq[:, z, 1:2]).then_inc(e["sqt"][z], 1)

            first(0)
            first_end(0)
            for p, last in pairs(act):
                act.wait_ge(m["dif_done"], p + 1)
                act.activation(ex[:], dif[:], ACT.Exp).then_inc(m["ex_done"], 1)
                for k in range(2):
                    for z in range(2):
                        act.wait_ge(e[f"in_mm{k}"][z], p + 1)
                        act.activation(sil[k][:, z], ps[z][0][:], ACT.Silu).then_inc(e[f"sil{k}"][z], 1)
                    if k == 1:
                        for j in range(2):
                            for z in range(2):
                                copy(p, z, f"ht_mm{j}", f"ht_c{j}", hidt[j], tp[z][:])
                if not last:
                    first(p + 1)
                last_square(p, 0)
                if not last:
                    first_end(p + 1)
                last_square(p, 1)
                for z in range(2):
                    act.wait_ge(e["y_done"][z], p + 1)
                    act.dma_start(d["x6"][bass.ds((p * 2 + z) * P, P), :], y[:, z]).then_inc(e["out"][z], 16)
            for z in range(2):
                act.wait_ge(e["out"][z], 16 * PAIRS)

        @block.tensor
        def _(pe):
            def transposes(z, v, n):
                for c in range(n):
                    ins = pe.transpose(tp[z][:, c * P:(c + 1) * P], v[:, c * P:(c + 1) * P], ident[:])
                return ins

            def first_transpose(p, z):
                pe.wait_ge(e["a_in"][z], 32 * p + 32)
                pe.wait_ge(e["ht_c1"][z], p)
                transposes(z, a[:, z], KD).then_inc(e["at_mm"][z], 1)

            def first_product(p, z):
                pe.wait_ge(e["at_c"][z], p + 1)
                for k in range(KD):
                    ins = pe.matmul(tp[z][:, D:2 * D], at[:, z, k * P:(k + 1) * P], wo[:, k], start=k == 0, stop=k == KD - 1)
                ins.then_inc(e["wo_mm"][z], 1)

            def norm_transpose(p, z):
                pe.wait_ge(e["x_done"][z], p + 1)
                transposes(z, x[:, z], KD).then_inc(e["xt_mm"][z], 1)

            def logits(p, z):
                pe.wait_ge(e["xt_c"][z], p + 1)
                for k in range(KD):
                    ins = pe.matmul(lp[:, z], xt[:, z, k * P:(k + 1) * P], wl[:, k], start=k == 0, stop=k == KD - 1)
                ins.then_inc(e["l_mm"][z], 1)

            def into(p, z, k):
                if k:
                    pe.wait_ge(e["hid0"][z], p + 1)
                else:
                    pe.wait_ge(e["acc_done"][z], p * NE)
                for a_ in range(2):
                    for c in range(KD):
                        ins = pe.matmul(ps[z][a_][:], xt[:, z, c * P:(c + 1) * P], wi[k][:, c, a_ * HID:(a_ + 1) * HID],
                                        start=c == 0, stop=c == KD - 1)
                ins.then_inc(e[f"in_mm{k}"][z], 1)

            def hidden_transpose(p, z, k):
                pe.wait_ge(e[f"hid{k}"][z], p + 1)
                if k:
                    pe.wait_ge(e["ht_c0"][z], p + 1)
                transposes(z, hid[k][:, z], KH).then_inc(e[f"ht_mm{k}"][z], 1)

            def shared_out(p, z):
                pe.wait_ge(e["ht_c0"][z], p + 1)
                pe.wait_ge(e["acc0"][1 - z], p + z)
                for k in range(KH):
                    ins = pe.matmul(so[:, z], hidt[0][:, z, k * P:(k + 1) * P], wso[:, k], start=k == 0, stop=k == KH - 1)
                ins.then_inc(e["so_mm"][z], 1)

            def experts(p, z, q):
                if q == 0:
                    pe.wait_ge(e["hid1"][z], p + 1)
                    pe.wait_ge(e["ht_c1"][z], p + 1)
                elif q >= 2:
                    pe.wait_ge(e["acc_done"][z], p * NE + (q - 1) * PAIR_E)
                for k in range(KH):
                    ins = pe.matmul(ps[z][q % 2][:], hidt[1][:, z, k * P:(k + 1) * P],
                                    w2[:, k, q * PAIR_E:(q + 1) * PAIR_E].rearrange("p e n -> p (e n)"), start=k == 0, stop=k == KH - 1)
                ins.then_inc(e["e_mm"][z], 1)

            pe.wait_ge(m["w_in"], 16 * 20)
            for step in (first_transpose, first_product, norm_transpose, logits):
                for z in range(2):
                    step(0, z)
            for p, last in pairs(pe):
                for z in range(2):
                    into(p, z, 0)
                for z in range(2):
                    into(p, z, 1)
                    hidden_transpose(p, z, 0)
                for z in range(2):
                    shared_out(p, z)
                    hidden_transpose(p, z, 1)
                for s in range(2 * SLOTS):
                    experts(p, s // SLOTS, s % SLOTS)
                    if not last:
                        step = {0: first_transpose, 1: first_product, 5: norm_transpose, 6: logits}.get(s)
                        if step:
                            for z in range(2):
                                step(p + 1, z)


SCRATCH = {
    "q3": ((3, D, T), BF16), "k3": ((3, D, T), BF16), "v0": ((T, D), F32), "aux": ((T, 4 + 3 * NH), F32),
    "ljd": ((3, T), F32), "attn": ((T, D), F32),
    "x1": ((T, D), F32), "x2": ((T, D), F32), "x3": ((T, D), F32), "x4": ((T, D), F32), "x5": ((T, D), F32),
    "qkv": ((T, 3 * GD), F32), "ab": ((T, 2 * GH), F32), "o": ((T, GD), F32),
    "src1": ((T, D), F32), "q1": ((3, B * D, S), BF16), "k1": ((3, B * D, S), BF16), "v1": ((4 * T, D // 4), F32),
    "mx1": ((3 * 2 * NH, 16, P), BF16), "at1": ((4 * T, D // 4), F32),
    "latt": ((B * NH, S, HD), F32),
    "x6": ((T, D), F32),
}


def layout(inputs):
    a = {k: np.asarray(v) for k, v in inputs.items()}
    out = {"ident": np.eye(P, dtype=np.float32)}
    out["head_mask"] = np.repeat(np.eye(NH // 2, dtype=np.float32), HD, axis=0)
    t, u = np.arange(P)[:, None], np.arange(P)[None, :]
    below = lambda n: ((t // n) % 2 == 1) & (u // n == t // n - 1)
    eye = np.eye(P, dtype=np.float32)
    out["eye4"] = np.repeat(eye[:, None], 4, axis=1)
    out["levels"] = np.stack([eye - below(2 ** n) for n in range(1, 7)], axis=1).astype(np.float32)
    out["level0t"] = -below(1).T.astype(np.float32)
    out["eye8"] = np.eye(GH, dtype=np.float32)
    out["alpha_mask"] = np.repeat(out["eye8"][:, :, None], P, axis=2)
    out["alpha_mask"][:, :, 0] = 0
    out["ctx"] = a["ctx_1024"].reshape(-1, D)
    out["mask_ff"] = a["mask_BxS2_ff1"].reshape(-1, 1)
    heads = np.repeat(np.eye(NH, dtype=np.float32), HD, axis=1)
    same = np.concatenate([heads.T @ heads > 0, heads.T > 0], axis=1).astype(np.float32)
    out["same_head"] = same.reshape(KD, P, -1).transpose(1, 0, 2)
    out["before"] = np.tril(np.ones((8, 8), np.float32), -1)
    freq = 1.0 / np.float32(10000.0) ** (np.arange(0, HD, 2, dtype=np.float32) / np.float32(HD))
    ang = (np.arange(S, dtype=np.float32)[None, :] * freq[:, None]).astype(np.float64)
    out["rope_cos"] = np.tile(np.repeat(np.cos(ang), 2, axis=0), (P // HD, 1)).astype(np.float32)
    out["rope_sin"] = np.tile(np.stack([-np.sin(ang), np.sin(ang)], axis=1).reshape(HD, S), (P // HD, 1)).astype(np.float32)
    for name in ("L1_ffn_Wq", "L1_ffn_Wk"):
        out[name + "_swapped"] = a[name].reshape(-1, D // 2, 2)[:, :, ::-1].reshape(-1, D)
    out["mask_words"] = np.repeat(a["mask_BxS2_bk0"].view(np.uint8), 4, axis=1).view(np.int32)
    out["x"] = a["x"].reshape(T, D)
    for k, v in a.items():
        if k in ("L0_attn_Wq", "L0_attn_Wk", "L0_attn_Wv", "L0_attn_Wo", "L0_attn_gate_W", "L0_attn_rel_W",
                 "L0_attn_logical_bias", "L0_xattn_Wq_w", "L0_xattn_Wkv_w", "L0_xattn_out_w",
                 "L0_ffn_w_gate", "L0_ffn_w_up", "L0_ffn_w_down"):
            out[k + "T"] = np.ascontiguousarray(v.T)
        elif k in ("L0_attn_bq", "L0_attn_bk"):
            out[k + "_cols"] = v.reshape(-1, P).T
        elif k not in ("x", "ctx_1024", "mask_BxS2_bk0"):
            out[k] = v
        if k in ("L0_xattn_Wq_b", "L0_xattn_Wkv_b"):
            out[k + "_cols"] = v.reshape(-1, P).T
    return {k: np.ascontiguousarray(v) for k, v in out.items()}


STAGES = (stage_pre0, stage_attn0, stage_mid0, stage_ffn0, stage_gdn_in, stage_gdn_core, stage_gdn_out, stage_lin,
          stage_lin_out, stage_pre1, stage_attn1, stage_moe)


def kernel(**inputs):
    import concourse.bacc as bacc
    from concourse.bass_utils import run_bass_kernel_spmd

    nc = bacc.Bacc("TRN2", target_bir_lowering=False, num_devices=1)
    arrays, d = {}, {}
    for name, a in layout(inputs).items():
        arrays[f"in_{name}"] = a
        d[name] = nc.dram_tensor(f"in_{name}", a.shape, mybir.dt.from_np(a.dtype), kind="ExternalInput").ap()
    for name, (shape, dtype) in SCRATCH.items():
        d[name] = nc.dram_tensor(f"s_{name}", shape, dtype, kind="ExternalOutput" if name == "x6" else "Internal").ap()
    for stage in STAGES:
        stage(nc, d)
    results = run_bass_kernel_spmd(nc, [arrays], core_ids=[0]).results[0]
    return results["s_x6"].reshape(B, S, D)
```

```python
import numpy as np
from contextlib import ExitStack

import concourse.bass as bass
from concourse import mybir

F32 = mybir.dt.float32
BF16 = mybir.dt.bfloat16
ALU = mybir.AluOpType
ACT = mybir.ActivationFunctionType
AX = mybir.AxisListType

P = 128
B, S, D = 4, 1024, 256
T = B * S
TILES = T // P
TPB = S // P
KD = D // P
NH = 16
HD = D // NH
SPLIT = 6
Q_PART = (0, 0, 1, 1, 0, 2)
K_PART = (0, 1, 0, 1, 2, 0)


class Link:

    def __init__(self, eng, sem, per, turn=None):
        self.eng, self.sem, self.per, self.turn, self.n = eng, sem, per, turn, 0

    def __call__(self, ins):
        self.n += 1
        ins.then_inc(self.sem, 1)
        self.eng.wait_ge(self.sem, self.n if self.turn is None else self.turn * self.per + self.n)

    def alone(self, ins, passed):
        self.n += 1
        ins.then_inc(self.sem, 1)
        hold(self.eng, passed, self.sem, self.n if self.turn is None else self.turn * self.per + self.n)

    def done(self):
        assert self.turn is None or self.n == self.per, (self.n, self.per)


def hold(eng, passed, sem, value):
    eng.wait_ge(sem, value)
    eng.sem_inc(passed, 1)


class Room:

    def __init__(self, nc, ctx, stage):
        self.nc, self.ctx, self.stage, self.sems = nc, ctx, stage, []
        ctx.callback(self.leave)
        self.passed = self.sem("passed")

    def sb(self, name, shape, dt=F32):
        return self.ctx.enter_context(self.nc.sbuf_tensor(f"{self.stage}_{name}", shape, dt))

    def ps(self, name, shape, dt=F32):
        return self.ctx.enter_context(self.nc.psum_tensor(f"{self.stage}_{name}", shape, dt))

    def sem(self, name):
        self.sems.append(self.nc.alloc_semaphore(f"{self.stage}_{name}"))
        return self.sems[-1]

    def leave(self):
        self.nc.all_engine_barrier()
        self.nc.clear_and_free_semaphores(self.sems)
        self.nc.all_engine_barrier()


def rows_in(w):
    return w.rearrange("(c p) n -> p c n", p=P)


def stage_pre0(nc, d):
    G = 4
    W = G * P
    NR = D + NH + 3
    with ExitStack() as ctx:
        r = Room(nc, ctx, "pre0")
        ident = r.sb("ident", [P, P])
        wq, wk = r.sb("wq", [P, KD, D]), r.sb("wk", [P, KD, D])
        wrow = r.sb("wrow", [P, KD, NR])
        wlj, wld = r.sb("wlj", [P, KD, 3]), r.sb("wld", [P, KD, 3])
        bq, bk = r.sb("bq", [P, KD]), r.sb("bk", [P, KD])
        bqs = r.sb("bqs", [P, KD])
        brow = r.sb("brow", [P, NR])
        lb = r.sb("lb", [P, 3, NH])
        x = r.sb("x", [P, G, D])
        st = r.sb("st", [P, G, 6])
        mv = r.sb("mv", [P, G, 2])
        var, rstd, half, eps = [r.sb(n, [P, G]) for n in ("var", "rstd", "half", "eps")]
        xn = r.sb("xn", [P, G, D])
        xt = r.sb("xt", [P, KD, W])
        qf, qr = r.sb("qf", [P, 2, W]), r.sb("qr", [P, 2, W])
        parts = r.sb("parts", [P, 2, 3, W], BF16)
        ljs = r.sb("ljs", [3, W])
        row = r.sb("row", [P, 2, NR])
        aux = r.sb("aux", [P, 2, 4 + 3 * NH])
        gate = r.sb("gate", [P, 2, NH])
        tp = [r.ps(f"tp{n}", [P, KD, P]) for n in range(2)]
        qk = [r.ps(f"qk{n}", [P, W]) for n in range(2)]
        ljp = r.ps("ljp", [3, W])
        rowp = [r.ps(f"rowp{n}", [P, NR]) for n in range(2)]

        w_in, consts, x_in, x_free = r.sem("w_in"), r.sem("consts"), r.sem("x_in"), r.sem("x_free")
        mv_done, rstd_done, xn_done = r.sem("mv_done"), r.sem("rstd_done"), r.sem("xn_done")
        tp_done, xt_done, mm_done = r.sem("tp_done"), r.sem("xt_done"), r.sem("mm_done")
        qk_done, qf_done, qk_free = r.sem("qk_done"), r.sem("qf_done"), r.sem("qk_free")
        parts_done, parts_out = r.sem("parts_done"), [r.sem(f"parts_out{n}") for n in range(2)]
        lj_done, lj_free, lj_out = r.sem("lj_done"), r.sem("lj_free"), r.sem("lj_out")
        row_done, row_free, gate_in, gate_done = r.sem("row_done"), r.sem("row_free"), r.sem("gate_in"), r.sem("gate_done")
        v_out, aux_out = [[r.sem(f"{a}{n}") for n in range(2)] for a in ("v_out", "aux_out")]
        aux_done = r.sem("aux_done")
        chain, pchain = r.sem("chain"), r.sem("pchain")
        block = ctx.enter_context(nc.Block())
        LOADS = 14

        @block.sync
        def _(sp):
            for dst, src in (
                (ident[:], d["ident"]), (wq[:], rows_in(d["L0_attn_WqT"])), (wk[:], rows_in(d["L0_attn_WkT"])),
                (wrow[:, :, 0:D], rows_in(d["L0_attn_WvT"])), (wrow[:, :, D:D + NH], rows_in(d["L0_attn_gate_WT"])),
                (wrow[:, :, D + NH:NR], rows_in(d["L0_attn_rel_WT"][0:D, :])),
                (wlj[:], rows_in(d["L0_attn_rel_WT"][D:2 * D, :])),
                (bq[:], d["L0_attn_bq_cols"]), (bk[:], d["L0_attn_bk_cols"]),
                (brow[:, 0:D], d["L0_attn_bv"].partition_broadcast(P)),
                (brow[:, D:D + NH], d["L0_attn_gate_b"].partition_broadcast(P)),
                (brow[:, D + NH:NR], d["L0_attn_rel_b"].partition_broadcast(P)),
                (lb[:], d["L0_attn_logical_biasT"].partition_broadcast(P)),
            ):
                sp.dma_start(dst, src).then_inc(w_in, 16)
            with sp.Fori(0, T // W) as i:
                hold(sp, r.passed, x_free, i + 1)
                sp.dma_start(x[:], d["x"][bass.ds(i * W, W), :].rearrange("(s p) c -> p s c", p=P)).then_inc(x_in, 16)
                for n in range(4):
                    dst = d["q3"] if n < 2 else d["k3"]
                    c = n % 2
                    hold(sp, r.passed, parts_done, i * 4 + n + 1)
                    sp.dma_start(dst[:, c * P:(c + 1) * P, bass.ds(i * W, W)].rearrange("a p t -> p a t"),
                                 parts[:, n % 2]).then_inc(parts_out[n % 2], 16)
                hold(sp, r.passed, lj_done, 2 * i + 2)
                sp.dma_start(d["ljd"][:, bass.ds(i * W, W)], ljs[:]).then_inc(lj_out, 16)
                for s in range(G):
                    hold(sp, r.passed, aux_done, i * G + s + 1)
                    sp.dma_start(d["v0"][bass.ds(i * W + s * P, P), :], row[:, s % 2, 0:D]).then_inc(v_out[s % 2], 16)
                    sp.dma_start(d["aux"][bass.ds(i * W + s * P, P), :], aux[:, s % 2]).then_inc(aux_out[s % 2], 16)
            sp.wait_ge(lj_out, 16 * (T // W))
            for n in range(2):
                sp.wait_ge(v_out[n], 16 * TILES // 2)
                sp.wait_ge(aux_out[n], 16 * TILES // 2)
                sp.wait_ge(parts_out[n], 16 * 2 * (T // W))

        @block.gpsimd
        def _(pool):
            pool.memset(eps[:], 1e-5)
            pool.memset(half[:], -0.5).then_inc(pchain, 1)
            pool.wait_ge(pchain, 1)
            with pool.Fori(0, T // W) as i:
                pool.wait_ge(mv_done, i + 1)
                pool.tensor_tensor(var[:], mv[:, :, 1], eps[:], ALU.add).then_inc(pchain, 1)
                pool.wait_ge(pchain, i + 2)
                pool.tensor_tensor(rstd[:], var[:], half[:], ALU.pow).then_inc(rstd_done, 1)

        @block.vector
        def _(dve):
            dve.wait_ge(w_in, 16 * 13)
            for c, (a, b) in enumerate(((1, 0), (2, 0), (2, 1))):
                dve.tensor_tensor(wld[:, :, c], wlj[:, :, a], wlj[:, :, b], ALU.subtract)
            dve.tensor_tensor(lb[:, 0:2], lb[:, 0:2], lb[:, 2:3].to_broadcast([P, 2, NH]), ALU.subtract)
            dve.tensor_scalar(bqs[:], bq[:], HD ** -0.5, None, ALU.mult).then_inc(consts, 1)
            dve.sem_inc(x_free, 1)
            dve.sem_inc(qk_free, 2)
            dve.sem_inc(row_free, 2)
            dve.sem_inc(lj_free, 1)
            with dve.Fori(0, T // W) as i:
                link = Link(dve, chain, 37, i)
                dve.wait_ge(x_in, i * 16 + 16)
                for s in range(G):
                    ins = dve.bn_stats(st[:, s], x[:, s])
                link.alone(ins, r.passed)
                for s in range(G):
                    ins = dve.bn_aggr(mv[:, s], st[:, s])
                ins.then_inc(mv_done, 1)
                dve.wait_ge(rstd_done, i + 1)
                for s in range(G):
                    ins = dve.tensor_scalar(xn[:, s], x[:, s], mv[:, s, 0:1], rstd[:, s:s + 1], ALU.subtract, ALU.mult)
                    ins.then_inc(xn_done, 1)
                dve.wait_ge(xn_done, i * G + G)
                dve.sem_inc(x_free, 1)
                for n in range(4):
                    h = n % 2
                    dve.wait_ge(qf_done, i * 4 + n + 1)
                    dve.wait_ge(parts_out[h], i * 32 + 16 * (n // 2))
                    link(dve.tensor_copy(parts[:, h, 0], qf[:, h]))
                    link(dve.tensor_tensor(qr[:, h], qf[:, h], parts[:, h, 0], ALU.subtract))
                    dve.sem_inc(qk_free, 1)
                    link(dve.tensor_copy(parts[:, h, 1], qr[:, h]))
                    link(dve.tensor_tensor(parts[:, h, 2], qr[:, h], parts[:, h, 1], ALU.subtract))
                    dve.sem_inc(parts_done, 1)
                dve.wait_ge(lj_done, 2 * i + 1)
                dve.wait_ge(lj_out, i * 16)
                dve.tensor_copy(ljs[:], ljp[:]).then_inc(lj_done, 1)
                for s in range(G):
                    h = s % 2
                    dve.wait_ge(row_done, i * G + s + 1)
                    dve.wait_ge(v_out[h], i * 32 + 16 * (s // 2))
                    dve.wait_ge(aux_out[h], i * 32 + 16 * (s // 2))
                    link(dve.tensor_tensor(row[:, h], rowp[h][:], brow[:], ALU.add))
                    dve.sem_inc(gate_in, 1)
                    link(dve.tensor_tensor(aux[:, h, 0:1], row[:, h, D + NH + 1:D + NH + 2], row[:, h, D + NH:D + NH + 1], ALU.subtract))
                    link(dve.tensor_tensor(aux[:, h, 1:3], row[:, h, D + NH + 2:D + NH + 3].to_broadcast([P, 2]), row[:, h, D + NH:D + NH + 2], ALU.subtract))
                    link(dve.tensor_tensor(aux[:, h, 3:4], row[:, h, D + NH:D + NH + 1], row[:, h, D + NH + 1:D + NH + 2], ALU.subtract))
                    dve.wait_ge(gate_done, i * G + s + 1)
                    link(dve.tensor_tensor(aux[:, h, 4:].rearrange("p (a h) -> p a h", a=3), lb[:],
                                           gate[:, h:h + 1].to_broadcast([P, 3, NH]), ALU.mult))
                    dve.sem_inc(aux_done, 1)
                    dve.sem_inc(row_free, 1)
                link.done()

        @block.scalar
        def _(act):
            act.wait_ge(consts, 1)
            with act.Fori(0, T // W) as i:
                act.wait_ge(mm_done, i)
                for s in range(G):
                    act.wait_ge(tp_done, i * G + s + 1)
                    act.activation(xt[:, :, s * P:(s + 1) * P], tp[s % 2][:], ACT.Copy).then_inc(xt_done, 1)
                for n in range(4):
                    c, h = n % 2, n % 2
                    act.wait_ge(qk_done, i * 4 + n + 1)
                    act.wait_ge(qk_free, i * 4 + n + 1)
                    if n < 2:
                        act.activation(qf[:, h], qk[h][:], ACT.Identity, bias=bqs[:, c:c + 1], scale=HD ** -0.5).then_inc(qf_done, 1)
                    else:
                        act.activation(qf[:, h], qk[h][:], ACT.Identity, bias=bk[:, c:c + 1]).then_inc(qf_done, 1)
                for s in range(G):
                    h = s % 2
                    act.wait_ge(gate_in, i * G + s + 1)
                    act.activation(gate[:, h], row[:, h, D:D + NH], ACT.Sigmoid).then_inc(gate_done, 1)

        @block.tensor
        def _(pe):
            pe.wait_ge(w_in, 16 * 13)
            pe.wait_ge(consts, 1)
            pe.sem_inc(xt_done, 2)
            with pe.Fori(0, T // W) as i:
                for s in range(G):
                    pe.wait_ge(xn_done, i * G + s + 1)
                    pe.wait_ge(xt_done, i * G + s + 1)
                    for c in range(KD):
                        ins = pe.transpose(tp[s % 2][:, c], xn[:, s, c * P:(c + 1) * P], ident[:])
                    ins.then_inc(tp_done, 1)
                pe.wait_ge(xt_done, i * G + G + 2)
                for n in range(4):
                    w = wq if n < 2 else wk
                    c = n % 2
                    if n >= 2:
                        pe.wait_ge(qf_done, i * 4 + n - 1)
                    else:
                        pe.wait_ge(qf_done, i * 4)
                    for k in range(KD):
                        ins = pe.matmul(qk[n % 2][:], w[:, k, c * P:(c + 1) * P], xt[:, k], start=k == 0, stop=k == KD - 1)
                    ins.then_inc(qk_done, 1)
                pe.wait_ge(lj_done, 2 * i)
                for k in range(KD):
                    ins = pe.matmul(ljp[:], wld[:, k], xt[:, k], start=k == 0, stop=k == KD - 1)
                ins.then_inc(lj_done, 1)
                for s in range(G):
                    pe.wait_ge(row_free, i * G + s + 1)
                    for k in range(KD):
                        ins = pe.matmul(rowp[s % 2][:], xt[:, k, s * P:(s + 1) * P], wrow[:, k], start=k == 0, stop=k == KD - 1)
                    if s < G - 1:
                        ins.then_inc(row_done, 1)
                ins.then_inc(row_done, 1)
                pe.wait_ge(row_done, i * G + G)
                pe.sem_inc(mm_done, 1)




def stage_attn0(nc, d):
    NB = S // P
    GR = 4
    ROWS = SPLIT * HD
    NT = 4
    STREAM = NT * NH
    PAIRS = TILES // 2
    BUF = 4
    LAG = 2
    with ExitStack() as ctx:
        r = Room(nc, ctx, "attn0")
        ident = r.sb("ident", [P, P])
        kt = r.sb("kt", [ROWS, NH, S], BF16)
        qt = r.sb("qt", [ROWS, 2, NH, P], BF16)
        vs = r.sb("vs", [P, NB, D])
        v32 = r.sb("v32", [P, NB, NH, 32])
        lj = r.sb("lj", [P, 3, S])
        aux = r.sb("aux", [P, 2, 4 + 3 * NH])
        ex = r.sb("ex", [P, 4, S])
        rel = r.sb("rel", [P, 2, 2, S])
        u = r.sb("u", [P, 4, S])
        pr = r.sb("pr", [P, BUF, S])
        nm = r.sb("nm", [P, 2, NH])
        pt = r.sb("pt", [P, 2 * GR, NB, P])
        os_ = r.sb("os", [P, GR, P])
        rs = r.sb("rs", [P, NH])
        row = r.sb("row", [P, 2, D])
        sc = [r.ps(f"s{n}", [P, 2, 512]) for n in range(2)]
        tp = [r.ps(f"tp{n}", [P, 4, P]) for n in range(2)]
        op = [r.ps(f"op{n}", [P, GR, P]) for n in range(2)]
        names = ("id_in consts kv_in kv_free v_ready lj_in lj_ok q_in0 q_in1 q_free ex_done sum_done ln_done rel_done "
                 "u_done mix_done ns_done qk_done exp_done tp_done pt_done pv_done os_done ot_done row_done out0 out1 chain")
        m = {n: r.sem(n) for n in names.split()}
        block = ctx.enter_context(nc.Block())

        def bodies(eng, before=None, after=None):
            with eng.Fori(0, B) as b:
                if before:
                    before(b)
                with eng.Fori(0, TPB // NT) as ih:
                    yield b * (TPB // NT) + ih
                if after:
                    after(b)

        tile = lambda v, z: v * NT + z
        use = lambda v, z: v * (NT // 2) + z // 2
        head = lambda v, x: v * STREAM + x

        @block.sync
        def _(sp):
            sp.dma_start(ident[:], d["ident"]).then_inc(m["id_in"], 16)

            def load_queries(pair, tiles=(0, 1)):
                for z in tiles:
                    i = pair * 2 + z
                    hold(sp, r.passed, m["q_free"], i + 1)
                    for slot in range(SPLIT):
                        sp.dma_start(qt[slot * HD:(slot + 1) * HD, z],
                                     d["q3"][Q_PART[slot], :, bass.ds(i * P, P)].rearrange("(h e) t -> e h t", e=HD)
                                     ).then_inc(m[f"q_in{z}"], 16)
                    sp.dma_start(aux[:, z], d["aux"][bass.ds(i * P, P), :]).then_inc(m[f"q_in{z}"], 16)

            with sp.Fori(0, B) as b:
                hold(sp, r.passed, m["ex_done"], b * TPB * 2)
                sp.dma_start(lj[:], d["ljd"][:, bass.ds(b * S, S)].partition_broadcast(P)).then_inc(m["lj_in"], 16)
                hold(sp, r.passed, m["lj_in"], b * 16 + 16)
                sp.sem_inc(m["lj_ok"], 1)
                load_queries(b * (TPB // 2), (0,))
                hold(sp, r.passed, m["kv_free"], b + 1)
                for slot in range(SPLIT):
                    sp.dma_start(kt[slot * HD:(slot + 1) * HD], d["k3"][K_PART[slot], :, bass.ds(b * S, S)]
                                 .rearrange("(h e) t -> e h t", e=HD)).then_inc(m["kv_in"], 16)
                sp.dma_start(vs[:], d["v0"][bass.ds(b * S, S), :].rearrange("(n p) c -> p n c", p=P)).then_inc(m["kv_in"], 16)
                load_queries(b * (TPB // 2), (1,))
                sp.sem_inc(m["lj_ok"], 1)
                with sp.Fori(1, TPB // 2 - 1) as ih:
                    load_queries(b * (TPB // 2) + ih)
                    sp.sem_inc(m["lj_ok"], 1)
                load_queries(b * (TPB // 2) + TPB // 2 - 1)
            sp.sem_inc(m["lj_ok"], 1)
            sp.wait_ge(m["q_in0"], 112 * PAIRS)
            sp.sem_inc(m["q_in0"], 112)

        @block.gpsimd
        def _(pool):
            pool.memset(v32[:, :, :, HD + 1:], 0.0)
            pool.memset(v32[:, :, :, HD:HD + 1], 1.0).then_inc(m["consts"], 1)
            pool.wait_ge(m["consts"], 1)

            def pad_values(b):
                hold(pool, r.passed, m["kv_in"], b * 112 + 112)
                hold(pool, r.passed, m["pv_done"], b * TPB * GR + 2)
                pool.tensor_copy(v32[:, :, :, 0:HD], vs[:].rearrange("p n (h e) -> p n h e", e=HD)).then_inc(m["v_ready"], 1)

            for v in bodies(pool, pad_values):
                for x in range(STREAM):
                    z, h = x // NH, x % NH
                    if h == 0:
                        hold(pool, r.passed, m["rel_done"], tile(v, z) + 1)
                    hold(pool, r.passed, m["ns_done"], head(v, x) + 1)
                    pool.tensor_scalar(u[:, x % 4], rel[:, z % 2, 1], aux[:, z % 2, 4 + NH + h:5 + NH + h],
                                       aux[:, z % 2, 4 + 2 * NH + h:5 + 2 * NH + h], ALU.mult, ALU.add).then_inc(m["u_done"], 1)
            for z in range(2):
                pool.wait_ge(m[f"out{z}"], PAIRS * 16)

        @block.vector
        def _(dve):
            dve.sem_inc(m["kv_free"], 1)
            dve.sem_inc(m["q_free"], 2)
            dve.sem_inc(m["ns_done"], 4)
            dve.sem_inc(m["row_done"], 1)

            def relation_sum(i, z, c):
                dve.wait_ge(m["ex_done"], i * 2 + c + 1)
                dve.tensor_tensor(rel[:, z % 2, c], ex[:, 2 * c], ex[:, 2 * c + 1], ALU.add).then_inc(m["sum_done"], 1)

            def mix(v, x):
                z, h = x // NH, x % NH
                if h == 0:
                    dve.wait_ge(m[f"q_in{z % 2}"], use(v, z) * 112 + 112)
                    dve.wait_ge(m["rel_done"], tile(v, z) + 1)
                dve.wait_ge(m["u_done"], head(v, x) + 1)
                dve.scalar_tensor_tensor(u[:, x % 4], rel[:, z % 2, 0], aux[:, z % 2, 4 + h:5 + h], u[:, x % 4], ALU.mult, ALU.add
                                         ).then_inc(m["mix_done"], 1)

            def score(v, x):
                dve.wait_ge(m["mix_done"], head(v, x) + 1)
                dve.wait_ge(m["qk_done"], head(v, x) + 1)
                hold(dve, r.passed, m["tp_done"], head(v, x) * 2 + 2)
                dve.tensor_tensor_reduce(pr[:, x % BUF], u[:, x % 4], sc[x % 2][:].rearrange("p a n -> p (a n)"), -1.0, 3e38,
                                         ALU.add, ALU.min, nm[:, x // NH % 2, x % NH:x % NH + 1]).then_inc(m["ns_done"], 1)

            def normalise(v, z):
                link = Link(dve, m["chain"], 1, tile(v, z))
                dve.wait_ge(m["ot_done"], tile(v, z) + 1)
                o = op[z % 2][:].rearrange("p g (h e) -> p (g h) e", e=32)
                link(dve.reciprocal(rs[:].rearrange("p (h o) -> p h o", o=1), o[:, :, HD:HD + 1]))
                dve.wait_ge(m[f"out{z % 2}"], use(v, z) * 16)
                dve.tensor_tensor(row[:, z % 2].rearrange("p (h e) -> p h e", e=HD), o[:, :, 0:HD],
                                  rs[:].rearrange("p (h o) -> p h o", o=1).to_broadcast([P, NH, HD]), ALU.mult).then_inc(m["row_done"], 1)
                link.done()

            for c in range(2):
                relation_sum(0, 0, c)
            for v in bodies(dve, after=lambda b: dve.sem_inc(m["kv_free"], 1)):
                for x in range(STREAM + 1):
                    if x < STREAM:
                        mix(v, x)
                    if x:
                        score(v, x - 1)
                        z, h = (x - 1) // NH, (x - 1) % NH
                        if h in (5, 9):
                            relation_sum(tile(v, z + 1), z + 1, (h - 5) // 4)
                        if h == NH - 1:
                            dve.wait_ge(m["ns_done"], tile(v, z + 1) * NH + 4)
                            dve.sem_inc(m["q_free"], 1)
                        if z and h == 13:
                            normalise(v, z - 1)
                normalise(v, NT - 1)

        @block.scalar
        def _(act):
            def relation(v, z, n):
                if n == 0:
                    act.wait_ge(m[f"q_in{z % 2}"], use(v, z) * 112 + 112)
                    act.wait_ge(m["lj_ok"], use(v, z) + 1)
                    act.wait_ge(m["sum_done"], tile(v, z) * 2)
                c, sign, bias = ((0, 1.0, 0), (1, 1.0, 1), (0, -1.0, 3), (2, 1.0, 2))[n]
                ins = act.activation(ex[:, n], lj[:, c], ACT.Exp, bias=aux[:, z % 2, bias:bias + 1], scale=sign)
                if n % 2:
                    ins.then_inc(m["ex_done"], 1)

            def relation_log(v, z):
                act.wait_ge(m["sum_done"], tile(v, z) * 2 + 2)
                act.activation(rel[:, z % 2], rel[:, z % 2], ACT.Ln, bias=1.0).then_inc(m["ln_done"], 1)

            def relation_end(v, z):
                act.wait_ge(m["ln_done"], tile(v, z) + 1)
                act.activation(rel[:, z % 2], rel[:, z % 2], ACT.Exp, scale=-1.0).then_inc(m["rel_done"], 1)

            def evacuate(v, z):
                act.wait_ge(m["pv_done"], tile(v, z) * GR + GR + 2)
                act.wait_ge(m["ot_done"], tile(v, z))
                act.activation(os_[:], op[z % 2][:], ACT.Copy).then_inc(m["os_done"], 1)

            def store(v, z):
                act.wait_ge(m["row_done"], tile(v, z) + 2)
                act.dma_start(d["attn"][bass.ds(tile(v, z) * P, P), :], row[:, z % 2]).then_inc(m[f"out{z % 2}"], 16)

            for n in range(4):
                relation(0, 0, n)
            relation_log(0, 0)
            relation_end(0, 0)
            for v in bodies(act):
                for x in range(STREAM + LAG):
                    z, h = x // NH, x % NH
                    if x >= LAG:
                        y = x - LAG
                        if y % GR == 0:
                            act.wait_ge(m["pv_done"], v * NT * GR + y // GR + 1)
                        for k in range(2):
                            act.wait_ge(m["tp_done"], head(v, y) * 2 + k + 1 + 2 * BUF)
                            act.activation(pt[:, y % (2 * GR), 4 * k:4 * k + 4], tp[k][:], ACT.Copy).then_inc(m["pt_done"], 1)
                    if x < STREAM:
                        act.wait_ge(m["ns_done"], head(v, x) + 5)
                        act.activation(pr[:, x % BUF], pr[:, x % BUF], ACT.Exp, bias=nm[:, z % 2, h:h + 1], scale=-1.0).then_inc(m["exp_done"], 1)
                    if x < STREAM:
                        if h in (0, 2, 4, 6):
                            relation(v, z + 1, h // 2)
                        if h == 9:
                            relation_log(v, z + 1)
                        if h == 10:
                            relation_end(v, z + 1)
                        if z and h == 7:
                            evacuate(v, z - 1)
                        if z and h == 15:
                            store(v, z - 1)
                evacuate(v, NT - 1)
                store(v, NT - 1)

        @block.tensor
        def _(pe):
            pe.wait_ge(m["id_in"], 16)
            pe.sem_inc(m["pv_done"], 2)
            pe.sem_inc(m["tp_done"], 2 * BUF)

            def scores(v, x):
                z, h = x // NH, x % NH
                if h == 0:
                    pe.wait_ge(m[f"q_in{z % 2}"], use(v, z) * 112 + 112)
                pe.wait_ge(m["ns_done"], head(v, x) + 3)
                for k in range(2):
                    ins = pe.matmul(sc[x % 2][:, k], qt[:, z % 2, h], kt[:, h, k * 512:(k + 1) * 512], start=True, stop=True)
                ins.then_inc(m["qk_done"], 1)

            def transposes(v, x):
                pe.wait_ge(m["exp_done"], head(v, x) + 1)
                for k in range(2):
                    if x:
                        pe.wait_ge(m["pt_done"], head(v, x) * 2 + k - 1)
                    else:
                        pe.wait_ge(m["pt_done"], head(v, 0) * 2)
                    for n in range(4):
                        ins = pe.transpose(tp[k][:, n], pr[:, x % BUF, (4 * k + n) * P:(4 * k + n + 1) * P], ident[:])
                    ins.then_inc(m["tp_done"], 1)

            def weigh(v, g, piece):
                if piece == 0:
                    pe.wait_ge(m["pt_done"], head(v, GR * (g + 1)) * 2)
                    if g % GR == 0:
                        pe.wait_ge(m["row_done"], tile(v, g // GR))
                for n in range(piece * NB // GR, (piece + 1) * NB // GR):
                    for h4 in range(GR):
                        x = g * GR + h4
                        ins = pe.matmul(op[g // GR % 2][32 * h4:32 * h4 + 32, g % GR], v32[:, n, x % NH], pt[:, x % (2 * GR), n],
                                        start=n == 0, stop=n == NB - 1)
                if piece == GR - 1:
                    ins.then_inc(m["pv_done"], 1)

            def turn(v, z):
                pe.wait_ge(m["os_done"], tile(v, z) + 1)
                for g in range(GR):
                    ins = pe.transpose(op[z % 2][:, g], os_[:, g], ident[:])
                ins.then_inc(m["ot_done"], 1)

            for v in bodies(pe, lambda b: hold(pe, r.passed, m["v_ready"], b + 1)):
                for s in range(STREAM + GR + LAG):
                    if s < STREAM:
                        scores(v, s)
                    if LAG <= s < STREAM + LAG:
                        transposes(v, s - LAG)
                    if s >= GR + LAG:
                        weigh(v, (s - GR - LAG) // GR, (s - GR - LAG) % GR)
                    if NH < s < STREAM and s % NH == 10:
                        turn(v, s // NH - 1)
                turn(v, NT - 1)


def stage_mid0(nc, d):
    SK = 77
    GR = 4
    with ExitStack() as ctx:
        r = Room(nc, ctx, "mid0")
        ident = r.sb("ident", [P, P])
        wo, wq, wk, wv = [r.sb(n, [P, KD, D]) for n in ("wo", "wq", "wk", "wv")]
        wx = r.sb("wx", [P, GR, D])
        bo, bx = r.sb("bo", [P, D]), r.sb("bx", [P, D])
        bq, bk, bks = r.sb("bq", [P, KD]), r.sb("bk", [P, KD]), r.sb("bks", [P, KD])
        bv = r.sb("bv", [SK, D])
        hm = r.sb("hm", [P, NH // 2])
        cx, cxt = r.sb("cx", [SK, D]), r.sb("cxt", [P, KD, SK])
        kt = r.sb("kt", [P, KD, SK])
        kbd = r.sb("kbd", [P, KD, NH // 2, SK])
        v32 = r.sb("v32", [SK, NH, 32])
        mski, mskf = r.sb("mski", [P, SK], mybir.dt.int32), r.sb("mskf", [P, SK])
        fb = r.sb("fb", [P, SK])
        a, x = r.sb("a", [P, 2, D]), r.sb("x", [P, 2, D])
        at = r.sb("at", [P, 2, D])
        x1 = r.sb("x1", [P, 2, D])
        st, mv = r.sb("st", [P, 2, 6]), r.sb("mv", [P, 2, 2])
        var, rstd, half, eps = [r.sb(n, [P, 2]) for n in ("var", "rstd", "half", "eps")]
        xn, xt, qt = r.sb("xn", [P, 2, D]), r.sb("xt", [P, 2, D]), r.sb("qt", [P, 2, D])
        pr = r.sb("pr", [P, 2, NH, SK])
        mx, sm = r.sb("mx", [P, 2, NH]), r.sb("sm", [P, 2, NH])
        pt = r.sb("pt", [SK, NH, P])
        ot = r.sb("ot", [P, 2, GR, P])
        x2 = r.sb("x2", [P, 2, D])
        ps = [r.ps(f"ps{z}", [P, 2, D]) for z in range(2)]
        sc = r.ps("sc", [P, 4, 512])
        op = r.ps("op", [P, GR, P])
        names = ("w_in consts chain first_chain pchain ctx_in ctx_free ctx_t ctx_c kv_mm kv_done kv_ready kv_used")
        m = {n: r.sem(n) for n in names.split()}
        steps = ("in free at_mm at_c wo_mm wo_c mv rstd xn xt_mm xt_c q_mm q_c sc_mm sub ex pr pt_mm pt_c pv_mm pv_c out_mm x2_done out")
        e = {n: [r.sem(f"{n}{z}") for z in range(2)] for n in steps.split()}
        block = ctx.enter_context(nc.Block())
        LOADS = 17

        def pairs(eng, before, after=None):
            with eng.Fori(0, B - 1) as b:
                before(b)
                with eng.Fori(0, TPB // 2) as ih:
                    yield b * (TPB // 2) + ih, False
                if after:
                    after(b)
            before(B - 1)
            with eng.Fori((B - 1) * (TPB // 2), B * (TPB // 2) - 1) as p:
                yield p, False
            yield B * (TPB // 2) - 1, True

        @block.sync
        def _(sp):
            for dst, src in (
                (ident[:], d["ident"]), (wo[:], rows_in(d["L0_attn_WoT"])), (wq[:], rows_in(d["L0_xattn_Wq_wT"])),
                (wk[:], rows_in(d["L0_xattn_Wkv_wT"][:, 0:D])), (wv[:], rows_in(d["L0_xattn_Wkv_wT"][:, D:2 * D])),
                (bo[:], d["L0_attn_bo"].partition_broadcast(P)), (bx[:], d["L0_xattn_out_b"].partition_broadcast(P)),
                (bq[:], d["L0_xattn_Wq_b_cols"]), (bk[:], d["L0_xattn_Wkv_b_cols"][:, 0:KD]),
                (bv[:], d["L0_xattn_Wkv_b"][D:2 * D].partition_broadcast(SK)), (hm[:], d["head_mask"]),
            ):
                sp.dma_start(dst, src).then_inc(m["w_in"], 16)
            sp.wait_ge(m["consts"], 1)
            wxd = d["L0_xattn_out_wT"].rearrange("(g a e) n -> a e g n", g=GR, e=HD)
            for h in range(GR):
                sp.dma_start(wx[32 * h:32 * h + HD], wxd[h]).then_inc(m["w_in"], 16)

            def load(p):
                for z in range(2):
                    hold(sp, r.passed, e["free"][z], p + 1)
                    sp.dma_start(a[:, z], d["attn"][bass.ds((p * 2 + z) * P, P), :]).then_inc(e["in"][z], 16)
                    sp.dma_start(x[:, z], d["x"][bass.ds((p * 2 + z) * P, P), :]).then_inc(e["in"][z], 16)

            def context(b):
                hold(sp, r.passed, m["ctx_free"], b + 1)
                sp.dma_start(cx[:], d["ctx"][bass.ds(b * SK, SK), :]).then_inc(m["ctx_in"], 16)
                sp.dma_start(mski[:], d["mask_words"][bass.ds(b, 1), :].partition_broadcast(P).rearrange("p a k -> p (a k)")).then_inc(m["ctx_in"], 16)
                sp.dma_start(fb[:], d["fside_BxS2_0"][bass.ds(b, 1), :].partition_broadcast(P).rearrange("p a k -> p (a k)")).then_inc(m["ctx_in"], 16)

            load(0)
            for p, last in pairs(sp, context):
                if not last:
                    load(p + 1)
                for z in range(2):
                    hold(sp, r.passed, e["x2_done"][z], p + 1)
                    sp.dma_start(d["x2"][bass.ds((p * 2 + z) * P, P), :], x2[:, z]).then_inc(e["out"][z], 16)
            for z in range(2):
                sp.wait_ge(e["out"][z], 16 * TILES // 2)

        @block.gpsimd
        def _(pool):
            pool.memset(eps[:], 1e-5)
            pool.memset(half[:], -0.5)
            pool.memset(v32[:], 0.0)
            pool.memset(wx[:], 0.0).then_inc(m["consts"], 1)
            pool.wait_ge(m["consts"], 1)

            def root(p):
                for z in range(2):
                    pool.wait_ge(e["mv"][z], p + 1)
                    pool.tensor_tensor(var[:, z:z + 1], mv[:, z, 1:2], eps[:, z:z + 1], ALU.add).then_inc(m["pchain"], 1)
                    pool.wait_ge(m["pchain"], p * 2 + z + 1)
                    pool.tensor_tensor(rstd[:, z:z + 1], var[:, z:z + 1], half[:, z:z + 1], ALU.pow).then_inc(e["rstd"][z], 1)

            root(0)
            for p, last in pairs(pool, lambda b: None):
                if not last:
                    root(p + 1)

        @block.vector
        def _(dve):
            dve.wait_ge(m["w_in"], 16 * 15)
            dve.tensor_scalar(bks[:], bk[:], HD ** -0.5, None, ALU.mult).then_inc(m["consts"], 1)
            dve.sem_inc(m["ctx_free"], 1)
            for z in range(2):
                dve.sem_inc(e["free"][z], 1)

            def context(b):
                dve.wait_ge(m["kv_done"], KD * b + KD)
                dve.wait_ge(m["ctx_in"], 48 * b + 48)
                for c in range(KD):
                    dve.tensor_tensor(kbd[:, c], kt[:, c:c + 1].to_broadcast([P, NH // 2, SK]),
                                      hm[:].rearrange("p (h o) -> p h o", o=1).to_broadcast([P, NH // 2, SK]), ALU.mult)
                dve.tensor_tensor(v32[:, :, 0:HD], ps[0][0:SK, 1].rearrange("k (h e) -> k h e", e=HD),
                                  bv[:].rearrange("k (h e) -> k h e", e=HD), ALU.add)
                dve.tensor_scalar(mskf[:], mski[:], 1.0, None, ALU.min).then_inc(m["kv_used"], 1)
                dve.wait_ge(m["kv_used"], 3 * b + 1)
                dve.tensor_scalar(mskf[:], mskf[:], 1.0, 1e30, ALU.subtract, ALU.mult).then_inc(m["kv_used"], 1)
                dve.wait_ge(m["kv_used"], 3 * b + 2)
                dve.tensor_tensor(fb[:], fb[:], mskf[:], ALU.add).then_inc(m["kv_used"], 1)
                hold(dve, r.passed, m["kv_used"], 3 * b + 3)
                dve.sem_inc(m["kv_ready"], 1)

            def first(p):
                link = Link(dve, m["first_chain"], 2 * 3, p)
                for z in range(2):
                    dve.wait_ge(e["in"][z], 32 * p + 32)
                    dve.wait_ge(e["wo_mm"][z], p + 1)
                    link(dve.tensor_tensor(x1[:, z], x[:, z], ps[z][:, 1], ALU.add))
                    dve.sem_inc(e["free"][z], 1)
                    link(dve.tensor_tensor(x1[:, z], x1[:, z], bo[:], ALU.add))
                    link.alone(dve.bn_stats(st[:, z], x1[:, z]), r.passed)
                    dve.bn_aggr(mv[:, z], st[:, z]).then_inc(e["mv"][z], 1)
                link.done()

            def norm(p):
                for z in range(2):
                    dve.wait_ge(e["rstd"][z], p + 1)
                    dve.tensor_scalar(xn[:, z], x1[:, z], mv[:, z, 0:1], rstd[:, z:z + 1], ALU.subtract, ALU.mult).then_inc(e["xn"][z], 1)

            def weights(link, p, z):
                dve.wait_ge(e["ex"][z], 2 * p + 2)
                link(dve.reduce_sum(sm[:, z], pr[:, z], AX.X))
                link(dve.reciprocal(sm[:, z], sm[:, z]))
                dve.tensor_tensor(pr[:, z], pr[:, z], sm[:, z].rearrange("p (h o) -> p h o", o=1).to_broadcast([P, NH, SK]),
                                  ALU.mult).then_inc(e["pr"][z], 1)

            first(0)
            norm(0)
            for p, last in pairs(dve, context, lambda b: dve.sem_inc(m["ctx_free"], 1)):
                link = Link(dve, m["chain"], 2 * 6, p)
                for z in range(2):
                    s4 = pr[:, z].rearrange("p (g h) k -> p g h k", g=GR)
                    dve.wait_ge(e["sc_mm"][z], p + 1)
                    link(dve.tensor_tensor(s4, sc[:, :, 0:GR * SK].rearrange("p g (h k) -> p g h k", k=SK),
                                           fb[:].rearrange("p (o q k) -> p o q k", o=1, q=1).to_broadcast([P, GR, GR, SK]), ALU.add))
                    dve.sem_inc(e["sub"][z], 1)
                    link(dve.reduce_max(mx[:, z], pr[:, z], AX.X))
                    link(dve.tensor_tensor(pr[:, z], pr[:, z], mx[:, z].rearrange("p (h o) -> p h o", o=1).to_broadcast([P, NH, SK]), ALU.subtract))
                    dve.sem_inc(e["ex"][z], 1)
                for z in range(2):
                    dve.wait_ge(e["out"][z], 16 * p)
                    link(dve.tensor_tensor(x2[:, z], x1[:, z], bx[:], ALU.add))
                weights(link, p, 0)
                if not last:
                    first(p + 1)
                weights(link, p, 1)
                if not last:
                    norm(p + 1)
                for z in range(2):
                    dve.wait_ge(e["out_mm"][z], p + 1)
                    dve.tensor_tensor(x2[:, z], x2[:, z], ps[z][:, 0], ALU.add).then_inc(e["x2_done"][z], 1)
                link.done()

        @block.scalar
        def _(act):
            act.wait_ge(m["w_in"], 16 * 15)
            act.wait_ge(m["consts"], 2)

            def context(b):
                act.wait_ge(m["ctx_t"], b + 1)
                act.activation(cxt[:], ps[0][:, 0, 0:KD * SK].rearrange("p (c k) -> p c k", c=KD), ACT.Copy).then_inc(m["ctx_c"], 1)
                act.wait_ge(m["kv_mm"], b + 1)
                for c in range(KD):
                    act.activation(kt[:, c], ps[0][:, 0, c * SK:(c + 1) * SK], ACT.Identity, bias=bks[:, c:c + 1],
                                   scale=HD ** -0.5).then_inc(m["kv_done"], 1)

            def out_copy(p):
                for z in range(2):
                    act.wait_ge(e["at_mm"][z], p + 1)
                    act.activation(at[:, z], ps[z][:, 0], ACT.Copy).then_inc(e["at_c"][z], 1)

            def query_copy(p):
                for z in range(2):
                    act.wait_ge(e["xt_mm"][z], p + 1)
                    act.activation(xt[:, z], ps[z][:, 0], ACT.Copy).then_inc(e["xt_c"][z], 1)
                for z in range(2):
                    act.wait_ge(e["q_mm"][z], p + 1)
                    for c in range(KD):
                        ins = act.activation(qt[:, z, c * P:(c + 1) * P], ps[z][:, 1, c * P:(c + 1) * P], ACT.Identity, bias=bq[:, c:c + 1])
                    ins.then_inc(e["q_c"][z], 1)

            def weights_copy(p, z):
                act.wait_ge(e["pt_mm"][z], p + 1)
                for g in range(GR):
                    ins = act.activation(pt[:, g * GR:(g + 1) * GR], sc[0:SK, g].rearrange("k (h n) -> k h n", h=GR), ACT.Copy)
                ins.then_inc(e["pt_c"][z], 1)

            def sums_copy(p, z):
                act.wait_ge(e["pv_mm"][z], p + 1)
                act.activation(ot[:, z], op[:], ACT.Copy).then_inc(e["pv_c"][z], 1)

            out_copy(0)
            query_copy(0)
            for p, last in pairs(act, context):
                if not last:
                    out_copy(p + 1)
                for z in range(2):
                    act.wait_ge(e["ex"][z], 2 * p + 1)
                    act.activation(pr[:, z], pr[:, z], ACT.Exp).then_inc(e["ex"][z], 1)
                weights_copy(p, 0)
                sums_copy(p, 0)
                weights_copy(p, 1)
                if not last:
                    query_copy(p + 1)
                sums_copy(p, 1)

        @block.tensor
        def _(pe):
            pe.wait_ge(m["w_in"], 16 * 15)

            def context(b):
                pe.wait_ge(m["ctx_in"], 48 * b + 48)
                pe.wait_ge(e["q_c"][0], b * (TPB // 2) + 1)
                pe.wait_ge(e["x2_done"][0], b * (TPB // 2))
                for c in range(KD):
                    ins = pe.transpose(ps[0][:, 0, c * SK:(c + 1) * SK], cx[:, c * P:(c + 1) * P], ident[0:SK, 0:SK])
                ins.then_inc(m["ctx_t"], 1)
                pe.wait_ge(m["ctx_c"], b + 1)
                for c in range(KD):
                    for k in range(KD):
                        pe.matmul(ps[0][:, 0, c * SK:(c + 1) * SK], wk[:, k, c * P:(c + 1) * P], cxt[:, k], start=k == 0, stop=k == KD - 1)
                for k in range(KD):
                    ins = pe.matmul(ps[0][0:SK, 1], cxt[:, k], wv[:, k], start=k == 0, stop=k == KD - 1)
                ins.then_inc(m["kv_mm"], 1)
                hold(pe, r.passed, m["kv_ready"], b + 1)

            def turn_rows(p):
                for z in range(2):
                    pe.wait_ge(e["in"][z], 32 * p + 32)
                    for c in range(KD):
                        ins = pe.transpose(ps[z][:, 0, c * P:(c + 1) * P], a[:, z, c * P:(c + 1) * P], ident[:])
                    ins.then_inc(e["at_mm"][z], 1)

            def out_projection(p):
                for z in range(2):
                    pe.wait_ge(e["at_c"][z], p + 1)
                    for k in range(KD):
                        ins = pe.matmul(ps[z][:, 1], at[:, z, k * P:(k + 1) * P], wo[:, k], start=k == 0, stop=k == KD - 1)
                    ins.then_inc(e["wo_mm"][z], 1)

            def queries(p):
                for z in range(2):
                    pe.wait_ge(e["xn"][z], p + 1)
                    for c in range(KD):
                        ins = pe.transpose(ps[z][:, 0, c * P:(c + 1) * P], xn[:, z, c * P:(c + 1) * P], ident[:])
                    ins.then_inc(e["xt_mm"][z], 1)
                for z in range(2):
                    pe.wait_ge(e["xt_c"][z], p + 1)
                    for c in range(KD):
                        for k in range(KD):
                            ins = pe.matmul(ps[z][:, 1, c * P:(c + 1) * P], wq[:, k, c * P:(c + 1) * P], xt[:, z, k * P:(k + 1) * P],
                                            start=k == 0, stop=k == KD - 1)
                    ins.then_inc(e["q_mm"][z], 1)

            def weigh(p, z):
                pe.wait_ge(e["pt_c"][z], p + 1)
                if z:
                    pe.wait_ge(e["pv_c"][0], p + 1)
                for g in range(GR):
                    for h4 in range(GR):
                        h = g * GR + h4
                        ins = pe.matmul(op[32 * h4:32 * h4 + 32, g], v32[:, h], pt[:, h], start=True, stop=True)
                ins.then_inc(e["pv_mm"][z], 1)

            def turn(p, z):
                pe.wait_ge(e["pr"][z], p + 1)
                if z:
                    pe.wait_ge(e["pt_c"][0], p + 1)
                for h in range(NH):
                    ins = pe.transpose(sc[0:SK, h // GR, (h % GR) * P:(h % GR + 1) * P], pr[:, z, h], ident[:])
                ins.then_inc(e["pt_mm"][z], 1)

            def projection(p, z):
                pe.wait_ge(e["pv_c"][z], p + 1)
                for g in range(GR):
                    ins = pe.matmul(ps[z][:, 0], ot[:, z, g], wx[:, g], start=g == 0, stop=g == GR - 1)
                ins.then_inc(e["out_mm"][z], 1)

            turn_rows(0)
            out_projection(0)
            queries(0)
            for p, last in pairs(pe, context):
                for z in range(2):
                    pe.wait_ge(e["q_c"][z], p + 1)
                    if z:
                        pe.wait_ge(e["sub"][0], p + 1)
                    else:
                        pe.wait_ge(e["pt_c"][1], p)
                    for g in range(GR):
                        c, h = g // 2, g % 2
                        ins = pe.matmul(sc[:, g, 0:GR * SK], qt[:, z, c * P:(c + 1) * P], kbd[:, c, h * GR:(h + 1) * GR], start=True, stop=True)
                    ins.then_inc(e["sc_mm"][z], 1)
                    if z == 0 and not last:
                        for y in range(2):
                            pe.wait_ge(e["q_c"][y], p + 1)
                            pe.wait_ge(e["x2_done"][y], p)
                        turn_rows(p + 1)
                if not last:
                    out_projection(p + 1)
                pe.wait_ge(e["sub"][1], p + 1)
                turn(p, 0)
                weigh(p, 0)
                turn(p, 1)
                if not last:
                    queries(p + 1)
                if not last:
                    for z in range(2):
                        pe.wait_ge(e["q_c"][z], p + 2)
                projection(p, 0)
                weigh(p, 1)
                projection(p, 1)


def stage_ffn0(nc, d):
    INNER = 1024
    KI = INNER // P
    ROUND = 12582912.0
    with ExitStack() as ctx:
        r = Room(nc, ctx, "ffn0")
        identb = r.sb("identb", [P, P], BF16)
        ident = r.sb("ident", [P, P])
        wf = [r.sb(f"wf{n}", [P, 2 * INNER]) for n in range(3)]
        wt = [r.sb(f"wt{n}", [P, 2 * INNER], BF16) for n in range(3)]
        ones = r.sb("ones", [P, P])
        wsum, wscale, winv = r.sb("wsum", [P, 3]), r.sb("wscale", [P, 3]), r.sb("winv", [P, 3])
        x = r.sb("x", [P, 2, D])
        st, mv = r.sb("st", [P, 2, 6]), r.sb("mv", [P, 2, 2])
        var, rstd, half, eps = [r.sb(n, [P, 2]) for n in ("var", "rstd", "half", "eps")]
        xn = r.sb("xn", [P, 2, D])
        xq, xqt = r.sb("xq", [P, 2, D], BF16), r.sb("xqt", [P, 2, KD, P], BF16)
        am, asc, ainv = r.sb("am", [P, 2, 2]), r.sb("asc", [P, 2, 2]), r.sb("ainv", [P, 2, 2])
        so = r.sb("so", [P, 2, 3])
        hg, hh = r.sb("hg", [P, 2, INNER]), r.sb("hh", [P, 2, INNER])
        hq, hqt = r.sb("hq", [P, 2, INNER], BF16), r.sb("hqt", [P, 2, KI, P], BF16)
        x3, xk = r.sb("x3", [P, 2, D]), r.sb("xk", [P, 2, D])
        sn = r.sb("sn", [P, 2, 2])
        pg, pu = r.ps("pg", [P, 2, 512]), r.ps("pu", [P, 2, 512])
        tp = [r.ps(f"tp{z}", [P, KI, P], BF16) for z in range(2)]
        po = [r.ps(f"po{z}", [P, D]) for z in range(2)]
        m = {n: r.sem(n) for n in "w_in consts wsum_done wtot_done w_ready chain first_chain pchain".split()}
        steps = "in free kept mv rstd xq xt_mm xt_c gu_mm g_c so_done h_done hq ht_mm ht_c out_mm x3_done out"
        e = {n: [r.sem(f"{n}{z}") for z in range(2)] for n in steps.split()}
        block = ctx.enter_context(nc.Block())
        PAIRS = TILES // 2

        def pairs(eng):
            with eng.Fori(0, PAIRS - 1) as p:
                yield p, False
            yield PAIRS - 1, True

        @block.sync
        def _(sp):
            sp.dma_start(ident[:], d["ident"]).then_inc(m["w_in"], 16)
            for n, w in enumerate(("L0_ffn_w_gateT", "L0_ffn_w_upT", "L0_ffn_w_downT")):
                c = D // P if n < 2 else KI
                sp.dma_start(wf[n][:].rearrange("p (c n) -> p c n", c=c), rows_in(d[w])).then_inc(m["w_in"], 16)

            def load(p):
                for z in range(2):
                    hold(sp, r.passed, e["free"][z], p + 1)
                    hold(sp, r.passed, e["kept"][z], p)
                    sp.dma_start(x[:, z], d["x2"][bass.ds((p * 2 + z) * P, P), :]).then_inc(e["in"][z], 16)

            load(0)
            for p, last in pairs(sp):
                if not last:
                    load(p + 1)
                for z in range(2):
                    hold(sp, r.passed, e["x3_done"][z], p + 1)
                    sp.dma_start(d["x3"][bass.ds((p * 2 + z) * P, P), :], x3[:, z]).then_inc(e["out"][z], 16)
            for z in range(2):
                sp.wait_ge(e["out"][z], 16 * PAIRS)

        @block.gpsimd
        def _(pool):
            pool.memset(eps[:], 1e-5)
            pool.memset(ones[:], 1.0)
            pool.memset(half[:], -0.5).then_inc(m["consts"], 1)
            pool.wait_ge(m["consts"], 1)

            def first(p):
                for z in range(2):
                    pool.wait_ge(e["mv"][z], p + 1)
                    pool.tensor_tensor(var[:, z:z + 1], mv[:, z, 1:2], eps[:, z:z + 1], ALU.add).then_inc(m["pchain"], 1)
                    pool.wait_ge(m["pchain"], p * 2 + z + 1)
                    pool.tensor_tensor(rstd[:, z:z + 1], var[:, z:z + 1], half[:, z:z + 1], ALU.pow).then_inc(e["rstd"][z], 1)

            first(0)
            for p, last in pairs(pool):
                for z in range(2):
                    hold(pool, r.passed, e["in"][z], 16 * p + 16)
                    hold(pool, r.passed, e["x3_done"][z], p)
                    pool.tensor_copy(xk[:, z], x[:, z]).then_inc(e["kept"][z], 1)
                if not last:
                    first(p + 1)

        @block.vector
        def _(dve):
            link = Link(dve, m["w_ready"], 0)
            dve.wait_ge(m["w_in"], 64)
            link(dve.tensor_copy(identb[:], ident[:]))
            dve.wait_ge(m["wtot_done"], 1)
            link(dve.tensor_scalar(wscale[:], po[0][:, 0:3], 1.0 / (D * INNER), 1e-5, ALU.mult, ALU.max))
            link(dve.reciprocal(wscale[:], wscale[:]))
            link(dve.reciprocal(winv[:], wscale[:]))
            for n in range(3):
                link(dve.tensor_scalar(wf[n][:], wf[n][:], wscale[:, n:n + 1], ROUND, ALU.mult, ALU.add))
                link(dve.tensor_scalar(wf[n][:], wf[n][:], ROUND, 1.0, ALU.subtract, ALU.min))
                link(dve.tensor_scalar(wt[n][:], wf[n][:], -1.0, None, ALU.max))
            prepared = link.n
            assert prepared == 13
            for z in range(2):
                dve.sem_inc(e["free"][z], 1)

            def quantise(link, q, f, z, k):
                link(dve.tensor_reduce(am[:, z, k:k + 1], f, AX.X, ALU.max, apply_absolute_value=True))
                link(dve.tensor_scalar(am[:, z, k:k + 1], am[:, z, k:k + 1], 1e-5, None, ALU.max))
                link(dve.reciprocal(asc[:, z, k:k + 1], am[:, z, k:k + 1]))
                link(dve.tensor_scalar(asc[:, z, k:k + 1], asc[:, z, k:k + 1], 127.0, None, ALU.mult))
                link(dve.reciprocal(ainv[:, z, k:k + 1], asc[:, z, k:k + 1]))
                link(dve.tensor_scalar(f, f, asc[:, z, k:k + 1], ROUND, ALU.mult, ALU.add))
                link(dve.tensor_scalar(q, f, ROUND, 127.0, ALU.subtract, ALU.min))
                link(dve.tensor_scalar(q, q, -128.0, None, ALU.max))

            def first(p):
                link = Link(dve, m["first_chain"], 2 * (1 + 9 + 1), p)
                for z in range(2):
                    dve.wait_ge(e["in"][z], 16 * p + 16)
                    link.alone(dve.bn_stats(st[:, z], x[:, z]), r.passed)
                    dve.bn_aggr(mv[:, z], st[:, z]).then_inc(e["mv"][z], 1)
                for z in range(2):
                    dve.wait_ge(e["rstd"][z], p + 1)
                    link(dve.tensor_scalar(xn[:, z], x[:, z], mv[:, z, 0:1], rstd[:, z:z + 1], ALU.subtract, ALU.mult))
                    dve.sem_inc(e["free"][z], 1)
                    quantise(link, xq[:, z], xn[:, z], z, 0)
                    link(dve.tensor_scalar(sn[:, z], winv[:, 0:2], ainv[:, z, 0:1], None, ALU.mult))
                    dve.sem_inc(e["xq"][z], 1)
                link.done()

            first(0)
            for p, last in pairs(dve):
                link = Link(dve, m["chain"], 2 * (9 + 1) + 1, p)
                for z in range(2):
                    ins = dve.tensor_copy(so[:, z, 0:2], sn[:, z])
                link(ins)
                for z in range(2):
                    dve.sem_inc(e["so_done"][z], 1)
                for z in range(2):
                    dve.wait_ge(e["g_c"][z], p + 1)
                    link(dve.scalar_tensor_tensor(hh[:, z].rearrange("p (c n) -> p c n", c=2), pu[:], so[:, z, 1:2],
                                                  hg[:, z].rearrange("p (c n) -> p c n", c=2), ALU.mult, ALU.mult))
                    dve.sem_inc(e["h_done"][z], 1)
                    quantise(link, hq[:, z], hh[:, z], z, 1)
                    dve.sem_inc(e["hq"][z], 1)
                    if z == 0 and not last:
                        first(p + 1)
                for z in range(2):
                    link(dve.tensor_tensor(so[:, z, 2:3], winv[:, 2:3], ainv[:, z, 1:2], ALU.mult))
                    dve.wait_ge(e["out"][z], 16 * p)
                    dve.wait_ge(e["kept"][z], p + 1)
                    dve.wait_ge(e["out_mm"][z], p + 1)
                    dve.scalar_tensor_tensor(x3[:, z], po[z][:], so[:, z, 2:3], xk[:, z], ALU.mult, ALU.add).then_inc(e["x3_done"][z], 1)
                link.done()

        @block.scalar
        def _(act):
            act.wait_ge(m["w_in"], 64)
            for n in range(3):
                ins = act.activation((hh, hg, hq)[n][:].rearrange("p z n -> p (z n)"), wf[n][:], ACT.Abs, accum_out=wsum[:, n:n + 1])
            ins.then_inc(m["wsum_done"], 1)

            def first(p):
                for z in range(2):
                    act.wait_ge(e["xt_mm"][z], p + 1)
                    act.activation(xqt[:, z], tp[z][:, 0:KD], ACT.Copy).then_inc(e["xt_c"][z], 1)

            first(0)
            for p, last in pairs(act):
                for z in range(2):
                    act.wait_ge(e["so_done"][z], p + 1)
                    act.wait_ge(e["gu_mm"][z], p + 1)
                    act.activation(hg[:, z].rearrange("p (c n) -> p c n", c=2), pg[:], ACT.Silu, scale=so[:, z, 0:1]).then_inc(e["g_c"][z], 1)
                for z in range(2):
                    act.wait_ge(e["ht_mm"][z], p + 1)
                    act.activation(hqt[:, z], tp[z][:], ACT.Copy).then_inc(e["ht_c"][z], 1)
                if not last:
                    first(p + 1)

        @block.tensor
        def _(pe):
            pe.wait_ge(m["consts"], 1)
            pe.wait_ge(m["wsum_done"], 1)
            pe.matmul(po[0][:, 0:3], ones[:], wsum[:], start=True, stop=True).then_inc(m["wtot_done"], 1)
            pe.wait_ge(m["w_ready"], 13)
            wg, wu = [wt[n][:].rearrange("p (c n) -> p c n", c=KD) for n in range(2)]
            wd = wt[2][:].rearrange("p (c n) -> p c n", c=KI)

            def first(p):
                for z in range(2):
                    pe.wait_ge(e["xq"][z], p + 1)
                    pe.wait_ge(e["ht_c"][z], p)
                    for c in range(KD):
                        ins = pe.transpose(tp[z][:, c], xq[:, z, c * P:(c + 1) * P], identb[:])
                    ins.then_inc(e["xt_mm"][z], 1)

            first(0)
            for p, last in pairs(pe):
                for z in range(2):
                    pe.wait_ge(e["xt_c"][z], p + 1)
                    pe.wait_ge(e["h_done"][1 - z], p + z)
                    for w, acc in ((wg, pg), (wu, pu)):
                        for n in range(2):
                            for k in range(KD):
                                ins = pe.matmul(acc[:, n], xqt[:, z, k], w[:, k, n * 512:(n + 1) * 512], start=k == 0, stop=k == KD - 1)
                    ins.then_inc(e["gu_mm"][z], 1)
                for z in range(2):
                    pe.wait_ge(e["hq"][z], p + 1)
                    for c in range(KI):
                        ins = pe.transpose(tp[z][:, c], hq[:, z, c * P:(c + 1) * P], identb[:])
                    ins.then_inc(e["ht_mm"][z], 1)
                for z in range(2):
                    pe.wait_ge(e["ht_c"][z], p + 1)
                    pe.wait_ge(e["x3_done"][z], p)
                    for k in range(KI):
                        ins = pe.matmul(po[z][:], hqt[:, z, k], wd[:, k], start=k == 0, stop=k == KI - 1)
                    ins.then_inc(e["out_mm"][z], 1)
                if not last:
                    first(p + 1)


GH = 8
DK = 128
GD = GH * DK


def stage_gdn_in(nc, d):
    NC = 3 * GD // 512
    with ExitStack() as ctx:
        r = Room(nc, ctx, "gin")
        ident = r.sb("ident", [P, P])
        w = r.sb("w", [P, KD, 3 * GD])
        wab = r.sb("wab", [P, KD, 2 * GH])
        x = r.sb("x", [P, 2, D])
        st, mv = r.sb("st", [P, 2, 6]), r.sb("mv", [P, 2, 2])
        va, rstd = r.sb("va", [P, 2, 2]), r.sb("rstd", [P, 2, 2])
        half = r.sb("half", [P, 2 * GH])
        ssq, junk = r.sb("ssq", [P, 2]), r.sb("junk", [P, 2, D])
        xn, xt = r.sb("xn", [P, 2, D]), r.sb("xt", [P, 2, KD, P])
        qkv = r.sb("qkv", [P, 2, 3 * GD])
        sq = r.sb("sq", [P, 2, 2 * GD])
        nq, rq = r.sb("nq", [P, 2, 2 * GH]), r.sb("rq", [P, 2, 2 * GH])
        ab = r.sb("ab", [P, 2, 2 * GH])
        tp = [r.ps(f"tp{z}", [P, KD, P]) for z in range(2)]
        pw = [r.ps(f"pw{n}", [P, 512]) for n in range(4)]
        pab = [r.ps(f"pab{z}", [P, 2 * GH]) for z in range(2)]
        m = {n: r.sem(n) for n in "w_in consts chain unit_chain pw_done pw_c0 pw_c1 pw_c2 pw_c3".split()}
        steps = "in free va rstd sq va2 rstd2 xn xt_mm xt_c ab_mm ab_done qk_sq nq rq qkv_done out"
        e = {n: [r.sem(f"{n}{z}") for z in range(2)] for n in steps.split()}
        block = ctx.enter_context(nc.Block())
        PAIRS = TILES // 2
        PER = 2 * NC // 4

        def pairs(eng):
            with eng.Fori(0, PAIRS - 1) as p:
                yield p, False
            yield PAIRS - 1, True

        @block.sync
        def _(sp):
            for dst, src in ((ident[:], d["ident"]), (w[:, :, 0:GD], rows_in(d["L1_attn_Wq"])),
                             (w[:, :, GD:2 * GD], rows_in(d["L1_attn_Wk"])), (w[:, :, 2 * GD:], rows_in(d["L1_attn_Wv"])),
                             (wab[:, :, 0:GH], rows_in(d["L1_attn_Wa"])), (wab[:, :, GH:], rows_in(d["L1_attn_Wb"]))):
                sp.dma_start(dst, src).then_inc(m["w_in"], 16)

            def load(p):
                for z in range(2):
                    hold(sp, r.passed, e["free"][z], p + 1)
                    sp.dma_start(x[:, z], d["x3"][bass.ds((p * 2 + z) * P, P), :]).then_inc(e["in"][z], 16)

            load(0)
            for p, last in pairs(sp):
                if not last:
                    load(p + 1)
                for z in range(2):
                    for k in (z * NC + NC - 2, z * NC + NC - 1):
                        hold(sp, r.passed, m[f"pw_c{k % 4}"], p * PER + k // 4 + 1)
                    hold(sp, r.passed, e["qkv_done"][z], p + 1)
                    sp.dma_start(d["qkv"][bass.ds((p * 2 + z) * P, P), :], qkv[:, z]).then_inc(e["out"][z], 16)
                    sp.dma_start(d["ab"][bass.ds((p * 2 + z) * P, P), :], ab[:, z]).then_inc(e["out"][z], 16)
            for z in range(2):
                sp.wait_ge(e["out"][z], 32 * PAIRS)

        @block.gpsimd
        def _(pool):
            pool.memset(half[:], -0.5).then_inc(m["consts"], 1)
            pool.wait_ge(m["consts"], 1)

            def first(p):
                for z in range(2):
                    pool.wait_ge(e["va"][z], p + 1)
                    pool.tensor_tensor(rstd[:, z, 0:1], va[:, z, 0:1], half[:, 0:1], ALU.pow).then_inc(e["rstd"][z], 1)
                for z in range(2):
                    pool.wait_ge(e["va2"][z], p + 1)
                    pool.tensor_tensor(rstd[:, z, 1:2], va[:, z, 1:2], half[:, 0:1], ALU.pow).then_inc(e["rstd2"][z], 1)

            first(0)
            for p, last in pairs(pool):
                for z in range(2):
                    pool.wait_ge(e["nq"][z], p + 1)
                    pool.tensor_tensor(rq[:, z], nq[:, z], half[:], ALU.pow).then_inc(e["rq"][z], 1)
                    if z == 0 and not last:
                        first(p + 1)

        @block.vector
        def _(dve):
            for z in range(2):
                dve.sem_inc(e["free"][z], 1)

            def first(p):
                link = Link(dve, m["chain"], 2 * 3, p)
                for z in range(2):
                    dve.wait_ge(e["in"][z], 16 * p + 16)
                    link.alone(dve.bn_stats(st[:, z], x[:, z]), r.passed)
                    link(dve.bn_aggr(mv[:, z], st[:, z]))
                    dve.tensor_scalar(va[:, z, 0:1], mv[:, z, 1:2], 1e-5, None, ALU.add).then_inc(e["va"][z], 1)
                for z in range(2):
                    dve.wait_ge(e["rstd"][z], p + 1)
                    dve.wait_ge(e["xt_mm"][z], p)
                    link(dve.tensor_scalar(xn[:, z], x[:, z], mv[:, z, 0:1], rstd[:, z, 0:1], ALU.subtract, ALU.mult))
                    dve.sem_inc(e["free"][z], 1)
                    dve.sem_inc(e["sq"][z], 1)
                for z in range(2):
                    dve.wait_ge(e["sq"][z], 2 * p + 2)
                    dve.tensor_scalar(va[:, z, 1:2], ssq[:, z:z + 1], 1.0 / D, 1e-6, ALU.mult, ALU.add).then_inc(e["va2"][z], 1)
                for z in range(2):
                    dve.wait_ge(e["rstd2"][z], p + 1)
                    dve.tensor_scalar(xn[:, z], xn[:, z], rstd[:, z, 1:2], None, ALU.mult).then_inc(e["xn"][z], 1)
                link.done()

            first(0)
            for p, last in pairs(dve):
                link = Link(dve, m["unit_chain"], 2 * 2, p)
                for z in range(2):
                    dve.wait_ge(e["ab_mm"][z], p + 1)
                    dve.wait_ge(e["out"][z], 32 * p)
                    dve.tensor_copy(ab[:, z], pab[z][:]).then_inc(e["ab_done"][z], 1)
                    dve.wait_ge(e["qk_sq"][z], p + 1)
                    link(dve.reduce_sum(nq[:, z], sq[:, z].rearrange("p (h e) -> p h e", e=DK), AX.X))
                    dve.tensor_scalar(nq[:, z], nq[:, z], 1e-6, None, ALU.add).then_inc(e["nq"][z], 1)
                    if z == 0 and not last:
                        first(p + 1)
                    dve.wait_ge(e["rq"][z], p + 1)
                    link(dve.tensor_scalar(rq[:, z, 0:GH], rq[:, z, 0:GH], DK ** -0.5, None, ALU.mult))
                    v = qkv[:, z, 0:2 * GD].rearrange("p (h e) -> p h e", e=DK)
                    dve.tensor_tensor(v, v, rq[:, z].rearrange("p (h o) -> p h o", o=1).to_broadcast([P, 2 * GH, DK]),
                                      ALU.mult).then_inc(e["qkv_done"][z], 1)
                link.done()

        @block.scalar
        def _(act):

            def square(p):
                for z in range(2):
                    act.wait_ge(e["sq"][z], 2 * p + 1)
                    act.activation(junk[:, z], xn[:, z], ACT.Square, accum_out=ssq[:, z:z + 1]).then_inc(e["sq"][z], 1)

            def copy(p, z):
                act.wait_ge(e["xt_mm"][z], p + 1)
                act.activation(xt[:, z], tp[z][:], ACT.Copy).then_inc(e["xt_c"][z], 1)

            square(0)
            for z in range(2):
                copy(0, z)
            for p, last in pairs(act):
                for z in range(2):
                    act.wait_ge(e["out"][z], 32 * p)
                    for n in range(NC):
                        k = z * NC + n
                        act.wait_ge(m["pw_done"], p * 2 * NC + k + 1)
                        act.activation(qkv[:, z, n * 512:(n + 1) * 512], pw[k % 4][:], ACT.Silu).then_inc(m[f"pw_c{k % 4}"], 1)
                        if n == 3:
                            act.wait_ge(m[f"pw_c{k % 4}"], p * PER + k // 4 + 1)
                            act.activation(sq[:, z], qkv[:, z, 0:2 * GD], ACT.Square).then_inc(e["qk_sq"][z], 1)
                        if z and n == 3 and not last:
                            copy(p + 1, 0)
                    if not last:
                        square(p + 1) if z == 0 else copy(p + 1, 1)

        @block.tensor
        def _(pe):
            pe.wait_ge(m["w_in"], 96)

            def transposes(p, z):
                pe.wait_ge(e["xn"][z], p + 1)
                for c in range(KD):
                    ins = pe.transpose(tp[z][:, c], xn[:, z, c * P:(c + 1) * P], ident[:])
                ins.then_inc(e["xt_mm"][z], 1)

            for z in range(2):
                transposes(0, z)
            for p, last in pairs(pe):
                for z in range(2):
                    pe.wait_ge(e["xt_c"][z], p + 1)
                    pe.wait_ge(e["ab_done"][z], p)
                    for k in range(KD):
                        ins = pe.matmul(pab[z][:], xt[:, z, k], wab[:, k], start=k == 0, stop=k == KD - 1)
                    ins.then_inc(e["ab_mm"][z], 1)
                    for n in range(NC):
                        u = z * NC + n
                        if u < 4:
                            pe.wait_ge(m[f"pw_c{u % 4}"], p * PER)
                        else:
                            pe.wait_ge(m[f"pw_c{u % 4}"], p * PER + u // 4)
                        for k in range(KD):
                            ins = pe.matmul(pw[u % 4][:], xt[:, z, k], w[:, k, n * 512:(n + 1) * 512], start=k == 0, stop=k == KD - 1)
                        ins.then_inc(m["pw_done"], 1)
                        if z and n in (3, NC - 1) and not last:
                            transposes(p + 1, n // 4)




def stage_gdn_core(nc, d):
    HG = 4
    NG = GH // HG
    LV = 6
    C = P
    USES = 22
    (KQ0, KQ1, A_T, KQ3, KQ2, GAMMA, ABC0, ABC1, GK, _5, _6, _7, KS0, KS1, QS0, QS1, W0, W1, O0, O1, DS0, DS1) = range(USES)
    TURNS = ((0, KQ0), (1, KQ1), (3, KQ3), (2, KQ2))
    with ExitStack() as ctx:
        r = Room(nc, ctx, "core")
        ident = r.sb("ident", [P, P])
        i4 = r.sb("i4", [P, HG, C])
        lvl = r.sb("lvl", [P, LV, C])
        m0t = r.sb("m0t", [P, C])
        amask, eye8, ones8 = r.sb("amask", [GH, GH, C]), r.sb("eye8", [GH, GH]), r.sb("ones8", [GH, P])
        alog, dtb = r.sb("alog", [P, GH]), r.sb("dtb", [P, GH])
        ab = r.sb("ab", [P, TILES, 2 * GH])
        al_all, be_all = r.sb("al_all", [P, TILES, GH]), r.sb("be_all", [P, TILES, GH])
        t1, t2, t3 = [r.sb(f"t{n}", [P, TILES, GH]) for n in range(3)]
        rows = r.sb("rows", [P, 2, 3, GH, DK])
        al, be = r.sb("al", [P, 2, GH]), r.sb("be", [P, 2, GH])
        at_, gt, gx = r.sb("aT", [GH, C]), r.sb("gT", [GH, C]), r.sb("gX", [GH, GH])
        ax = r.sb("aX", [GH, GH, C])
        zero8 = r.sb("zero8", [GH, C])
        ga, ng, gc = r.sb("ga", [P, GH]), r.sb("ng", [P, GH]), r.sb("gc", [P, GH])
        dt = r.sb("DT", [P, GH, C])
        db = r.sb("DB", [P, GH, C])
        kp = r.sb("KP", [P, GH, DK])
        kqt = r.sb("KQT", [P, GH, 2, C])
        att = r.sb("At", [P, GH, C])
        attn = r.sb("attn", [P, GH, C])
        bt = r.sb("Bt", [P, GH, C])
        tm, um, xm = r.sb("Tm", [P, GH, C]), r.sb("Um", [P, GH, C]), r.sb("Xm", [P, GH, C])
        rr, dl, o1 = r.sb("R", [P, GH, DK]), r.sb("delta", [P, GH, DK]), r.sb("o1", [P, GH, DK])
        st = r.sb("S", [P, GH, DK])
        o = r.sb("o", [P, 2, GH, DK])
        mb = [r.ps(f"m{n}", [P, HG, C]) for n in range(2)]
        px, pt, pu = [[r.ps(f"p{a}{g}", [P, HG, C]) for g in range(NG)] for a in "xtu"]
        m = {n: r.sem(n) for n in ("w_in ab_in prep consts chain ab_done a_c g_done ax_done g_c dt_done db_done kq_c at_done kp_done "
                                   "r_done o1_c delta_c s_zero s_done full0 full1 free0 free1").split()}
        e = {n: [r.sem(f"{n}{g}") for g in range(2)] for n in "in rows_free o_done out bt u1 x_mm x_c t_mm t_c u_mm u_c".split()}
        block = ctx.enter_context(nc.Block())
        gs = lambda g: slice(g * HG, (g + 1) * HG)
        bc = lambda v, n, w: v.rearrange("p (h o) -> p h o", o=1).to_broadcast([P, n, w])
        lv4 = lambda v: v.rearrange("p (o n) -> p o n", o=1).to_broadcast([P, HG, C])

        def wait_full(eng, i, k):
            eng.wait_ge(m[f"full{k % 2}"], i * (USES // 2) + k // 2 + 1)

        def wait_free(eng, i, k):
            eng.wait_ge(m[f"free{k % 2}"], i * (USES // 2) + k // 2 + 1)

        def chunks(eng, before=None):
            with eng.Fori(0, B) as b:
                if before:
                    before(b)
                with eng.Fori(0, TPB // 2) as ih:
                    for z in range(2):
                        yield b, z, b * TPB + ih * 2 + z, b * (TPB // 2) + ih

        @block.sync
        def _(sp):
            for dst, src in ((ident[:], d["ident"]), (i4[:], d["eye4"]), (lvl[:], d["levels"]), (m0t[:], d["level0t"]),
                             (amask[:], d["alpha_mask"]), (eye8[:], d["eye8"]),
                             (alog[:], d["L1_attn_A_log"].partition_broadcast(P)), (dtb[:], d["L1_attn_dt_bias"].partition_broadcast(P)),
                             (ab[:], d["ab"].rearrange("(i p) c -> p i c", p=P))):
                sp.dma_start(dst, src).then_inc(m["w_in"], 16)
            for b, z, i, pair in chunks(sp):
                hold(sp, r.passed, e["rows_free"][z], pair + 1)
                sp.dma_start(rows[:, z].rearrange("p a h e -> p (a h e)"), d["qkv"][bass.ds(i * P, P), :]).then_inc(e["in"][z], 16)

        @block.gpsimd
        def _(pool):
            pool.memset(zero8[:], 0.0)
            pool.memset(ones8[:], 1.0).then_inc(m["consts"], 1)
            for b, z, i, pair in chunks(pool):
                for g in range(NG):
                    hold(pool, r.passed, m["dt_done"], i * NG + g + 1)
                    pool.tensor_tensor(db[:, gs(g)], dt[:, gs(g)], bc(be[:, z, gs(g)], HG, C), ALU.mult).then_inc(m["db_done"], 1)
                for g in range(NG):
                    hold(pool, r.passed, m["at_done"], i * 4 + 2 * g + 2)
                    pool.affine_select(out=bt[:, gs(g)], in_=att[:, gs(g)], compare_op=ALU.not_equal, fill=1.0, base=0,
                                       pattern=[[0, HG], [-1, C]], channel_multiplier=1).then_inc(e["bt"][g], 1)
                hold(pool, r.passed, e["in"][z], 16 * pair + 16)
                pool.tensor_tensor(kp[:], rows[:, z, 1], dt[:, :, C - 1:C].to_broadcast([P, GH, DK]), ALU.mult).then_inc(m["kp_done"], 1)

        @block.scalar
        def _(act):
            act.wait_ge(m["prep"], 1)
            act.activation(t1[:], ab[:, :, 0:GH], ACT.Abs).then_inc(m["prep"], 1)
            act.wait_ge(m["prep"], 2)
            act.activation(t2[:], t1[:], ACT.Exp, scale=-1.0).then_inc(m["prep"], 1)
            act.activation(be_all[:], ab[:, :, GH:], ACT.Exp, scale=-1.0)
            act.activation(alog[:], alog[:], ACT.Exp).then_inc(m["prep"], 1)
            act.wait_ge(m["prep"], PREP - 1)
            act.activation(al_all[:], t1[:], ACT.Exp, scale=-1.0).then_inc(m["prep"], 1)
            for b, z, i, pair in chunks(act):
                for n, (k, turn) in enumerate(TURNS):
                    if n == 2:
                        wait_full(act, i, A_T)
                        act.activation(at_[:], mb[0][0:GH, 0], ACT.Copy).then_inc(m["a_c"], 1)
                        act.wait_ge(m["a_c"], i + 1)
                        act.sem_inc(m["free0"], 1)
                    wait_full(act, i, turn)
                    act.activation(kqt[:, 2 * k:2 * k + 2].rearrange("p h a t -> p (h a) t"), mb[k % 2][:], ACT.Copy).then_inc(m["kq_c"], 1)
                    act.wait_ge(m["kq_c"], i * 4 + n + 1)
                    act.sem_inc(m[f"free{k % 2}"], 1)
                wait_full(act, i, GAMMA)
                act.activation(ga[:], mb[1][:, 0, 0:GH], ACT.Copy)
                act.activation(ng[:], mb[1][:, 0, 0:GH], ACT.Copy, scale=-1.0)
                act.activation(gc[:], mb[1][:, 0, GH:2 * GH], ACT.Copy).then_inc(m["g_c"], 1)
                act.wait_ge(m["g_c"], i + 1)
                act.sem_inc(m["free1"], 1)
                for g in range(NG):
                    act.wait_ge(e["t_mm"][g], i * LV + 1)
                    act.activation(tm[:, gs(g)], pt[g][:], ACT.Copy).then_inc(e["t_c"][g], 1)
                for g in range(NG):
                    wait_full(act, i, QS0 + g)
                    for h in range(HG):
                        ins = act.activation(o1[:, g * HG + h], mb[g][:, h], ACT.Copy, scale=ga[:, g * HG + h:g * HG + h + 1])
                    ins.then_inc(m["o1_c"], 1)
                    act.wait_ge(m["o1_c"], i * NG + g + 1)
                    act.sem_inc(m[f"free{g}"], 1)
                for l in range(1, LV + 1):
                    if l < LV:
                        for g in range(NG):
                            act.wait_ge(e["t_mm"][g], i * LV + l + 1)
                            act.activation(tm[:, gs(g)], pt[g][:], ACT.Copy).then_inc(e["t_c"][g], 1)
                    for g in range(NG):
                        act.wait_ge(e["u_mm"][g], i * LV + l)
                        act.activation(um[:, gs(g)], pu[g][:], ACT.Copy).then_inc(e["u_c"][g], 1)
                for g in range(NG):
                    wait_full(act, i, W0 + g)
                    for h in range(HG):
                        ins = act.activation(dl[:, g * HG + h], mb[g][:, h], ACT.Copy, scale=be[:, z, g * HG + h:g * HG + h + 1])
                    ins.then_inc(m["delta_c"], 1)
                    act.wait_ge(m["delta_c"], i * NG + g + 1)
                    act.sem_inc(m[f"free{g}"], 1)
                for g in range(NG):
                    act.wait_ge(e["o_done"][z], pair * NG + g + 1)
                act.dma_start(d["o"][bass.ds(i * P, P), :], o[:, z].rearrange("p h e -> p (h e)")).then_inc(e["out"][z], 16)
            for z in range(2):
                act.wait_ge(e["out"][z], 16 * TILES // 2)

        @block.vector
        def _(dve):
            link = Link(dve, m["prep"], 0)
            b8 = lambda v: v.rearrange("p (o h) -> p o h", o=1).to_broadcast([P, TILES, GH])
            dve.wait_ge(m["w_in"], 16 * 9)
            link(dve.tensor_tensor(ab[:, :, 0:GH], ab[:, :, 0:GH], b8(dtb[:]), ALU.add))
            link.n += 3
            dve.wait_ge(m["prep"], 4)
            link(dve.tensor_scalar(t1[:], t2[:], 2.0, None, ALU.add))
            link(dve.reciprocal(t1[:], t1[:]))
            link(dve.tensor_tensor(t2[:], t2[:], t1[:], ALU.mult))
            link(dve.tensor_tensor(t3[:], t2[:], t2[:], ALU.mult))
            link(dve.tensor_scalar(t1[:], t3[:], 1.0 / 19, None, ALU.mult))
            for odd in (17, 15, 13, 11, 9, 7, 5, 3):
                link(dve.scalar_tensor_tensor(t1[:], t1[:], 1.0 / odd, t3[:], ALU.add, ALU.mult))
            link(dve.scalar_tensor_tensor(t1[:], t1[:], 1.0, t2[:], ALU.add, ALU.mult))
            link(dve.tensor_scalar(t1[:], t1[:], 2.0, None, ALU.mult))
            link(dve.tensor_scalar(ab[:, :, 0:GH], ab[:, :, 0:GH], 0.0, None, ALU.max))
            link(dve.tensor_tensor(t1[:], t1[:], ab[:, :, 0:GH], ALU.add))
            link(dve.tensor_tensor(t1[:], t1[:], b8(alog[:]), ALU.mult))
            link(dve.tensor_scalar(be_all[:], be_all[:], 1.0, None, ALU.add))
            link(dve.reciprocal(be_all[:], be_all[:]))
            assert link.n == PREP - 1
            dve.wait_ge(m["prep"], PREP)
            dve.wait_ge(m["consts"], 1)
            for z in range(2):
                dve.sem_inc(e["rows_free"][z], 1)
                dve.sem_inc(m[f"free{z}"], 1)

            def clear_state(b):
                dve.memset(st[:], 0.0).then_inc(m["s_zero"], 1)

            for b, z, i, pair in chunks(dve, clear_state):
                link = Link(dve, m["chain"], CHAIN, i)
                dve.tensor_copy(al[:, z], al_all[:, bass.ds(i, 1)].rearrange("p o h -> p (o h)"))
                link(dve.tensor_copy(be[:, z], be_all[:, bass.ds(i, 1)].rearrange("p o h -> p (o h)")))
                dve.sem_inc(m["ab_done"], 1)
                dve.wait_ge(m["a_c"], i + 1)
                link(dve.tensor_tensor_scan(gt[:], at_[:], zero8[:], 1.0, ALU.mult, ALU.add))
                dve.tensor_scalar(gx[:], eye8[:], gt[:, C - 1:C], None, ALU.mult).then_inc(m["g_done"], 1)
                dve.tensor_tensor(ax[:], at_[:].rearrange("p (o t) -> p o t", o=1).to_broadcast([GH, GH, C]), amask[:], ALU.mult
                                  ).then_inc(m["ax_done"], 1)
                for g in range(NG):
                    wait_full(dve, i, ABC0 + g)
                    link(dve.tensor_tensor_scan(dt[:, gs(g)].rearrange("p h t -> p (h t)"), mb[g][:].rearrange("p h t -> p (h t)"),
                                                i4[:].rearrange("p h t -> p (h t)"), 0.0, ALU.mult, ALU.add))
                    dve.sem_inc(m["dt_done"], 1)
                    dve.sem_inc(m[f"free{g}"], 1)
                for k in range(4):
                    wait_full(dve, i, GK + k)
                    dve.wait_ge(m["db_done"], i * NG + k // 2 + 1)
                    v = mb[k % 2][:].rearrange("p (h a) t -> p h a t", a=2)
                    dve.tensor_tensor(att[:, 2 * k:2 * k + 2], v[:, :, 0], db[:, 2 * k:2 * k + 2], ALU.mult).then_inc(m["at_done"], 1)
                    link(dve.tensor_tensor(attn[:, 2 * k:2 * k + 2], v[:, :, 1], dt[:, 2 * k:2 * k + 2], ALU.mult))
                    dve.sem_inc(m[f"free{k % 2}"], 1)
                for g in range(NG):
                    link(dve.tensor_tensor(xm[:, gs(g)], att[:, gs(g)], lv4(m0t[:]), ALU.mult))
                    dve.tensor_tensor(um[:, gs(g)], xm[:, gs(g)], i4[:], ALU.add).then_inc(e["u1"][g], 1)
                for g in range(NG):
                    wait_full(dve, i, KS0 + g)
                    for h in range(HG):
                        hh = g * HG + h
                        ins = dve.scalar_tensor_tensor(rr[:, hh], mb[g][:, h], ng[:, hh:hh + 1], rows[:, z, 2, hh], ALU.mult, ALU.add)
                    link(ins)
                    dve.sem_inc(m["r_done"], 1)
                    dve.sem_inc(m[f"free{g}"], 1)
                for l in range(1, LV + 1):
                    for g in range(NG):
                        dve.wait_ge(e["x_mm"][g], i * LV + l)
                        dve.tensor_tensor(xm[:, gs(g)], px[g][:], lv4(lvl[:, l - 1]), ALU.mult).then_inc(e["x_c"][g], 1)
                dve.wait_ge(e["out"][z], 16 * pair)
                for g in range(NG):
                    wait_full(dve, i, O0 + g)
                    dve.wait_ge(m["o1_c"], i * NG + g + 1)
                    link(dve.tensor_tensor(o[:, z, gs(g)], mb[g][:], o1[:, gs(g)], ALU.add))
                    dve.sem_inc(e["o_done"][z], 1)
                    dve.sem_inc(m[f"free{g}"], 1)
                for g in range(NG):
                    wait_full(dve, i, DS0 + g)
                    for h in range(HG):
                        hh = g * HG + h
                        ins = dve.scalar_tensor_tensor(st[:, hh], st[:, hh], gc[:, hh:hh + 1], mb[g][:, h], ALU.mult, ALU.add)
                    link(ins)
                    dve.sem_inc(m["s_done"], 1)
                    dve.sem_inc(m[f"free{g}"], 1)
                dve.sem_inc(e["rows_free"][z], 1)
                link.done()

        @block.tensor
        def _(pe):
            pe.wait_ge(m["w_in"], 16 * 9)
            pe.wait_ge(m["consts"], 1)

            def use(i, k):
                wait_free(pe, i, k)
                return mb[k % 2]

            def wrote(ins, k):
                ins.then_inc(m[f"full{k % 2}"], 1)

            for b, z, i, pair in chunks(pe):
                pe.wait_ge(e["in"][z], 16 * pair + 16)
                for n, (k, turn) in enumerate(TURNS):
                    if n == 2:
                        pe.wait_ge(m["ab_done"], i + 1)
                        q = use(i, A_T)
                        wrote(pe.transpose(q[0:GH, 0], al[:, z], ident[:]), A_T)
                    q = use(i, turn)
                    for h in range(2):
                        pe.transpose(q[:, 2 * h], rows[:, z, 1, 2 * k + h], ident[:])
                        ins = pe.transpose(q[:, 2 * h + 1], rows[:, z, 0, 2 * k + h], ident[:])
                    wrote(ins, turn)
                q = use(i, GAMMA)
                hold(pe, r.passed, m["g_done"], i + 1)
                pe.transpose(q[:, 0, 0:GH], gt[:], ident[0:GH, 0:GH])
                wrote(pe.matmul(q[:, 0, GH:2 * GH], ones8[:], gx[:], start=True, stop=True), GAMMA)
                pe.wait_ge(m["ax_done"], i + 1)
                for g in range(NG):
                    q = use(i, ABC0 + g)
                    wrote(pe.matmul(q[:], ones8[:], ax[:, gs(g)], start=True, stop=True), ABC0 + g)
                for k in range(4):
                    pe.wait_ge(m["kq_c"], i * 4 + (k + 1 if k < 2 else 4))
                    q = use(i, GK + k)
                    for h in range(2):
                        ins = pe.matmul(q[:, 2 * h:2 * h + 2], kqt[:, 2 * k + h, 0], kqt[:, 2 * k + h], start=True, stop=True)
                    wrote(ins, GK + k)
                pe.wait_ge(m["s_zero"], b + 1)
                pe.wait_ge(m["s_done"], i * NG)
                def with_state(a, first):
                    for g in range(NG):
                        q = use(i, first + g)
                        for h in range(HG):
                            ins = pe.matmul(q[:, h], kqt[:, g * HG + h, a], st[:, g * HG + h], start=True, stop=True)
                        wrote(ins, first + g)

                with_state(0, KS0)
                for g in range(NG):
                    pe.wait_ge(e["u1"][g], i + 1)
                    for h in range(HG):
                        ins = pe.transpose(pt[g][:, h], um[:, g * HG + h], ident[:])
                    ins.then_inc(e["t_mm"][g], 1)
                with_state(1, QS0)
                for l in range(1, LV + 1):
                    for g in range(NG):
                        if l == 1:
                            pe.wait_ge(e["bt"][g], i + 1)
                        pe.wait_ge(e["t_c"][g], i * LV + l)
                        for h in range(HG):
                            hh = g * HG + h
                            ins = pe.matmul(px[g][:, h], bt[:, hh], tm[:, hh], start=True, stop=True)
                        ins.then_inc(e["x_mm"][g], 1)
                    for g in range(NG):
                        pe.wait_ge(e["x_c"][g], i * LV + l)
                        if l > 1:
                            pe.wait_ge(e["u_c"][g], i * LV + l - 1)
                        if l < LV:
                            for h in range(HG):
                                hh = g * HG + h
                                ins = pe.matmul(pt[g][:, h], um[:, hh], xm[:, hh], start=True, stop=True)
                            ins.then_inc(e["t_mm"][g], 1)
                        else:
                            for h in range(HG):
                                hh = g * HG + h
                                ins = pe.matmul(pu[g][:, h], xm[:, hh], um[:, hh], start=True, stop=True)
                            ins.then_inc(e["u_mm"][g], 1)
                    if l < LV:
                        for g in range(NG):
                            pe.wait_ge(e["t_c"][g], i * LV + l + 1)
                            for h in range(HG):
                                ins = pe.transpose(pu[g][:, h], tm[:, g * HG + h], ident[:])
                            ins.then_inc(e["u_mm"][g], 1)
                for g in range(NG):
                    pe.wait_ge(e["u_c"][g], i * LV + LV)
                    pe.wait_ge(m["r_done"], i * NG + g + 1)
                    q = use(i, W0 + g)
                    for h in range(HG):
                        hh = g * HG + h
                        ins = pe.matmul(q[:, h], um[:, hh], rr[:, hh], start=True, stop=True)
                    wrote(ins, W0 + g)
                pe.wait_ge(m["kp_done"], i + 1)
                for left, first in ((attn, O0), (kp, DS0)):
                    for g in range(NG):
                        pe.wait_ge(m["delta_c"], i * NG + g + 1)
                        q = use(i, first + g)
                        for h in range(HG):
                            hh = g * HG + h
                            ins = pe.matmul(q[:, h], left[:, hh], dl[:, hh], start=True, stop=True)
                        wrote(ins, first + g)


PREP = 25
CHAIN = 2 + 2 + 4 + 2 + 2 + 2 + 2


def stage_gdn_out(nc, d):
    FF = 1024
    KF = FF // P
    PAIRS = TILES // 2
    with ExitStack() as ctx:
        r = Room(nc, ctx, "gout")
        ident = r.sb("ident", [P, P])
        wg, wfc = r.sb("wg", [P, KD, GD]), r.sb("wfc", [P, KD, FF])
        wo, wp = r.sb("wo", [P, GD // P, D]), r.sb("wp", [P, KF, D])
        onw = r.sb("onw", [P, DK])
        x, o = r.sb("x", [P, 2, D]), r.sb("o", [P, 2, GD])
        st, mv = r.sb("st", [P, 2, 6]), r.sb("mv", [P, 2, 2])
        va, rstd = r.sb("va", [P, 2, 3]), r.sb("rstd", [P, 2, 3])
        half = r.sb("half", [P, GH])
        ssq, junk = r.sb("ssq", [P, 2, 2]), r.sb("junk", [P, 2, 2, D])
        xk, xin, xn, xt, xm, mn, mt, base, y = [r.sb(n, [P, 2, D]) for n in "xk xin xn xt xm mn mt base y".split()]
        sq = r.sb("sq", [P, 2, GD])
        no, ro = r.sb("no", [P, 2, GH]), r.sb("ro", [P, 2, GH])
        gate, ff = r.sb("gate", [P, 2, GD]), r.sb("ff", [P, 2, FF])
        ot, ft = r.sb("ot", [P, 2, GD]), r.sb("ft", [P, 2, FF])
        ps = [r.ps(f"ps{z}", [P, 2, 512]) for z in range(2)]
        ta, tb = [[r.ps(f"t{n}{z}", [P, 2, D]) for z in range(2)] for n in "ab"]
        m = {n: r.sem(n) for n in "w_in consts chain a_chain".split()}
        steps = ("x_in o_in x_free x_kept o_free va rstd sq1 sq1_c va2 rstd2 xn xt_mm xt_c g_mm g_c osq no ro on gated ot_mm ot_c wo_mm "
                 "xm base_done sq2 va3 rstd3 mn mt_mm mt_c f_mm f_c f_sq ft_mm ft_c p_mm y_done out")
        e = {n: [r.sem(f"{n}{z}") for z in range(2)] for n in steps.split()}
        block = ctx.enter_context(nc.Block())
        wide = lambda v: v.rearrange("p (a n) -> p a n", a=2)

        def pairs(eng):
            with eng.Fori(0, PAIRS - 1) as p:
                yield p, False
            yield PAIRS - 1, True

        @block.sync
        def _(sp):
            for dst, src in ((ident[:], d["ident"]), (wg[:], rows_in(d["L1_attn_Wg"])), (wfc[:], rows_in(d["L1_attn_W_fc"])),
                             (wo[:], rows_in(d["L1_attn_Wo"])), (wp[:], rows_in(d["L1_attn_W_proj"])),
                             (onw[:], d["L1_attn_o_norm_w"].partition_broadcast(P))):
                sp.dma_start(dst, src).then_inc(m["w_in"], 16)

            def load(p):
                for z in range(2):
                    hold(sp, r.passed, e["x_free"][z], 2 * p + 2)
                    sp.dma_start(x[:, z], d["x3"][bass.ds((p * 2 + z) * P, P), :]).then_inc(e["x_in"][z], 16)
                for z in range(2):
                    hold(sp, r.passed, e["o_free"][z], p + 1)
                    sp.dma_start(o[:, z], d["o"][bass.ds((p * 2 + z) * P, P), :]).then_inc(e["o_in"][z], 16)

            load(0)
            for p, last in pairs(sp):
                if not last:
                    load(p + 1)
                for z in range(2):
                    hold(sp, r.passed, e["y_done"][z], p + 1)
                    sp.dma_start(d["x4"][bass.ds((p * 2 + z) * P, P), :], y[:, z]).then_inc(e["out"][z], 16)
            for z in range(2):
                sp.wait_ge(e["out"][z], 16 * PAIRS)

        @block.gpsimd
        def _(pool):
            pool.memset(half[:], -0.5).then_inc(m["consts"], 1)
            pool.wait_ge(m["consts"], 1)

            def root(p, signal, done, k):
                for z in range(2):
                    pool.wait_ge(e[signal][z], p + 1)
                    pool.tensor_tensor(rstd[:, z, k:k + 1], va[:, z, k:k + 1], half[:, 0:1], ALU.pow).then_inc(e[done][z], 1)

            def mixer(p):
                root(p, "va", "rstd", 0)
                for z in range(2):
                    hold(pool, r.passed, e["x_in"][z], 16 * p + 16)
                    pool.tensor_copy(xk[:, z], x[:, z]).then_inc(e["x_kept"][z], 1)
                    hold(pool, r.passed, e["x_kept"][z], p + 1)
                    pool.sem_inc(e["x_free"][z], 1)
                root(p, "va2", "rstd2", 1)
                for z in range(2):
                    pool.wait_ge(e["no"][z], p + 1)
                    pool.tensor_tensor(ro[:, z], no[:, z], half[:], ALU.pow).then_inc(e["ro"][z], 1)
                root(p, "va3", "rstd3", 2)

            mixer(0)
            for p, last in pairs(pool):
                if not last:
                    mixer(p + 1)

        @block.vector
        def _(dve):
            for z in range(2):
                dve.sem_inc(e["x_free"][z], 2)

            def norms(p):
                link = Link(dve, m["a_chain"], 2 * 2, p)
                for z in range(2):
                    dve.wait_ge(e["x_in"][z], 16 * p + 16)
                    link.alone(dve.bn_stats(st[:, z], x[:, z]), r.passed)
                    link(dve.bn_aggr(mv[:, z], st[:, z]))
                    dve.tensor_scalar(va[:, z, 0:1], mv[:, z, 1:2], 1e-5, None, ALU.add).then_inc(e["va"][z], 1)
                for z in range(2):
                    dve.wait_ge(e["rstd"][z], p + 1)
                    dve.tensor_scalar(xin[:, z], x[:, z], mv[:, z, 0:1], rstd[:, z, 0:1], ALU.subtract, ALU.mult).then_inc(e["sq1"][z], 1)
                    dve.wait_ge(e["sq1"][z], p + 1)
                    dve.sem_inc(e["x_free"][z], 1)
                for z in range(2):
                    dve.wait_ge(e["sq1_c"][z], p + 1)
                    dve.tensor_scalar(va[:, z, 1:2], ssq[:, z, 0:1], 1.0 / D, 1e-6, ALU.mult, ALU.add).then_inc(e["va2"][z], 1)
                for z in range(2):
                    dve.wait_ge(e["rstd2"][z], p + 1)
                    dve.tensor_scalar(xn[:, z], xin[:, z], rstd[:, z, 1:2], None, ALU.mult).then_inc(e["xn"][z], 1)
                link.done()

            def heads(p):
                link = Link(dve, m["chain"], 2 * 2, p)
                for z in range(2):
                    dve.wait_ge(e["osq"][z], p + 1)
                    link(dve.reduce_sum(no[:, z], sq[:, z].rearrange("p (h e) -> p h e", e=DK), AX.X))
                    dve.tensor_scalar(no[:, z], no[:, z], 1.0 / DK, 1e-6, ALU.mult, ALU.add).then_inc(e["no"][z], 1)
                for z in range(2):
                    dve.wait_ge(e["ro"][z], p + 1)
                    for h in range(GH):
                        v = o[:, z, h * DK:(h + 1) * DK]
                        ins = dve.scalar_tensor_tensor(v, v, ro[:, z, h:h + 1], onw[:], ALU.mult, ALU.mult)
                    link(ins)
                    dve.wait_ge(e["g_c"][z], p + 1)
                    dve.tensor_tensor(o[:, z], o[:, z], gate[:, z], ALU.mult).then_inc(e["gated"][z], 1)
                link.done()

            def mixed(p):
                for z in range(2):
                    dve.wait_ge(e["wo_mm"][z], p + 1)
                    dve.tensor_tensor(xm[:, z], xin[:, z], ta[z][:, 1], ALU.add).then_inc(e["xm"][z], 1)
                for z in range(2):
                    dve.wait_ge(e["sq2"][z], p + 1)
                    dve.tensor_scalar(va[:, z, 2:3], ssq[:, z, 1:2], 1.0 / D, 1e-6, ALU.mult, ALU.add).then_inc(e["va3"][z], 1)
                for z in range(2):
                    dve.wait_ge(e["x_kept"][z], p + 1)
                    dve.tensor_tensor(base[:, z], xk[:, z], xm[:, z], ALU.add).then_inc(e["base_done"][z], 1)
                for z in range(2):
                    dve.wait_ge(e["rstd3"][z], p + 1)
                    dve.tensor_scalar(mn[:, z], xm[:, z], rstd[:, z, 2:3], None, ALU.mult).then_inc(e["mn"][z], 1)

            norms(0)
            heads(0)
            mixed(0)
            for p, last in pairs(dve):
                if not last:
                    norms(p + 1)
                for z in range(2):
                    dve.wait_ge(e["f_c"][z], p + 1)
                    dve.tensor_tensor(ff[:, z], ff[:, z], ff[:, z], ALU.mult).then_inc(e["f_sq"][z], 1)
                if not last:
                    heads(p + 1)
                for z in range(2):
                    dve.wait_ge(e["out"][z], 16 * p)
                    dve.wait_ge(e["p_mm"][z], p + 1)
                    dve.wait_ge(e["base_done"][z], p + 1)
                    dve.tensor_tensor(y[:, z], base[:, z], tb[z][:, 1], ALU.add).then_inc(e["y_done"][z], 1)
                if not last:
                    mixed(p + 1)

        @block.scalar
        def _(act):
            act.wait_ge(m["w_in"], 96)

            def step(p, signal, done, f):
                for z in range(2):
                    act.wait_ge(e[signal][z], p + 1)
                    f(z).then_inc(e[done][z], 1)

            def square_rows(p):
                step(p, "sq1", "sq1_c", lambda z: act.activation(junk[:, z, 0], xin[:, z], ACT.Square, accum_out=ssq[:, z, 0:1]))

            def square_heads(p):
                for z in range(2):
                    act.wait_ge(e["o_in"][z], 16 * p + 16)
                    act.activation(sq[:, z], o[:, z], ACT.Square).then_inc(e["osq"][z], 1)

            def gates(p):
                step(p, "xt_mm", "xt_c", lambda z: act.activation(xt[:, z], ta[z][:, 0], ACT.Copy))
                step(p, "g_mm", "g_c", lambda z: act.activation(wide(gate[:, z]), ps[z][:], ACT.Silu))

            def mixer_end(p):
                step(p, "ot_mm", "ot_c", lambda z: act.activation(wide(ot[:, z]), ps[z][:], ACT.Copy))

            def square_sum(p):
                step(p, "xm", "sq2", lambda z: act.activation(junk[:, z, 1], xm[:, z], ACT.Square, accum_out=ssq[:, z, 1:2]))

            square_rows(0)
            square_heads(0)
            gates(0)
            mixer_end(0)
            square_sum(0)
            for p, last in pairs(act):
                step(p, "mt_mm", "mt_c", lambda z: act.activation(mt[:, z], tb[z][:, 0], ACT.Copy))
                if not last:
                    square_rows(p + 1)
                step(p, "f_mm", "f_c", lambda z: act.activation(wide(ff[:, z]), ps[z][:], ACT.Relu))
                if not last:
                    square_heads(p + 1)
                    gates(p + 1)
                step(p, "ft_mm", "ft_c", lambda z: act.activation(wide(ft[:, z]), ps[z][:], ACT.Copy))
                if not last:
                    mixer_end(p + 1)
                    square_sum(p + 1)

        @block.tensor
        def _(pe):
            pe.wait_ge(m["w_in"], 96)
            for z in range(2):
                pe.sem_inc(e["o_free"][z], 1)

            def transposes(dst, src, n):
                for c in range(n):
                    ins = pe.transpose(dst[:, c], src[:, c * P:(c + 1) * P], ident[:])
                return ins

            def product(dst, left, w, n):
                chunks = w.shape[1]
                for k in range(chunks):
                    ins = pe.matmul(dst, left[:, k * P:(k + 1) * P], w[:, k, n[0]:n[1]],
                                    start=k == 0, stop=k == chunks - 1)
                return ins

            split = lambda v: v.rearrange("p (c n) -> p c n", n=P)
            blocks = lambda z: ps[z][:].rearrange("p a (h n) -> p (a h) n", n=P)

            def gate_products(p):
                for z in range(2):
                    pe.wait_ge(e["xn"][z], p + 1)
                    transposes(split(ta[z][:, 0]), xn[:, z], KD).then_inc(e["xt_mm"][z], 1)
                for z in range(2):
                    pe.wait_ge(e["xt_c"][z], p + 1)
                    pe.wait_ge(e["f_c"][z], p)
                    for a in range(2):
                        ins = product(ps[z][:, a], xt[:, z], wg, (a * 512, a * 512 + 512))
                    ins.then_inc(e["g_mm"][z], 1)

            def head_transposes(p, z):
                pe.wait_ge(e["gated"][z], p + 1)
                pe.wait_ge(e["ft_c"][z], p)
                transposes(blocks(z), o[:, z], GH).then_inc(e["ot_mm"][z], 1)
                pe.wait_ge(e["ot_mm"][z], p + 1)
                pe.sem_inc(e["o_free"][z], 1)

            def mixer_products(p):
                for z in range(2):
                    pe.wait_ge(e["ot_c"][z], p + 1)
                    product(ta[z][:, 1], ot[:, z], wo, (0, D)).then_inc(e["wo_mm"][z], 1)

            gate_products(0)
            for z in range(2):
                head_transposes(0, z)
            mixer_products(0)
            for p, last in pairs(pe):
                for z in range(2):
                    pe.wait_ge(e["mn"][z], p + 1)
                    pe.wait_ge(e["y_done"][z], p)
                    transposes(split(tb[z][:, 0]), mn[:, z], KD).then_inc(e["mt_mm"][z], 1)
                for z in range(2):
                    pe.wait_ge(e["mt_c"][z], p + 1)
                    for a in range(2):
                        ins = product(ps[z][:, a], mt[:, z], wfc, (a * 512, a * 512 + 512))
                    ins.then_inc(e["f_mm"][z], 1)
                if not last:
                    gate_products(p + 1)
                for z in range(2):
                    pe.wait_ge(e["f_sq"][z], p + 1)
                    if not last:
                        pe.wait_ge(e["g_c"][z], p + 2)
                    transposes(blocks(z), ff[:, z], KF).then_inc(e["ft_mm"][z], 1)
                for z in range(2):
                    if not last:
                        head_transposes(p + 1, z)
                    pe.wait_ge(e["ft_c"][z], p + 1)
                    product(tb[z][:, 1], ft[:, z], wp, (0, D)).then_inc(e["p_mm"][z], 1)
                if not last:
                    mixer_products(p + 1)


def stage_lin(nc, d):
    SK = 77
    NZ = 4
    GROUPS = TILES // NZ
    NKV = D + NH
    STEPS = 14
    with ExitStack() as ctx:
        r = Room(nc, ctx, "lin")
        ident = r.sb("ident", [P, P])
        wq, wk, wv = [r.sb(n, [P, KD, D]) for n in ("wq", "wk", "wv")]
        lg, lb = r.sb("lg", [P, D]), r.sb("lb", [P, D])
        same = r.sb("same", [P, KD, NKV])
        cx, cxt, em = r.sb("cx", [SK, D]), r.sb("cxt", [P, KD, SK]), r.sb("em", [SK, 1])
        cst, cmv, cva, crs = [r.sb(n, s) for n, s in (("cst", [SK, 2, 6]), ("cmv", [SK, 2, 2]), ("cva", [SK, 2]), ("crs", [SK, 2]))]
        kv = r.sb("kv", [SK, 2, D])
        ones = r.sb("ones", [SK, 1])
        kvb = r.sb("kvb", [P, KD, NKV])
        half = r.sb("half", [P, 2])
        x = r.sb("x", [P, NZ, D])
        st, mv = r.sb("st", [P, NZ, 2, 6]), r.sb("mv", [P, NZ, 2, 2])
        va, rs = r.sb("va", [P, NZ, 2]), r.sb("rs", [P, NZ, 2])
        xn, xt, q, qt = [r.sb(n, [P, NZ, D]) for n in ("xn", "xt", "q", "qt")]
        den = r.sb("den", [P, NZ, NH])
        att = r.sb("att", [P, NZ, D])
        tp, mm = [[r.ps(f"{a}{z}", [P, 512]) for z in range(NZ)] for a in ("tp", "mm")]
        m = {n: r.sem(n) for n in "w_in consts chain cx_in cx_free cx".split()}
        steps = "in x_free va rstd xn xt_mm xt_c q_mm va2 rstd2 q_done qt_mm qt_c a_mm att_done out"
        e = {n: [r.sem(f"{n}{z}") for z in range(NZ)] for n in steps.split()}
        block = ctx.enter_context(nc.Block())
        split = lambda v: v.rearrange("p (c n) -> p c n", n=P)

        def groups(eng, before):
            with eng.Fori(0, B) as b:
                before(b)
                with eng.Fori(0, TPB // NZ) as ih:
                    yield b, ih, b * (TPB // NZ) + ih

        @block.sync
        def _(sp):
            for dst, src in (
                (ident[:], d["ident"]), (wq[:], rows_in(d["L1_xattn_wq"])), (wk[:], rows_in(d["L1_xattn_wk"])),
                (wv[:], rows_in(d["L1_xattn_wv"])), (same[:], d["same_head"]),
                (lg[:], d["L1_xattn_ln_gamma"].partition_broadcast(P)), (lb[:], d["L1_xattn_ln_beta"].partition_broadcast(P)),
            ):
                sp.dma_start(dst, src).then_inc(m["w_in"], 16)

            def context(b):
                hold(sp, r.passed, m["cx"], b * STEPS)
                sp.dma_start(cx[:], d["ctx"][bass.ds(b * SK, SK), :]).then_inc(m["cx_in"], 16)
                sp.dma_start(em[:], d["mask_ff"][bass.ds(b * SK, SK), :]).then_inc(m["cx_in"], 16)

            for b, ih, p in groups(sp, context):
                for z in range(NZ):
                    hold(sp, r.passed, e["x_free"][z], p + 1)
                    sp.dma_start(x[:, z], d["x4"][bass.ds((p * NZ + z) * P, P), :]).then_inc(e["in"][z], 16)
                for z in range(NZ):
                    hold(sp, r.passed, e["att_done"][z], p + 1)
                    sp.dma_start(d["latt"][bass.ds(b * NH, NH), bass.ds((ih * NZ + z) * P, P), :].rearrange("h n e -> n h e"),
                                 att[:, z].rearrange("p (h e) -> p h e", e=HD)).then_inc(e["out"][z], 16)
            for z in range(NZ):
                sp.wait_ge(e["out"][z], 16 * GROUPS)

        @block.gpsimd
        def _(pool):
            pool.memset(ones[:], 1.0)
            pool.memset(half[:], -0.5).then_inc(m["consts"], 1)
            pool.wait_ge(m["consts"], 1)

            def context(b):
                pool.wait_ge(m["cx"], b * STEPS + 6)
                pool.tensor_tensor(crs[:], cva[:], half[0:SK], ALU.pow).then_inc(m["cx"], 1)

            for b, ih, p in groups(pool, context):
                for k, (signal, done) in enumerate((("va", "rstd"), ("va2", "rstd2"))):
                    for z in range(NZ):
                        pool.wait_ge(e[signal][z], p + 1)
                        pool.tensor_tensor(rs[:, z, k:k + 1], va[:, z, k:k + 1], half[:, 0:1], ALU.pow).then_inc(e[done][z], 1)

        @block.vector
        def _(dve):
            dve.wait_ge(m["w_in"], 16 * 7)
            for z in range(NZ):
                dve.sem_inc(e["x_free"][z], 1)

            def context(b):
                step = lambda ins: ins.then_inc(m["cx"], 1)
                at_step = lambda k: hold(dve, r.passed, m["cx"], b * STEPS + k)
                two = lambda v: v.rearrange("k (o c) -> k o c", o=1).to_broadcast([SK, 2, D])
                at_step(3)
                for a in range(2):
                    ins = dve.bn_stats(cst[:, a], mm[a][0:SK, 0:D])
                step(ins)
                at_step(4)
                for a in range(2):
                    ins = dve.bn_aggr(cmv[:, a], cst[:, a])
                step(ins)
                at_step(5)
                step(dve.tensor_scalar(cva[:], cmv[:, :, 1], 1e-6, None, ALU.add))
                at_step(7)
                for a in range(2):
                    ins = dve.tensor_scalar(kv[:, a], mm[a][0:SK, 0:D], cmv[:, a, 0:1], crs[:, a:a + 1], ALU.subtract, ALU.mult)
                step(ins)
                at_step(8)
                step(dve.tensor_tensor(kv[:], kv[:], two(lg[0:SK]), ALU.mult))
                at_step(9)
                step(dve.tensor_tensor(kv[:], kv[:], two(lb[0:SK]), ALU.add))
                at_step(10)
                step(dve.tensor_scalar(kv[:, 0], kv[:, 0], 0.0, 1e-6, ALU.max, ALU.add))
                dve.wait_ge(m["cx_in"], 32 * b + 32)
                at_step(11)
                step(dve.tensor_scalar(kv[:], kv[:], em[:], None, ALU.mult))
                at_step(13)
                for c in range(KD):
                    dve.tensor_tensor(kvb[:, c, 0:D], tp[c][:, 0:D], same[:, c, 0:D], ALU.mult)
                    ins = dve.tensor_tensor(kvb[:, c, D:], tp[c][:, D:D + 1].to_broadcast([P, NH]), same[:, c, D:], ALU.mult)
                step(ins)

            def scaled(link, v):
                link(dve.tensor_tensor(v, v, lg[:], ALU.mult))
                link(dve.tensor_tensor(v, v, lb[:], ALU.add))

            for b, ih, p in groups(dve, context):
                link = Link(dve, m["chain"], NZ * (2 + 2 + 3 + 2), p)

                def stats(v, z, k, eps, signal):
                    link.alone(dve.bn_stats(st[:, z, k], v), r.passed)
                    link(dve.bn_aggr(mv[:, z, k], st[:, z, k]))
                    dve.tensor_scalar(va[:, z, k:k + 1], mv[:, z, k, 1:2], eps, None, ALU.add).then_inc(e[signal][z], 1)

                for z in range(NZ):
                    dve.wait_ge(e["in"][z], 16 * p + 16)
                    stats(x[:, z], z, 0, 1e-5, "va")
                for z in range(NZ):
                    dve.wait_ge(e["rstd"][z], p + 1)
                    dve.tensor_scalar(xn[:, z], x[:, z], mv[:, z, 0, 0:1], rs[:, z, 0:1], ALU.subtract, ALU.mult).then_inc(e["xn"][z], 1)
                    dve.wait_ge(e["xn"][z], p + 1)
                    dve.sem_inc(e["x_free"][z], 1)
                for z in range(NZ):
                    hold(dve, r.passed, e["q_mm"][z], p + 1)
                    stats(mm[z][:, 0:D], z, 1, 1e-6, "va2")
                for z in range(NZ):
                    dve.wait_ge(e["rstd2"][z], p + 1)
                    link(dve.tensor_scalar(q[:, z], mm[z][:, 0:D], mv[:, z, 1, 0:1], rs[:, z, 1:2], ALU.subtract, ALU.mult))
                    scaled(link, q[:, z])
                    dve.tensor_scalar(q[:, z], q[:, z], 0.0, 1e-6, ALU.max, ALU.add).then_inc(e["q_done"][z], 1)
                for z in range(NZ):
                    dve.wait_ge(e["a_mm"][z], p + 1)
                    link(dve.tensor_scalar(den[:, z], mm[z][:, D:NKV], 1e-6, None, ALU.add))
                    link(dve.reciprocal(den[:, z], den[:, z]))
                    dve.wait_ge(e["out"][z], 16 * p)
                    dve.tensor_tensor(att[:, z].rearrange("p (h e) -> p h e", e=HD), mm[z][:, 0:D].rearrange("p (h e) -> p h e", e=HD),
                                      den[:, z].rearrange("p (h o) -> p h o", o=1).to_broadcast([P, NH, HD]), ALU.mult
                                      ).then_inc(e["att_done"][z], 1)
                link.done()

        @block.scalar
        def _(act):
            def context(b):
                act.wait_ge(m["cx"], b * STEPS + 1)
                act.activation(cxt[:], tp[0][:, 0:KD * SK].rearrange("p (c k) -> p c k", c=KD), ACT.Copy).then_inc(m["cx"], 1)

            for b, ih, p in groups(act, context):
                for signal, done, dst in (("xt_mm", "xt_c", xt), ("qt_mm", "qt_c", qt)):
                    for z in range(NZ):
                        act.wait_ge(e[signal][z], p + 1)
                        act.activation(dst[:, z], tp[z][:, 0:D], ACT.Copy).then_inc(e[done][z], 1)

        @block.tensor
        def _(pe):
            pe.wait_ge(m["w_in"], 16 * 7)
            pe.wait_ge(m["consts"], 1)

            def context(b):
                step = lambda ins: ins.then_inc(m["cx"], 1)
                pe.wait_ge(m["cx_in"], 32 * b + 32)
                for z in range(NZ):
                    pe.wait_ge(e["att_done"][z], b * (TPB // NZ))
                for c in range(KD):
                    ins = pe.transpose(tp[0][:, c * SK:(c + 1) * SK], cx[:, c * P:(c + 1) * P], ident[0:SK, 0:SK])
                step(ins)
                pe.wait_ge(m["cx"], b * STEPS + 2)
                for a, w in enumerate((wk, wv)):
                    for k in range(KD):
                        ins = pe.matmul(mm[a][0:SK, 0:D], cxt[:, k], w[:, k], start=k == 0, stop=k == KD - 1)
                step(ins)
                pe.wait_ge(m["cx"], b * STEPS + 12)
                for c in range(KD):
                    pe.matmul(tp[c][:, 0:D], kv[:, 0, c * P:(c + 1) * P], kv[:, 1], start=True, stop=True)
                    ins = pe.matmul(tp[c][:, D:D + 1], kv[:, 0, c * P:(c + 1) * P], ones[:], start=True, stop=True)
                step(ins)
                hold(pe, r.passed, m["cx"], b * STEPS + 14)

            def turn(p, signal, src, done):
                for z in range(NZ):
                    pe.wait_ge(e[signal][z], p + 1)
                    for c in range(KD):
                        ins = pe.transpose(tp[z][:, c * P:(c + 1) * P], src[:, z, c * P:(c + 1) * P], ident[:])
                    ins.then_inc(e[done][z], 1)

            def product(p, signal, left, w, n, done):
                for z in range(NZ):
                    pe.wait_ge(e[signal][z], p + 1)
                    for k in range(KD):
                        ins = pe.matmul(mm[z][:, 0:n], left[:, z, k * P:(k + 1) * P], w[:, k], start=k == 0, stop=k == KD - 1)
                    ins.then_inc(e[done][z], 1)

            for b, ih, p in groups(pe, context):
                turn(p, "xn", xn, "xt_mm")
                product(p, "xt_c", xt, wq, D, "q_mm")
                turn(p, "q_done", q, "qt_mm")
                product(p, "qt_c", qt, kvb, NKV, "a_mm")


def stage_lin_out(nc, d):
    NZ = 4
    GROUPS = TILES // NZ
    with ExitStack() as ctx:
        r = Room(nc, ctx, "linout")
        ident = r.sb("ident", [P, P])
        wd = r.sb("wd", [P, KD, D])
        lg, lb, bd = r.sb("lg", [P, D]), r.sb("lb", [P, D]), r.sb("bd", [P, D])
        half = r.sb("half", [P, 2])
        a, at, x, y, src = [r.sb(n, [P, NZ, D]) for n in ("a", "at", "x", "y", "src")]
        st, mv = r.sb("st", [P, NZ, 2, 6]), r.sb("mv", [P, NZ, 2, 2])
        va, rs = r.sb("va", [P, NZ, 2]), r.sb("rs", [P, NZ, 2])
        tp, mm = [[r.ps(f"{n}{z}", [P, KD, P]) for z in range(NZ)] for n in ("tp", "mm")]
        m = {n: r.sem(n) for n in "w_in consts chain".split()}
        steps = "a_in x_in a_free x_free at_mm at_c d_mm va rstd y_done va2 rstd2 src_done out"
        e = {n: [r.sem(f"{n}{z}") for z in range(NZ)] for n in steps.split()}
        block = ctx.enter_context(nc.Block())

        @block.sync
        def _(sp):
            for dst, src_d in (
                (ident[:], d["ident"]), (wd[:], rows_in(d["L1_xattn_dense_w"])),
                (lg[:], d["L1_xattn_ln_gamma"].partition_broadcast(P)), (lb[:], d["L1_xattn_ln_beta"].partition_broadcast(P)),
                (bd[:], d["L1_xattn_dense_b"].partition_broadcast(P)),
            ):
                sp.dma_start(dst, src_d).then_inc(m["w_in"], 16)
            rows = d["latt"].rearrange("h (t m) e -> (h t) (m e)", m=NH)
            with sp.Fori(0, GROUPS) as p:
                for z in range(NZ):
                    hold(sp, r.passed, e["a_free"][z], p + 1)
                    sp.dma_start(a[:, z], rows[bass.ds((p * NZ + z) * P, P), :]).then_inc(e["a_in"][z], 16)
                    hold(sp, r.passed, e["x_free"][z], p + 1)
                    sp.dma_start(x[:, z], d["x4"][bass.ds((p * NZ + z) * P, P), :]).then_inc(e["x_in"][z], 16)
                for z in range(NZ):
                    hold(sp, r.passed, e["src_done"][z], p + 1)
                    sp.dma_start(d["x5"][bass.ds((p * NZ + z) * P, P), :], y[:, z]).then_inc(e["out"][z], 16)
                    sp.dma_start(d["src1"][bass.ds((p * NZ + z) * P, P), :], src[:, z]).then_inc(e["out"][z], 16)
            for z in range(NZ):
                sp.wait_ge(e["out"][z], 32 * GROUPS)

        @block.gpsimd
        def _(pool):
            pool.memset(half[:], -0.5).then_inc(m["consts"], 1)
            pool.wait_ge(m["consts"], 1)
            with pool.Fori(0, GROUPS) as p:
                for k, (signal, done) in enumerate((("va", "rstd"), ("va2", "rstd2"))):
                    for z in range(NZ):
                        pool.wait_ge(e[signal][z], p + 1)
                        pool.tensor_tensor(rs[:, z, k:k + 1], va[:, z, k:k + 1], half[:, 0:1], ALU.pow).then_inc(e[done][z], 1)

        @block.vector
        def _(dve):
            dve.wait_ge(m["w_in"], 16 * 5)
            for z in range(NZ):
                dve.sem_inc(e["x_free"][z], 1)
            with dve.Fori(0, GROUPS) as p:
                link = Link(dve, m["chain"], NZ * (3 + 4 + 2), p)

                def stats(v, z, k, eps, signal):
                    link.alone(dve.bn_stats(st[:, z, k], v), r.passed)
                    link(dve.bn_aggr(mv[:, z, k], st[:, z, k]))
                    dve.tensor_scalar(va[:, z, k:k + 1], mv[:, z, k, 1:2], eps, None, ALU.add).then_inc(e[signal][z], 1)

                for z in range(NZ):
                    dve.wait_ge(e["out"][z], 32 * p)
                    dve.wait_ge(e["d_mm"][z], p + 1)
                    link(dve.tensor_tensor(y[:, z], mm[z][:].rearrange("p c n -> p (c n)"), bd[:], ALU.add))
                    stats(y[:, z], z, 0, 1e-6, "va")
                for z in range(NZ):
                    dve.wait_ge(e["rstd"][z], p + 1)
                    link(dve.tensor_scalar(y[:, z], y[:, z], mv[:, z, 0, 0:1], rs[:, z, 0:1], ALU.subtract, ALU.mult))
                    link(dve.tensor_tensor(y[:, z], y[:, z], lg[:], ALU.mult))
                    link(dve.tensor_tensor(y[:, z], y[:, z], lb[:], ALU.add))
                    dve.wait_ge(e["x_in"][z], 16 * p + 16)
                    link(dve.tensor_tensor(y[:, z], y[:, z], x[:, z], ALU.add))
                    dve.sem_inc(e["x_free"][z], 1)
                    stats(y[:, z], z, 1, 1e-5, "va2")
                for z in range(NZ):
                    dve.wait_ge(e["rstd2"][z], p + 1)
                    dve.tensor_scalar(src[:, z], y[:, z], mv[:, z, 1, 0:1], rs[:, z, 1:2], ALU.subtract, ALU.mult).then_inc(e["src_done"][z], 1)
                link.done()

        @block.scalar
        def _(act):
            with act.Fori(0, GROUPS) as p:
                for z in range(NZ):
                    act.wait_ge(e["at_mm"][z], p + 1)
                    act.activation(at[:, z], tp[z][:].rearrange("p c n -> p (c n)"), ACT.Copy).then_inc(e["at_c"][z], 1)

        @block.tensor
        def _(pe):
            pe.wait_ge(m["w_in"], 16 * 5)
            for z in range(NZ):
                pe.sem_inc(e["a_free"][z], 1)
            with pe.Fori(0, GROUPS) as p:
                for z in range(NZ):
                    pe.wait_ge(e["a_in"][z], 16 * p + 16)
                    for c in range(KD):
                        ins = pe.transpose(tp[z][:, c], a[:, z, c * P:(c + 1) * P], ident[:])
                    ins.then_inc(e["at_mm"][z], 1)
                    pe.wait_ge(e["at_mm"][z], p + 1)
                    pe.sem_inc(e["a_free"][z], 1)
                for z in range(NZ):
                    pe.wait_ge(e["at_c"][z], p + 1)
                    pe.wait_ge(e["va"][z], p)
                    for k in range(KD):
                        ins = pe.matmul(mm[z][:].rearrange("p c n -> p (c n)"), at[:, z, k * P:(k + 1) * P], wd[:, k], start=k == 0, stop=k == KD - 1)
                    ins.then_inc(e["d_mm"][z], 1)


def stage_pre1(nc, d):
    G = 4
    W = G * P
    DC = D // 4
    HALVES = S // W
    GROUPS = B * HALVES
    with ExitStack() as ctx:
        r = Room(nc, ctx, "pre1")
        ident = r.sb("ident", [P, P])
        wq = [r.sb(f"wq{n}", [P, KD, D]) for n in range(2)]
        wc = r.sb("wc", [P, KD, 2 * DC])
        wk = [r.sb(f"wk{n}", [DC, D]) for n in range(2)]
        wv = r.sb("wv", [2 * DC, D])
        cos, sin = r.sb("cos", [P, S]), r.sb("sin", [P, S])
        x = r.sb("x", [P, G, D])
        xt = r.sb("xt", [P, KD, W])
        kvc = r.sb("kvc", [2 * DC, W])
        t1, t2, qf, qr = [r.sb(n, [P, 2, W]) for n in ("t1", "t2", "qf", "qr")]
        parts = r.sb("parts", [P, 2, 3, W], BF16)
        row = r.sb("row", [P, G, D])
        tp = [r.ps(f"tp{n}", [P, KD, P]) for n in range(2)]
        qk = [[r.ps(f"qk{n}_{a}", [P, W]) for a in range(2)] for n in range(2)]
        kvp = r.ps("kvp", [2 * DC, W])
        rowp = r.ps("rowp", [P, D])
        names = ("w_in x_in x_free tp_done xt_done kvc_mm kvc_done qk_done qk_free parts_done "
                 "row_mm row_done chain parts_out0 parts_out1 v_out")
        m = {n: r.sem(n) for n in names.split()}
        block = ctx.enter_context(nc.Block())

        def groups(eng):
            with eng.Fori(0, B) as b:
                for g in range(HALVES):
                    yield b, g, b * HALVES + g

        @block.sync
        def _(sp):
            for dst, src in (
                (ident[:], d["ident"]), (wq[0][:], rows_in(d["L1_ffn_Wq"])), (wq[1][:], rows_in(d["L1_ffn_Wq_swapped"])),
                (wc[:, :, 0:DC], rows_in(d["L1_ffn_Wk_c"])), (wc[:, :, DC:], rows_in(d["L1_ffn_Wv_c"])),
                (wk[0][:], d["L1_ffn_Wk"]), (wk[1][:], d["L1_ffn_Wk_swapped"]), (wv[DC:], d["L1_ffn_Wv"]),
                (cos[:], d["rope_cos"]), (sin[:], d["rope_sin"]),
            ):
                sp.dma_start(dst, src).then_inc(m["w_in"], 16)
            for b, g, i in groups(sp):
                hold(sp, r.passed, m["x_free"], i + 1)
                sp.dma_start(x[:], d["src1"][bass.ds(i * W, W), :].rearrange("(s p) c -> p s c", p=P)).then_inc(m["x_in"], 16)
                for n in range(4):
                    dst = d["q1"] if n < 2 else d["k1"]
                    c = n % 2
                    hold(sp, r.passed, m["parts_done"], i * 4 + n + 1)
                    sp.dma_start(dst[:, bass.ds(b * D + c * P, P), g * W:(g + 1) * W].rearrange("a p t -> p a t"),
                                 parts[:, n % 2]).then_inc(m[f"parts_out{n % 2}"], 16)
                hold(sp, r.passed, m["row_done"], i * G + G)
                for n in range(4):
                    sp.dma_start(d["v1"][bass.ds((b * 4 + n) * S + g * W, W), :].rearrange("(s p) c -> p s c", p=P),
                                 row[:, :, n * D // 4:(n + 1) * D // 4]).then_inc(m["v_out"], 16)
            sp.wait_ge(m["v_out"], 64 * GROUPS)
            for n in range(2):
                sp.wait_ge(m[f"parts_out{n}"], 32 * GROUPS)

        @block.vector
        def _(dve):
            dve.wait_ge(m["w_in"], 16 * 10)
            dve.sem_inc(m["x_free"], 1)
            dve.sem_inc(m["qk_free"], 2)
            for b, g, i in groups(dve):
                link = Link(dve, m["chain"], 4 * 7, i)
                at = slice(g * W, (g + 1) * W)
                for n in range(4):
                    h = n % 2
                    scale = HD ** -0.5 if n < 2 else 1.0
                    dve.wait_ge(m["qk_done"], i * 4 + n + 1)
                    dve.wait_ge(m[f"parts_out{h}"], i * 32 + 16 * (n // 2))
                    link(dve.scalar_tensor_tensor(t1[:, h], qk[h][0][:], scale, cos[:, at], ALU.mult, ALU.mult))
                    link(dve.scalar_tensor_tensor(t2[:, h], qk[h][1][:], scale, sin[:, at], ALU.mult, ALU.mult))
                    dve.sem_inc(m["qk_free"], 1)
                    link(dve.tensor_tensor(qf[:, h], t1[:, h], t2[:, h], ALU.add))
                    link(dve.tensor_copy(parts[:, h, 0], qf[:, h]))
                    link(dve.tensor_tensor(qr[:, h], qf[:, h], parts[:, h, 0], ALU.subtract))
                    link(dve.tensor_copy(parts[:, h, 1], qr[:, h]))
                    link(dve.tensor_tensor(parts[:, h, 2], qr[:, h], parts[:, h, 1], ALU.subtract))
                    dve.sem_inc(m["parts_done"], 1)
                link.done()

        @block.scalar
        def _(act):
            for b, g, i in groups(act):
                act.wait_ge(m["row_mm"], i * G)
                for s in range(G):
                    act.wait_ge(m["tp_done"], i * G + s + 1)
                    act.activation(xt[:, :, s * P:(s + 1) * P], tp[s % 2][:], ACT.Copy).then_inc(m["xt_done"], 1)
                act.wait_ge(m["kvc_mm"], i + 1)
                act.activation(kvc[:], kvp[:], ACT.Copy).then_inc(m["kvc_done"], 1)
                act.wait_ge(m["v_out"], 64 * i)
                for s in range(G):
                    act.wait_ge(m["row_mm"], i * G + s + 1)
                    act.activation(row[:, s], rowp[:], ACT.Copy).then_inc(m["row_done"], 1)

        @block.tensor
        def _(pe):
            pe.wait_ge(m["w_in"], 16 * 10)
            pe.sem_inc(m["xt_done"], 2)
            for b, g, i in groups(pe):
                pe.wait_ge(m["x_in"], 16 * i + 16)
                for s in range(G):
                    pe.wait_ge(m["xt_done"], i * G + s + 1)
                    for c in range(KD):
                        ins = pe.transpose(tp[s % 2][:, c], x[:, s, c * P:(c + 1) * P], ident[:])
                    ins.then_inc(m["tp_done"], 1)
                pe.wait_ge(m["tp_done"], i * G + G)
                pe.sem_inc(m["x_free"], 1)
                pe.wait_ge(m["xt_done"], i * G + G + 2)
                for k in range(KD):
                    ins = pe.matmul(kvp[:], wc[:, k], xt[:, k], start=k == 0, stop=k == KD - 1)
                ins.then_inc(m["kvc_mm"], 1)
                for n in range(4):
                    c = n % 2
                    pe.wait_ge(m["qk_free"], i * 4 + n + 1)
                    if n == 2:
                        pe.wait_ge(m["kvc_done"], i + 1)
                    for a in range(2):
                        if n < 2:
                            for k in range(KD):
                                ins = pe.matmul(qk[c][a][:], wq[a][:, k, c * P:(c + 1) * P], xt[:, k], start=k == 0, stop=k == KD - 1)
                        else:
                            ins = pe.matmul(qk[c][a][:], wk[a][:, c * P:(c + 1) * P], kvc[0:DC], start=True, stop=True)
                    ins.then_inc(m["qk_done"], 1)
                for s in range(G):
                    pe.wait_ge(m["row_done"], i * G + s)
                    pe.matmul(rowp[:], kvc[DC:, s * P:(s + 1) * P], wv[DC:], start=True, stop=True).then_inc(m["row_mm"], 1)


def stage_attn1(nc, d):
    NB = S // P
    GR = 4
    W = 512
    QT = W // P
    GC = GR * HD
    ROWS = SPLIT * HD
    STEPS = B * (NH // GR) * (S // W)
    BODY = 4
    BODIES = STEPS // BODY
    AHEAD = 4
    LAG = 2
    with ExitStack() as ctx:
        r = Room(nc, ctx, "attn1")
        ident = r.sb("ident", [P, P])
        kt = [r.sb(f"kt{n}", [ROWS + 3, GR, S], BF16) for n in range(2)]
        qt = [r.sb(f"qt{n}", [ROWS + 3, GR, W], BF16) for n in range(BODY)]
        vs = r.sb("vs", [P, NB, GC])
        v32 = [r.sb(f"v32_{n}", [P, NB, GR, 32]) for n in range(2)]
        mx = [r.sb(f"mx{n}", [P, GR, QT, 2]) for n in range(2)]
        nm = r.sb("nm", [P, GR * QT])
        nf, nr = r.sb("nf", [GR * QT, P]), r.sb("nr", [GR * QT, P])
        nt = r.sb("nt", [GR * QT, 3, P], BF16)
        pt = r.sb("pt", [P, 4, GR, W])
        os_ = r.sb("os", [P, W])
        rs = r.sb("rs", [P, QT, GR, 1])
        row = r.sb("row", [P, 2, QT, GC])
        mp = [r.ps(f"mp{n}", [P, W]) for n in range(2)]
        st = [r.ps(f"st{n}", [P, 2, W]) for n in range(2)]
        op = r.ps("op", [P, W])
        tb = r.ps("tb", [P, QT, P])
        names = ("id_in vs_in v_ready ones max_mm max_done nm_done nm_mm nt_done nt_out nm_in "
                 "st_mm exp_done pv_mm os_done ot_mm row_done chain schain out0 out1 k_in0 k_in1 q_in0 q_in1 q_in2 q_in3")
        m = {n: r.sem(n) for n in names.split()}
        block = ctx.enter_context(nc.Block())

        def bodies(eng):
            with eng.Fori(0, BODIES - 1) as v:
                yield v, False
            yield BODIES - 1, True

        def maxima(w, n, last):
            w, n = (w + 1, n + AHEAD) if n < NB - AHEAD else (w + 2, n + AHEAD - NB)
            return None if last and w >= BODY else (w, n)

        FIRST = [(0, n) for n in range(NB)] + [(1, n) for n in range(AHEAD)]

        def load_k(sp, v, w):
            u = v * 2 + w // 2
            n = w // 2 % 2
            for slot in range(SPLIT):
                sp.dma_start(kt[n][slot * HD:(slot + 1) * HD], d["k1"][K_PART[slot], bass.ds(u * GC, GC), :]
                             .rearrange("(h e) t -> e h t", e=HD)).then_inc(m[f"k_in{n}"], 16)

        def load_q(sp, v, w):
            u = v * 2 + w // 2
            for slot in range(SPLIT):
                sp.dma_start(qt[w % 4][slot * HD:(slot + 1) * HD], d["q1"][Q_PART[slot], bass.ds(u * GC, GC), (w % 2) * W:(w % 2 + 1) * W]
                             .rearrange("(h e) t -> e h t", e=HD)).then_inc(m[f"q_in{w % 4}"], 16)

        @block.sync
        def _(sp):
            def load_v(v, w):
                sp.dma_start(vs[:], d["v1"][bass.ds((v * 2 + w // 2) * S, S), :].rearrange("(n p) c -> p n c", p=P)).then_inc(m["vs_in"], 16)

            def negated_maxima(v, w):
                it = v * BODY + w
                hold(sp, r.passed, m["nt_done"], it + 1)
                sp.dma_start(d["mx1"][bass.ds(it * 3, 3)].rearrange("a s i -> s a i"), nt[:]).then_inc(m["nt_out"], 16)
                hold(sp, r.passed, m["nt_out"], it * 16 + 16)
                sp.dma_start(qt[w % 4][ROWS:ROWS + 3], d["mx1"][bass.ds(it * 3, 3)].rearrange("a (h t) i -> a h (t i)", h=GR)
                             ).then_inc(m["nm_in"], 16)

            def store(v, w):
                it = v * BODY + w
                hold(sp, r.passed, m["row_done"], it + 1)
                u = v * 2 + w // 2
                sp.dma_start(d["at1"][bass.ds(u * S + (w % 2) * W, W), :].rearrange("(t p) c -> p t c", p=P),
                             row[:, w % 2]).then_inc(m[f"out{w % 2}"], 16)

            sp.dma_start(ident[:], d["ident"]).then_inc(m["id_in"], 16)
            load_k(sp, 0, 0)
            for w in range(3):
                load_q(sp, 0, w)
            load_v(0, 0)
            negated_maxima(0, 0)
            for v, last in bodies(sp):
                for w in range(BODY):
                    hold(sp, r.passed, m["st_mm"], (v * BODY + w) * 2 * NB)
                    if w % 2 == 0 and not (last and w + 2 >= BODY):
                        load_k(sp, v, w + 2)
                    if not (last and w + 3 >= BODY):
                        load_q(sp, v, w + 3)
                    if w % 2 == 0 and not (last and w + 2 >= BODY):
                        hold(sp, r.passed, m["v_ready"], v * 2 + w // 2 + 1)
                        load_v(v, w + 2)
                    if w:
                        store(v, w - 1)
                    if not (last and w + 1 >= BODY):
                        negated_maxima(v, w + 1)
                store(v, BODY - 1)
            for z in range(2):
                sp.wait_ge(m[f"out{z}"], STEPS // 2 * 16)

        @block.gpsimd
        def _(pool):
            for n in range(2):
                pool.memset(v32[n][:, :, :, HD + 1:], 0.0)
                ins = pool.memset(v32[n][:, :, :, HD:HD + 1], 1.0)
            ins.then_inc(m["ones"], 1)

            def values(v, w):
                hold(pool, r.passed, m["vs_in"], (v * 2 + w // 2) * 16 + 16)
                pool.tensor_copy(v32[w // 2 % 2][:, :, :, 0:HD], vs[:].rearrange("p n (h e) -> p n h e", e=HD)).then_inc(m["v_ready"], 1)

            values(0, 0)
            for v, last in bodies(pool):
                for w in (0, 2):
                    if not (last and w + 2 >= BODY):
                        hold(pool, r.passed, m["pv_mm"], (v * BODY + w) * NB)
                        values(v, w + 2)

        @block.vector
        def _(dve):
            def row_maxima(v, w, n):
                for j in range(4 * n, 4 * n + 4):
                    dve.wait_ge(m["max_mm"], (v * BODY + w) * 4 * NB + j + 1)
                    dve.reduce_max(mx[w % 2][:].rearrange("p h t a -> p (h t a)")[:, j:j + 1], mp[j % 2][:], AX.X).then_inc(m["max_done"], 1)

            def negate(v, w):
                dve.wait_ge(m["max_done"], (v * BODY + w + 1) * 4 * NB)
                dve.tensor_reduce(nm[:].rearrange("p (h t) -> p h t", h=GR), mx[w % 2][:], AX.X, ALU.max, negate=True).then_inc(m["nm_done"], 1)

            def split(v, w):
                it = v * BODY + w
                link = Link(dve, m["schain"], 4, it)
                hold(dve, r.passed, m["nm_mm"], it + 1)
                link(dve.tensor_copy(nf[:], tb[0:GR * QT, 0]))
                dve.wait_ge(m["nt_out"], it * 16)
                link(dve.tensor_copy(nt[:, 0], nf[:]))
                link(dve.tensor_tensor(nr[:], nf[:], nt[:, 0], ALU.subtract))
                link(dve.tensor_copy(nt[:, 1], nr[:]))
                dve.tensor_tensor(nt[:, 2], nr[:], nt[:, 1], ALU.subtract).then_inc(m["nt_done"], 1)
                link.done()

            def normalise(v, w):
                it = v * BODY + w
                link = Link(dve, m["chain"], 1, it)
                dve.wait_ge(m["ot_mm"], it + 1)
                o = tb[:].rearrange("p t (h e) -> p t h e", e=32)
                link(dve.reciprocal(rs[:], o[:, :, :, HD:HD + 1]))
                dve.wait_ge(m[f"out{w % 2}"], (v * 2 + w // 2) * 16)
                dve.tensor_tensor(row[:, w % 2].rearrange("p t (h e) -> p t h e", e=HD), o[:, :, :, 0:HD],
                                  rs[:].to_broadcast([P, QT, GR, HD]), ALU.mult).then_inc(m["row_done"], 1)
                link.done()

            for n in range(2):
                ins = dve.memset(kt[n][ROWS:ROWS + 3], 1.0)
            ins.then_inc(m["ones"], 1)
            for w, n in FIRST:
                row_maxima(0, w, n)
                if (w, n) == (0, NB - 1):
                    negate(0, 0)
                    split(0, 0)
            for v, last in bodies(dve):
                for w in range(BODY):
                    for n in range(NB):
                        at = maxima(w, n, last)
                        if at:
                            row_maxima(v, *at)
                        if n == 3 and w:
                            normalise(v, w - 1)
                        if n == 3 and at:
                            negate(v, w + 1)
                        if n == 4 and not (last and w + 1 >= BODY):
                            split(v, w + 1)
                normalise(v, BODY - 1)

        @block.scalar
        def _(act):
            act.sem_inc(m["exp_done"], 2)

            def evacuate(v, w):
                it = v * BODY + w
                act.wait_ge(m["pv_mm"], it * NB + NB)
                act.wait_ge(m["ot_mm"], it)
                act.activation(os_[:], op[:], ACT.Copy).then_inc(m["os_done"], 1)

            for v, last in bodies(act):
                for x in range(BODY * NB):
                    slot = v * BODY * NB + x
                    for a in range(2):
                        act.wait_ge(m["st_mm"], slot * 2 + a + 1)
                        if a == 0:
                            if x >= 4:
                                act.wait_ge(m["pv_mm"], slot - 3)
                            else:
                                act.wait_ge(m["pv_mm"], v * BODY * NB)
                        act.activation(pt[:, x % 4, 2 * a:2 * a + 2], st[a][:], ACT.Exp).then_inc(m["exp_done"], 1)
                    if x % NB == 1 and x >= NB:
                        evacuate(v, x // NB - 1)
                evacuate(v, BODY - 1)

        @block.tensor
        def _(pe):
            def score_rows(v, w, j):
                if j == 0:
                    hold(pe, r.passed, m[f"q_in{w % 4}"], (v + w // 4) * 96 + 96)
                    hold(pe, r.passed, m[f"k_in{w // 2 % 2}"], (v + w // 4) * 96 + 96)
                for j in range(j, j + 2):
                    h, t, a = j // 8, j // 2 % 4, j % 2
                    if isinstance(v, int) and v == 0 and w == 0 and j < 2:
                        pass
                    else:
                        pe.wait_ge(m["max_done"], (v * BODY + w) * 4 * NB + j - 1)
                    pe.matmul(mp[a][:], qt[w % 4][0:ROWS, h, t * P:(t + 1) * P], kt[w // 2 % 2][0:ROWS, h, a * W:(a + 1) * W],
                              start=True, stop=True).then_inc(m["max_mm"], 1)

            def transpose_maxima(v, w):
                hold(pe, r.passed, m["nm_done"], v * BODY + w + 1)
                pe.transpose(tb[0:GR * QT, 0], nm[:], ident[:]).then_inc(m["nm_mm"], 1)

            def score_columns(v, w, n, a):
                pe.wait_ge(m["exp_done"], ((v * BODY + w) * NB + n) * 2 + a + 1)
                for h in (2 * a, 2 * a + 1):
                    ins = pe.matmul(st[a][:, h % 2], kt[w // 2 % 2][:, h, n * P:(n + 1) * P], qt[w % 4][:, h], start=True, stop=True)
                ins.then_inc(m["st_mm"], 1)

            def weigh(v, x):
                w, n = x // NB, x % NB
                slot = v * BODY * NB + x
                pe.wait_ge(m["exp_done"], slot * 2 + 4)
                if n == 0:
                    pe.wait_ge(m["os_done"], v * BODY + w)
                for h in range(GR):
                    ins = pe.matmul(op[32 * h:32 * h + 32], v32[w // 2 % 2][:, n, h], pt[:, x % 4, h], start=n == 0, stop=n == NB - 1)
                ins.then_inc(m["pv_mm"], 1)

            def transpose_sums(v, w):
                pe.wait_ge(m["os_done"], v * BODY + w + 1)
                for t in range(QT):
                    ins = pe.transpose(tb[:, t], os_[:, t * P:(t + 1) * P], ident[:])
                ins.then_inc(m["ot_mm"], 1)

            pe.wait_ge(m["id_in"], 16)
            pe.wait_ge(m["ones"], 2)
            for w, n in FIRST:
                for j in (4 * n, 4 * n + 2):
                    score_rows(0, w, j)
                if (w, n) == (0, NB - 1):
                    transpose_maxima(0, 0)
            for v, last in bodies(pe):
                for w in range(BODY):
                    for n in range(NB):
                        x = w * NB + n
                        at = maxima(w, n, last)
                        if n == 0:
                            hold(pe, r.passed, m["nm_in"], (v * BODY + w) * 16 + 16)
                            hold(pe, r.passed, m["v_ready"], v * 2 + w // 2 + 1)
                        for a in range(2):
                            score_columns(v, w, n, a)
                            if at:
                                score_rows(v, at[0], 4 * at[1] + 2 * a)
                            if a == 0 and x >= LAG:
                                weigh(v, x - LAG)
                        if n == 3 and w:
                            pe.wait_ge(m["nt_done"], v * BODY + w)
                            transpose_sums(v, w - 1)
                        if n == 4 and not (last and w + 1 >= BODY):
                            pe.wait_ge(m["row_done"], v * BODY + w)
                            transpose_maxima(v, w + 1)
                for x in range(BODY * NB - LAG, BODY * NB):
                    weigh(v, x)
                if last:
                    pe.wait_ge(m["row_done"], v * BODY + BODY - 1)
                else:
                    pe.wait_ge(m["nt_done"], v * BODY + BODY + 1)
                transpose_sums(v, BODY - 1)


def stage_moe(nc, d):
    HID = 512
    KH = HID // P
    NG, NE = 2, 8
    NL = NG + NE
    TOPK = 2
    BIG = 1e30
    PAIRS = TILES // 2
    PAIR_E = HID // D
    SLOTS = NE // PAIR_E
    with ExitStack() as ctx:
        r = Room(nc, ctx, "moe")
        ident = r.sb("ident", [P, P])
        wo = r.sb("wo", [P, KD, D])
        wi = [r.sb(f"wi{n}", [P, KD, 2 * HID]) for n in range(2)]
        wso = r.sb("wso", [P, KH, D])
        w2 = r.sb("w2", [P, KH, NE, D])
        wl, bl = r.sb("wl", [P, KD, NL]), r.sb("bl", [P, NL])
        n1, n2 = r.sb("n1", [P, D]), r.sb("n2", [P, D])
        before = r.sb("before", [P, NE, NE])
        half = r.sb("half", [P, 1])
        a, src, x5, at, xs, x, xt, acc, y = [r.sb(n, [P, 2, D]) for n in "a src x5 at xs x xt acc y".split()]
        junk = r.sb("junk", [P, 4, D])
        ssq, va, rs = [r.sb(n, [P, 2, 2]) for n in ("ssq", "va", "rs")]
        sil, hid, hidt = [[r.sb(f"{n}{k}", [P, 2, HID]) for k in range(2)] for n in ("sil", "hid", "hidt")]
        lg, gm, em, dif, ex = r.sb("lg", [P, 2, NL]), r.sb("gm", [P, 2, 1]), r.sb("em", [P, 2, 1]), r.sb("dif", [P, 2, NL]), r.sb("ex", [P, 2, NL])
        ing, sm, pe_, w = r.sb("ing", [P, 2, NE]), r.sb("sm", [P, 2, 2]), r.sb("pe", [P, 2, NE]), r.sb("w", [P, 2, NE])
        gt, eq, rank = r.sb("gt", [P, 2, NE, NE]), r.sb("eq", [P, 2, NE, NE]), r.sb("rank", [P, 2, NE])
        ps = [[r.ps(f"ps{z}{a_}", [P, HID]) for a_ in range(2)] for z in range(2)]
        tp = [r.ps(f"tp{z}", [P, HID]) for z in range(2)]
        so = r.ps("so", [P, 2, D])
        lp = r.ps("lp", [P, 2, NL])
        m = {n: r.sem(n) for n in "w_in consts chain fchain dif_done ex_done w_done so_used".split()}
        steps = ("a_in x5_in a_free x5_free at_mm at_c wo_mm xs_done sqf vaf rsf x_done xt_mm xt_c l_mm in_mm0 in_mm1 sil0 sil1 "
                 "hid0 hid1 ht_mm0 ht_mm1 ht_c0 ht_c1 so_mm acc0 e_mm e_used acc_done sqt vat rst y_done out")
        e = {n: [r.sem(f"{n}_{z}") for z in range(2)] for n in steps.split()}
        block = ctx.enter_context(nc.Block())

        def pairs(eng):
            with eng.Fori(0, PAIRS - 1) as p:
                yield p, False
            yield PAIRS - 1, True

        @block.sync
        def _(sp):
            loads = [(ident[:], d["ident"]), (wo[:], rows_in(d["L1_ffn_Wo"])), (wi[0][:], rows_in(d["L1_ffn_W_shared_in"])),
                     (wi[1][:], rows_in(d["L1_ffn_W1_shared"])), (wso[:], rows_in(d["L1_ffn_W_shared_out"])),
                     (wl[:, :, 0:NG], rows_in(d["L1_ffn_Wg_gate"])), (wl[:, :, NG:], rows_in(d["L1_ffn_We_gate"])),
                     (bl[:, 0:NG], d["L1_ffn_group_bias"].partition_broadcast(P)), (bl[:, NG:], d["L1_ffn_expert_bias"].partition_broadcast(P)),
                     (n1[:], d["L1_ffn_norm1_w"].partition_broadcast(P)), (n2[:], d["L1_ffn_norm2_w"].partition_broadcast(P)),
                     (before[:], d["before"].partition_broadcast(P))]
            loads += [(w2[:, :, n], rows_in(d["L1_ffn_W2_experts"][n])) for n in range(NE)]
            assert len(loads) == 20
            for dst, s in loads:
                sp.dma_start(dst, s).then_inc(m["w_in"], 16)
            with sp.Fori(0, B) as b:
                with sp.Fori(0, TPB // 2) as ih:
                    p = b * (TPB // 2) + ih
                    for z in range(2):
                        hold(sp, r.passed, e["a_free"][z], p + 1)
                        sp.dma_start(a[:, z].rearrange("p (h c) -> p h c", h=4), d["at1"].rearrange("(u s) c -> u s c", s=S)
                                     [bass.ds(b * 4, 4), bass.ds((ih * 2 + z) * P, P), :].rearrange("h p c -> p h c")).then_inc(e["a_in"][z], 16)
                        sp.dma_start(src[:, z], d["src1"][bass.ds((p * 2 + z) * P, P), :]).then_inc(e["a_in"][z], 16)
                    for z in range(2):
                        hold(sp, r.passed, e["x5_free"][z], p + 1)
                        sp.dma_start(x5[:, z], d["x5"][bass.ds((p * 2 + z) * P, P), :]).then_inc(e["x5_in"][z], 16)

        @block.gpsimd
        def _(pool):
            pool.memset(half[:], -0.5).then_inc(m["consts"], 1)
            pool.wait_ge(m["consts"], 1)

            def root(p, k, signal, done, z):
                pool.wait_ge(e[signal][z], p + 1)
                pool.tensor_tensor(rs[:, z, k:k + 1], va[:, z, k:k + 1], half[:], ALU.pow).then_inc(e[done][z], 1)

            for z in range(2):
                root(0, 0, "vaf", "rsf", z)
            for p, last in pairs(pool):
                if not last:
                    for z in range(2):
                        root(p + 1, 0, "vaf", "rsf", z)
                for z in range(2):
                    root(p, 1, "vat", "rst", z)

        @block.vector
        def _(dve):
            dve.wait_ge(m["w_in"], 16 * 20)
            for z in range(2):
                dve.sem_inc(e["x5_free"][z], 1)
                dve.sem_inc(e["a_free"][z], 1)

            def first_sum(p, z):
                dve.wait_ge(e["a_in"][z], 32 * p + 32)
                dve.wait_ge(e["wo_mm"][z], p + 1)
                dve.tensor_tensor(xs[:, z], src[:, z], tp[z][:, D:2 * D], ALU.add).then_inc(e["xs_done"][z], 1)
                dve.wait_ge(e["xs_done"][z], p + 1)
                dve.sem_inc(e["a_free"][z], 1)

            def variance(p, z, k, signal, done):
                dve.wait_ge(e[signal][z], p + 1)
                dve.tensor_scalar(va[:, z, k:k + 1], ssq[:, z, k:k + 1], 1.0 / D, 1e-6, ALU.mult, ALU.add).then_inc(e[done][z], 1)

            def first_norm(p, z):
                dve.wait_ge(e["rsf"][z], p + 1)
                dve.scalar_tensor_tensor(x[:, z], xs[:, z], rs[:, z, 0:1], n1[:], ALU.mult, ALU.mult).then_inc(e["x_done"][z], 1)

            def last_norm(p, z):
                link = Link(dve, e["chain"][z], 1, p)
                dve.wait_ge(e["rst"][z], p + 1)
                dve.wait_ge(e["out"][z], 16 * p)
                link(dve.scalar_tensor_tensor(y[:, z], acc[:, z], rs[:, z, 1:2], n2[:], ALU.mult, ALU.mult))
                dve.wait_ge(e["x5_in"][z], 16 * p + 16)
                dve.tensor_tensor(y[:, z], y[:, z], x5[:, z], ALU.add).then_inc(e["y_done"][z], 1)
                dve.wait_ge(e["y_done"][z], p + 1)
                dve.sem_inc(e["x5_free"][z], 1)
                link.done()

            e["chain"] = [r.sem(f"last_chain{z}") for z in range(2)]
            wide = lambda v, n: v.to_broadcast([P, 2, n])

            def route(p):
                link = Link(dve, m["chain"], 19, p)
                for z in range(2):
                    dve.wait_ge(e["l_mm"][z], p + 1)
                for z in range(2):
                    ins = dve.tensor_tensor(lg[:, z], lp[:, z], bl[:], ALU.add)
                link(ins)
                link(dve.reduce_max(gm[:], lg[:, :, 0:NG], AX.X))
                link(dve.tensor_tensor(ing[:, :, NE // 2:], wide(lg[:, :, 1:2], NE // 2), wide(lg[:, :, 0:1], NE // 2), ALU.is_gt))
                link(dve.tensor_scalar(ing[:, :, 0:NE // 2], ing[:, :, NE // 2:], -1.0, 1.0, ALU.mult, ALU.add))
                link(dve.tensor_tensor(lg[:, :, NG:], lg[:, :, NG:], ing[:], ALU.mult))
                link(dve.tensor_scalar(ing[:], ing[:], 1.0, BIG, ALU.subtract, ALU.mult))
                link(dve.tensor_tensor(lg[:, :, NG:], lg[:, :, NG:], ing[:], ALU.add))
                link(dve.reduce_max(em[:], lg[:, :, NG:], AX.X))
                link(dve.tensor_tensor(dif[:, :, 0:NG], lg[:, :, 0:NG], wide(gm[:], NG), ALU.subtract))
                link(dve.tensor_tensor(dif[:, :, NG:], lg[:, :, NG:], wide(em[:], NE), ALU.subtract))
                dve.sem_inc(m["dif_done"], 1)
                dve.wait_ge(m["ex_done"], p + 1)
                for n, (lo, hi) in enumerate(((0, NG), (NG, NL))):
                    ins = dve.reduce_sum(sm[:, :, n:n + 1].rearrange("p z o -> p (z o)"), ex[:, :, lo:hi], AX.X)
                link(ins)
                link(dve.reciprocal(sm[:], sm[:]))
                link(dve.tensor_tensor(pe_[:], ex[:, :, NG:], wide(sm[:, :, 1:2], NE), ALU.mult))
                link(dve.tensor_tensor(pe_[:], pe_[:], wide(sm[:, :, 0:1], NE), ALU.mult))
                for z in range(2):
                    mine = pe_[:, z].rearrange("p (e o) -> p e o", o=1).to_broadcast([P, NE, NE])
                    other = pe_[:, z].rearrange("p (o f) -> p o f", o=1).to_broadcast([P, NE, NE])
                    dve.tensor_tensor(gt[:, z], other, mine, ALU.is_gt)
                    ins = dve.tensor_tensor(eq[:, z], other, mine, ALU.is_equal)
                link(ins)
                for z in range(2):
                    ins = dve.tensor_tensor(eq[:, z], eq[:, z], before[:], ALU.mult)
                link(ins)
                link(dve.tensor_tensor(gt[:], gt[:], eq[:], ALU.add))
                link(dve.reduce_sum(rank[:], gt[:], AX.X))
                link(dve.tensor_scalar(rank[:], rank[:], float(TOPK), None, ALU.is_lt))
                dve.tensor_tensor(w[:], rank[:], pe_[:], ALU.mult).then_inc(m["w_done"], 1)
                link.done()

            for z in range(2):
                first_sum(0, z)
            for z in range(2):
                variance(0, z, 0, "sqf", "vaf")
            for z in range(2):
                first_norm(0, z)
            for p, last in pairs(dve):
                route(p)
                for k in range(2):
                    for z in range(2):
                        dve.wait_ge(e[f"sil{k}"][z], p + 1)
                        dve.tensor_tensor(hid[k][:, z], sil[k][:, z], ps[z][1][:], ALU.mult).then_inc(e[f"hid{k}"][z], 1)
                for z in range(2):
                    dve.wait_ge(e["so_mm"][z], p + 1)
                    dve.tensor_tensor(acc[:, z], x[:, z], so[:, z], ALU.add).then_inc(e["acc0"][z], 1)
                dve.wait_ge(m["w_done"], p + 1)
                for s in range(2 * SLOTS):
                    z, q = s // SLOTS, s % SLOTS
                    dve.wait_ge(e["e_mm"][z], p * SLOTS + q + 1)
                    for n in range(PAIR_E):
                        k = q * PAIR_E + n
                        if k == 0:
                            dve.wait_ge(e["acc0"][z], p + 1)
                        else:
                            dve.wait_ge(e["acc_done"][z], p * NE + k)
                        dve.scalar_tensor_tensor(acc[:, z], ps[z][q % 2][:, n * D:(n + 1) * D], w[:, z, k:k + 1], acc[:, z],
                                                 ALU.mult, ALU.add).then_inc(e["acc_done"][z], 1)
                    if s == 2 and not last:
                        for y_ in range(2):
                            first_sum(p + 1, y_)
                    if s == 3 and not last:
                        for y_ in range(2):
                            variance(p + 1, y_, 0, "sqf", "vaf")
                    if s == 4:
                        if not last:
                            for y_ in range(2):
                                first_norm(p + 1, y_)
                        variance(p, 0, 1, "sqt", "vat")
                    if s == 5:
                        last_norm(p, 0)
                variance(p, 1, 1, "sqt", "vat")
                last_norm(p, 1)

        @block.scalar
        def _(act):
            def copy(p, z, signal, done, dst, source):
                act.wait_ge(e[signal][z], p + 1)
                act.activation(dst[:, z], source, ACT.Copy).then_inc(e[done][z], 1)

            def first(p):
                for z in range(2):
                    copy(p, z, "at_mm", "at_c", at, tp[z][:, 0:D])
                for z in range(2):
                    act.wait_ge(e["xs_done"][z], p + 1)
                    act.activation(junk[:, z], xs[:, z], ACT.Square, accum_out=ssq[:, z, 0:1]).then_inc(e["sqf"][z], 1)

            def first_end(p):
                for z in range(2):
                    copy(p, z, "xt_mm", "xt_c", xt, tp[z][:, 0:D])

            def last_square(p, z):
                act.wait_ge(e["acc_done"][z], p * NE + NE)
                act.activation(junk[:, 2 + z], acc[:, z], ACT.Square, accum_out=ssq[:, z, 1:2]).then_inc(e["sqt"][z], 1)

            first(0)
            first_end(0)
            for p, last in pairs(act):
                act.wait_ge(m["dif_done"], p + 1)
                act.activation(ex[:], dif[:], ACT.Exp).then_inc(m["ex_done"], 1)
                for k in range(2):
                    for z in range(2):
                        act.wait_ge(e[f"in_mm{k}"][z], p + 1)
                        act.activation(sil[k][:, z], ps[z][0][:], ACT.Silu).then_inc(e[f"sil{k}"][z], 1)
                    if k == 1:
                        for j in range(2):
                            for z in range(2):
                                copy(p, z, f"ht_mm{j}", f"ht_c{j}", hidt[j], tp[z][:])
                if not last:
                    first(p + 1)
                last_square(p, 0)
                if not last:
                    first_end(p + 1)
                last_square(p, 1)
                for z in range(2):
                    act.wait_ge(e["y_done"][z], p + 1)
                    act.dma_start(d["x6"][bass.ds((p * 2 + z) * P, P), :], y[:, z]).then_inc(e["out"][z], 16)
            for z in range(2):
                act.wait_ge(e["out"][z], 16 * PAIRS)

        @block.tensor
        def _(pe):
            def transposes(z, v, n):
                for c in range(n):
                    ins = pe.transpose(tp[z][:, c * P:(c + 1) * P], v[:, c * P:(c + 1) * P], ident[:])
                return ins

            def first_transpose(p, z):
                pe.wait_ge(e["a_in"][z], 32 * p + 32)
                pe.wait_ge(e["ht_c1"][z], p)
                transposes(z, a[:, z], KD).then_inc(e["at_mm"][z], 1)

            def first_product(p, z):
                pe.wait_ge(e["at_c"][z], p + 1)
                for k in range(KD):
                    ins = pe.matmul(tp[z][:, D:2 * D], at[:, z, k * P:(k + 1) * P], wo[:, k], start=k == 0, stop=k == KD - 1)
                ins.then_inc(e["wo_mm"][z], 1)

            def norm_transpose(p, z):
                pe.wait_ge(e["x_done"][z], p + 1)
                transposes(z, x[:, z], KD).then_inc(e["xt_mm"][z], 1)

            def logits(p, z):
                pe.wait_ge(e["xt_c"][z], p + 1)
                for k in range(KD):
                    ins = pe.matmul(lp[:, z], xt[:, z, k * P:(k + 1) * P], wl[:, k], start=k == 0, stop=k == KD - 1)
                ins.then_inc(e["l_mm"][z], 1)

            def into(p, z, k):
                if k:
                    pe.wait_ge(e["hid0"][z], p + 1)
                else:
                    pe.wait_ge(e["acc_done"][z], p * NE)
                for a_ in range(2):
                    for c in range(KD):
                        ins = pe.matmul(ps[z][a_][:], xt[:, z, c * P:(c + 1) * P], wi[k][:, c, a_ * HID:(a_ + 1) * HID],
                                        start=c == 0, stop=c == KD - 1)
                ins.then_inc(e[f"in_mm{k}"][z], 1)

            def hidden_transpose(p, z, k):
                pe.wait_ge(e[f"hid{k}"][z], p + 1)
                if k:
                    pe.wait_ge(e["ht_c0"][z], p + 1)
                transposes(z, hid[k][:, z], KH).then_inc(e[f"ht_mm{k}"][z], 1)

            def shared_out(p, z):
                pe.wait_ge(e["ht_c0"][z], p + 1)
                pe.wait_ge(e["acc0"][1 - z], p + z)
                for k in range(KH):
                    ins = pe.matmul(so[:, z], hidt[0][:, z, k * P:(k + 1) * P], wso[:, k], start=k == 0, stop=k == KH - 1)
                ins.then_inc(e["so_mm"][z], 1)

            def experts(p, z, q):
                if q == 0:
                    pe.wait_ge(e["hid1"][z], p + 1)
                    pe.wait_ge(e["ht_c1"][z], p + 1)
                elif q >= 2:
                    pe.wait_ge(e["acc_done"][z], p * NE + (q - 1) * PAIR_E)
                for k in range(KH):
                    ins = pe.matmul(ps[z][q % 2][:], hidt[1][:, z, k * P:(k + 1) * P],
                                    w2[:, k, q * PAIR_E:(q + 1) * PAIR_E].rearrange("p e n -> p (e n)"), start=k == 0, stop=k == KH - 1)
                ins.then_inc(e["e_mm"][z], 1)

            pe.wait_ge(m["w_in"], 16 * 20)
            for step in (first_transpose, first_product, norm_transpose, logits):
                for z in range(2):
                    step(0, z)
            for p, last in pairs(pe):
                for z in range(2):
                    into(p, z, 0)
                for z in range(2):
                    into(p, z, 1)
                    hidden_transpose(p, z, 0)
                for z in range(2):
                    shared_out(p, z)
                    hidden_transpose(p, z, 1)
                for s in range(2 * SLOTS):
                    experts(p, s // SLOTS, s % SLOTS)
                    if not last:
                        step = {0: first_transpose, 1: first_product, 5: norm_transpose, 6: logits}.get(s)
                        if step:
                            for z in range(2):
                                step(p + 1, z)


SCRATCH = {
    "q3": ((3, D, T), BF16), "k3": ((3, D, T), BF16), "v0": ((T, D), F32), "aux": ((T, 4 + 3 * NH), F32),
    "ljd": ((3, T), F32), "attn": ((T, D), F32),
    "x1": ((T, D), F32), "x2": ((T, D), F32), "x3": ((T, D), F32), "x4": ((T, D), F32), "x5": ((T, D), F32),
    "qkv": ((T, 3 * GD), F32), "ab": ((T, 2 * GH), F32), "o": ((T, GD), F32),
    "src1": ((T, D), F32), "q1": ((3, B * D, S), BF16), "k1": ((3, B * D, S), BF16), "v1": ((4 * T, D // 4), F32),
    "mx1": ((3 * 2 * NH, 16, P), BF16), "at1": ((4 * T, D // 4), F32),
    "latt": ((B * NH, S, HD), F32),
    "x6": ((T, D), F32),
}


def layout(inputs):
    a = {k: np.asarray(v) for k, v in inputs.items()}
    out = {"ident": np.eye(P, dtype=np.float32)}
    out["head_mask"] = np.repeat(np.eye(NH // 2, dtype=np.float32), HD, axis=0)
    t, u = np.arange(P)[:, None], np.arange(P)[None, :]
    below = lambda n: ((t // n) % 2 == 1) & (u // n == t // n - 1)
    eye = np.eye(P, dtype=np.float32)
    out["eye4"] = np.repeat(eye[:, None], 4, axis=1)
    out["levels"] = np.stack([eye - below(2 ** n) for n in range(1, 7)], axis=1).astype(np.float32)
    out["level0t"] = -below(1).T.astype(np.float32)
    out["eye8"] = np.eye(GH, dtype=np.float32)
    out["alpha_mask"] = np.repeat(out["eye8"][:, :, None], P, axis=2)
    out["alpha_mask"][:, :, 0] = 0
    out["ctx"] = a["ctx_1024"].reshape(-1, D)
    out["mask_ff"] = a["mask_BxS2_ff1"].reshape(-1, 1)
    heads = np.repeat(np.eye(NH, dtype=np.float32), HD, axis=1)
    same = np.concatenate([heads.T @ heads > 0, heads.T > 0], axis=1).astype(np.float32)
    out["same_head"] = same.reshape(KD, P, -1).transpose(1, 0, 2)
    out["before"] = np.tril(np.ones((8, 8), np.float32), -1)
    freq = 1.0 / np.float32(10000.0) ** (np.arange(0, HD, 2, dtype=np.float32) / np.float32(HD))
    ang = (np.arange(S, dtype=np.float32)[None, :] * freq[:, None]).astype(np.float64)
    out["rope_cos"] = np.tile(np.repeat(np.cos(ang), 2, axis=0), (P // HD, 1)).astype(np.float32)
    out["rope_sin"] = np.tile(np.stack([-np.sin(ang), np.sin(ang)], axis=1).reshape(HD, S), (P // HD, 1)).astype(np.float32)
    for name in ("L1_ffn_Wq", "L1_ffn_Wk"):
        out[name + "_swapped"] = a[name].reshape(-1, D // 2, 2)[:, :, ::-1].reshape(-1, D)
    out["mask_words"] = np.repeat(a["mask_BxS2_bk0"].view(np.uint8), 4, axis=1).view(np.int32)
    out["x"] = a["x"].reshape(T, D)
    for k, v in a.items():
        if k in ("L0_attn_Wq", "L0_attn_Wk", "L0_attn_Wv", "L0_attn_Wo", "L0_attn_gate_W", "L0_attn_rel_W",
                 "L0_attn_logical_bias", "L0_xattn_Wq_w", "L0_xattn_Wkv_w", "L0_xattn_out_w",
                 "L0_ffn_w_gate", "L0_ffn_w_up", "L0_ffn_w_down"):
            out[k + "T"] = np.ascontiguousarray(v.T)
        elif k in ("L0_attn_bq", "L0_attn_bk"):
            out[k + "_cols"] = v.reshape(-1, P).T
        elif k not in ("x", "ctx_1024", "mask_BxS2_bk0"):
            out[k] = v
        if k in ("L0_xattn_Wq_b", "L0_xattn_Wkv_b"):
            out[k + "_cols"] = v.reshape(-1, P).T
    return {k: np.ascontiguousarray(v) for k, v in out.items()}


STAGES = (stage_pre0, stage_attn0, stage_mid0, stage_ffn0, stage_gdn_in, stage_gdn_core, stage_gdn_out, stage_lin,
          stage_lin_out, stage_pre1, stage_attn1, stage_moe)


def kernel(**inputs):
    import concourse.bacc as bacc
    from concourse.bass_utils import run_bass_kernel_spmd

    nc = bacc.Bacc("TRN2", target_bir_lowering=False, num_devices=1)
    arrays, d = {}, {}
    for name, a in layout(inputs).items():
        arrays[f"in_{name}"] = a
        d[name] = nc.dram_tensor(f"in_{name}", a.shape, mybir.dt.from_np(a.dtype), kind="ExternalInput").ap()
    for name, (shape, dtype) in SCRATCH.items():
        d[name] = nc.dram_tensor(f"s_{name}", shape, dtype, kind="ExternalOutput" if name == "x6" else "Internal").ap()
    for stage in STAGES:
        stage(nc, d)
    results = run_bass_kernel_spmd(nc, [arrays], core_ids=[0]).results[0]
    return results["s_x6"].reshape(B, S, D)
```
